# Optimizing a Trainium2 kernel written in Bass

```python
import numpy as np
import jax
import jax.numpy as jnp

def _softmax(x, axis=-1):
    return jax.nn.softmax(x, axis=axis)

def _gelu(x):
    return jax.nn.gelu(x, approximate=True)

def _silu(x):
    return jax.nn.silu(x)

def _sigmoid(x):
    return jax.nn.sigmoid(x)

def _layernorm(x, axis=-1, eps=1e-05):
    m = jnp.mean(x, axis=axis, keepdims=True)
    v = jnp.var(x, axis=axis, keepdims=True)
    return (x - m) / jnp.sqrt(v + eps)

def _scatter_add(tgt, idx, src, axis=0):
    return tgt.at[idx].add(src)

def _segment_sum(src, seg, n):
    return jax.ops.segment_sum(src, seg, n)
kernel_name = 'mk_vit_tower_d2_tok_img1024_r4_9e879d'

def setup_inputs(seed: int=0):
    np.random.seed(seed)
    _w = jnp.asarray

    def _rec_inputs():
        import jax
        import jax.numpy as jnp
        _rk = jax.random.key(seed)
        x = -0.00016672 + 0.999947 * jax.random.normal(jax.random.fold_in(_rk, 1), (64, 3, 128, 128), jnp.float32)
        return x
    x = _rec_inputs()

    def _L0_tok_setup():
        import jax, jax.numpy as jnp
        import numpy as np
        IMG = 96
        P = 16
        C = 3
        D = 256
        B = 64
        key = jax.random.key(seed)
        kx, kw, kb = jax.random.split(key, 3)
        fan_in = C * P * P
        bound = 1.0 / np.sqrt(fan_in)
        x = jax.random.normal(kx, (B, C, IMG, IMG), dtype=jnp.float32)
        W = jax.random.uniform(kw, (D, fan_in), dtype=jnp.float32, minval=-bound, maxval=bound)
        b = jax.random.uniform(kb, (D,), dtype=jnp.float32, minval=-bound, maxval=bound)
        return {'x': x, 'W': W, 'b': b}
    _L0_tok_all = _L0_tok_setup()
    _L0_tok_in = {k: v for k, v in _L0_tok_all.items() if k in ('W', 'b')}
    del _L0_tok_all

    def _L0_attn_setup():
        import jax, jax.numpy as jnp
        import numpy as np
        H = 16
        G = 4
        THETA = 10000.0

        def _rope(x, cos, sin):
            x0 = x[..., ::2]
            x1 = x[..., 1::2]
            r0 = x0 * cos - x1 * sin
            r1 = x0 * sin + x1 * cos
            return jnp.stack([r0, r1], axis=-1).reshape(x.shape)
        key = jax.random.key(seed)
        ks = jax.random.split(key, 5)
        B, S, D = (2, 512, 256)
        return {'x': jax.random.normal(ks[0], (B, S, D), jnp.float32), 'Wq': jax.random.normal(ks[1], (D, D), jnp.float32) * 0.02, 'Wk': jax.random.normal(ks[2], (D, D // G), jnp.float32) * 0.02, 'Wv': jax.random.normal(ks[3], (D, D // G), jnp.float32) * 0.02, 'Wo': jax.random.normal(ks[4], (D, D), jnp.float32) * 0.02}
    _L0_attn_all = _L0_attn_setup()
    _L0_attn_in = {k: v for k, v in _L0_attn_all.items() if k in ('Wq', 'Wk', 'Wv', 'Wo')}
    del _L0_attn_all

    def _L0_ffn_setup():
        import jax, jax.numpy as jnp
        import numpy as np
        BLOCK = 32
        W_BITS = 4
        ACT_BITS = 16

        def act_qdq(x):
            qmax = 2.0 ** (ACT_BITS - 1) - 1.0
            scale = jnp.maximum(jnp.max(jnp.abs(x)) / qmax, 1e-12)
            return jnp.clip(jnp.round(x / scale), -qmax - 1.0, qmax) * scale

        def fixed_qdq_u16(x):
            scale = 1.0 / 65536.0
            return jnp.clip(jnp.round(x / scale), 0.0, 65535.0) * scale

        def lpbq_dequant(w):
            O, I = w.shape
            qmax = 2.0 ** (W_BITS - 1) - 1.0
            wb = w.reshape(O, I // BLOCK, BLOCK)
            s = jnp.maximum(jnp.max(jnp.abs(wb), axis=-1, keepdims=True) / qmax, 1e-12)
            wq = jnp.clip(jnp.round(wb / s), -qmax - 1.0, qmax) * s
            return wq.reshape(O, I)
        key = jax.random.key(seed)
        k1, k2, k3, k4 = jax.random.split(key, 4)
        B, S, H, I = (2, 1024, 256, 768)
        x = jax.random.normal(k1, (B, S, H), jnp.float32)
        w_gate = jax.random.normal(k2, (I, H), jnp.float32) * 0.02
        w_up = jax.random.normal(k3, (I, H), jnp.float32) * 0.02
        w_down = jax.random.normal(k4, (H, I), jnp.float32) * 0.02
        return {'x': x, 'w_gate': w_gate, 'w_up': w_up, 'w_down': w_down}
    _L0_ffn_all = _L0_ffn_setup()
    _L0_ffn_in = {k: v for k, v in _L0_ffn_all.items() if k in ('w_gate', 'w_up', 'w_down')}
    del _L0_ffn_all

    def _L1_attn_setup():
        import jax, jax.numpy as jnp
        import numpy as np
        D = 256
        H = 16
        KVH = 4
        HD = D // H
        LAT = 64
        WIN = 64
        B, S = (1, 512)
        BASE_G, BASE_L = (1000000.0, 10000.0)
        EPS = 1e-06

        def rmsnorm(x, w):
            return x * jax.lax.rsqrt(jnp.mean(x * x, axis=-1, keepdims=True) + EPS) * w

        def qk_norm(x):
            return x * jax.lax.rsqrt(jnp.mean(x * x, axis=-1, keepdims=True) + EPS)

        def rope(x, base):
            s, hd = (x.shape[-2], x.shape[-1])
            inv_freq = 1.0 / base ** (jnp.arange(0, hd, 2, dtype=jnp.float32) / hd)
            freqs = jnp.arange(s, dtype=jnp.float32)[:, None] * inv_freq[None, :]
            cos, sin = (jnp.cos(freqs), jnp.sin(freqs))
            xe, xo = (x[..., ::2], x[..., 1::2])
            out = jnp.stack([xe * cos - xo * sin, xe * sin + xo * cos], axis=-1)
            return out.reshape(x.shape)

        def split_heads(x, n_heads):
            b, s, _ = x.shape
            return x.reshape(b, s, n_heads, HD).transpose(0, 2, 1, 3)

        def repeat_kv(x):
            return jnp.repeat(x, H // KVH, axis=1)

        def sdpa(q, k, v, mask):
            scores = jnp.einsum('bhqd,bhkd->bhqk', q, k) / np.sqrt(HD).astype(np.float32)
            scores = jnp.where(mask, scores, jnp.float32(-1e+30))
            probs = jax.nn.softmax(scores, axis=-1)
            return jnp.einsum('bhqk,bhkd->bhqd', probs, v)

        def merge_heads(x):
            b, h, s, hd = x.shape
            return x.transpose(0, 2, 1, 3).reshape(b, s, h * hd)

        def global_latent_attn(x, wq, w_kv_down, w_k_up, w_v_up, wo):
            q = split_heads(x @ wq, H)
            latent = x @ w_kv_down
            k = split_heads(latent @ w_k_up, KVH)
            v = split_heads(latent @ w_v_up, KVH)
            q, k = (rope(q, BASE_G), rope(k, BASE_G))
            q, k = (qk_norm(q), qk_norm(k))
            k, v = (repeat_kv(k), repeat_kv(v))
            i = jnp.arange(x.shape[1])
            causal = i[:, None] >= i[None, :]
            return merge_heads(sdpa(q, k, v, causal)) @ wo

        def local_gqa_attn(x, wq, wk, wv, wo):
            q = split_heads(x @ wq, H)
            k = split_heads(x @ wk, KVH)
            v = split_heads(x @ wv, KVH)
            q, k = (rope(q, BASE_L), rope(k, BASE_L))
            q, k = (qk_norm(q), qk_norm(k))
            k, v = (repeat_kv(k), repeat_kv(v))
            i = jnp.arange(x.shape[1])
            diff = i[:, None] - i[None, :]
            mask = (diff >= 0) & (diff < WIN)
            return merge_heads(sdpa(q, k, v, mask)) @ wo
        key = jax.random.key(seed)
        ks = jax.random.split(key, 12)
        std = 0.02
        return {'hidden': jax.random.normal(ks[0], (B, S, D), dtype=jnp.float32), 'norm1_w': jnp.ones((D,), jnp.float32), 'norm2_w': jnp.ones((D,), jnp.float32), 'g_wq': jax.random.normal(ks[1], (D, H * HD), jnp.float32) * std, 'g_kv_down': jax.random.normal(ks[2], (D, LAT), jnp.float32) * std, 'g_k_up': jax.random.normal(ks[3], (LAT, KVH * HD), jnp.float32) * std, 'g_v_up': jax.random.normal(ks[4], (LAT, KVH * HD), jnp.float32) * std, 'g_wo': jax.random.normal(ks[5], (D, D), jnp.float32) * std, 'l_wq': jax.random.normal(ks[6], (D, H * HD), jnp.float32) * std, 'l_wk': jax.random.normal(ks[7], (D, KVH * HD), jnp.float32) * std, 'l_wv': jax.random.normal(ks[8], (D, KVH * HD), jnp.float32) * std, 'l_wo': jax.random.normal(ks[9], (D, D), jnp.float32) * std}
    _L1_attn_all = _L1_attn_setup()
    _L1_attn_in = {k: v for k, v in _L1_attn_all.items() if k in ('norm1_w', 'norm2_w', 'g_wq', 'g_kv_down', 'g_k_up', 'g_v_up', 'g_wo', 'l_wq', 'l_wk', 'l_wv', 'l_wo')}
    del _L1_attn_all

    def _L1_ffn_setup():
        import jax, jax.numpy as jnp
        import numpy as np
        IN_DIM, OUT_DIM, N_PROTO, RANK = (256, 256, 32, 16)
        key = jax.random.key(seed)
        ks = jax.random.split(key, 5)
        x = jax.random.normal(ks[0], (2, 1024, IN_DIM), dtype=jnp.float32)
        prototypes = jax.random.normal(ks[1], (N_PROTO, IN_DIM), dtype=jnp.float32) * 0.02
        B = jax.random.normal(ks[2], (N_PROTO, RANK, IN_DIM), dtype=jnp.float32) * 0.02
        A = jax.random.normal(ks[3], (N_PROTO, OUT_DIM, RANK), dtype=jnp.float32) * 0.02
        bias = jnp.zeros((N_PROTO, OUT_DIM), dtype=jnp.float32)
        temp = jnp.asarray(1.0, dtype=jnp.float32)
        return {'x': x, 'prototypes': prototypes, 'B': B, 'A': A, 'bias': bias, 'temp': temp}
    _L1_ffn_all = _L1_ffn_setup()
    _L1_ffn_in = {k: v for k, v in _L1_ffn_all.items() if k in ('prototypes', 'B', 'A', 'bias', 'temp')}
    del _L1_ffn_all
    return {'x': x, 'L0_tok_W': _L0_tok_in['W'], 'L0_tok_b': _L0_tok_in['b'], 'L0_attn_Wq': _L0_attn_in['Wq'], 'L0_attn_Wk': _L0_attn_in['Wk'], 'L0_attn_Wv': _L0_attn_in['Wv'], 'L0_attn_Wo': _L0_attn_in['Wo'], 'L0_ffn_w_gate': _L0_ffn_in['w_gate'], 'L0_ffn_w_up': _L0_ffn_in['w_up'], 'L0_ffn_w_down': _L0_ffn_in['w_down'], 'L1_attn_norm1_w': _L1_attn_in['norm1_w'], 'L1_attn_norm2_w': _L1_attn_in['norm2_w'], 'L1_attn_g_wq': _L1_attn_in['g_wq'], 'L1_attn_g_kv_down': _L1_attn_in['g_kv_down'], 'L1_attn_g_k_up': _L1_attn_in['g_k_up'], 'L1_attn_g_v_up': _L1_attn_in['g_v_up'], 'L1_attn_g_wo': _L1_attn_in['g_wo'], 'L1_attn_l_wq': _L1_attn_in['l_wq'], 'L1_attn_l_wk': _L1_attn_in['l_wk'], 'L1_attn_l_wv': _L1_attn_in['l_wv'], 'L1_attn_l_wo': _L1_attn_in['l_wo'], 'L1_ffn_prototypes': _L1_ffn_in['prototypes'], 'L1_ffn_B': _L1_ffn_in['B'], 'L1_ffn_A': _L1_ffn_in['A'], 'L1_ffn_bias': _L1_ffn_in['bias'], 'L1_ffn_temp': _L1_ffn_in['temp']}

def reference(x, L0_tok_W, L0_tok_b, L0_attn_Wq, L0_attn_Wk, L0_attn_Wv, L0_attn_Wo, L0_ffn_w_gate, L0_ffn_w_up, L0_ffn_w_down, L1_attn_norm1_w, L1_attn_norm2_w, L1_attn_g_wq, L1_attn_g_kv_down, L1_attn_g_k_up, L1_attn_g_v_up, L1_attn_g_wo, L1_attn_l_wq, L1_attn_l_wk, L1_attn_l_wv, L1_attn_l_wo, L1_ffn_prototypes, L1_ffn_B, L1_ffn_A, L1_ffn_bias, L1_ffn_temp):
    import jax
    import jax.numpy as jnp

    def _L0_tok_ref(x, W, b):
        import jax, jax.numpy as jnp
        import numpy as np
        IMG = 96
        P = 16
        C = 3
        D = 256
        B = 64
        Bsz, Cc, H, Wd = x.shape
        gh, gw = (H // P, Wd // P)
        patches = x.reshape(Bsz, Cc, gh, P, gw, P).transpose(0, 2, 4, 1, 3, 5)
        patches = patches.reshape(Bsz, gh * gw, Cc * P * P)
        return jnp.einsum('bnf,df->bnd', patches, W) + b

    def _L0_attn_ref(x, Wq, Wk, Wv, Wo):
        import jax, jax.numpy as jnp
        import numpy as np
        H = 16
        G = 4
        THETA = 10000.0

        def _rope(x, cos, sin):
            x0 = x[..., ::2]
            x1 = x[..., 1::2]
            r0 = x0 * cos - x1 * sin
            r1 = x0 * sin + x1 * cos
            return jnp.stack([r0, r1], axis=-1).reshape(x.shape)
        B, S, D = x.shape
        hd = D // H
        Hkv = H // G
        q = x @ Wq
        k = x @ Wk
        v = x @ Wv
        k = jnp.repeat(k.reshape(B, S, Hkv, hd), G, axis=2)
        v = jnp.repeat(v.reshape(B, S, Hkv, hd), G, axis=2)
        inv = 1.0 / THETA ** (jnp.arange(0, D, 2, dtype=jnp.float32) / D)
        ang = jnp.arange(S, dtype=jnp.float32)[:, None] * inv[None, :]
        q = _rope(q, jnp.cos(ang)[None], jnp.sin(ang)[None])
        angk = ang[:, :hd // 2]
        k = _rope(k, jnp.cos(angk)[None, :, None, :], jnp.sin(angk)[None, :, None, :])
        q = q.reshape(B, S, H, hd).transpose(0, 2, 1, 3)
        k = k.transpose(0, 2, 1, 3)
        v = v.transpose(0, 2, 1, 3)
        scores = jnp.einsum('bhqd,bhkd->bhqk', q, k) / jnp.sqrt(jnp.float32(D))
        p = jax.nn.softmax(scores, axis=-1)
        o = jnp.einsum('bhqk,bhkd->bhqd', p, v)
        o = o.transpose(0, 2, 1, 3).reshape(B, S, D)
        return o @ Wo

    def _L0_ffn_ref(x, w_gate, w_up, w_down):
        import jax, jax.numpy as jnp
        import numpy as np
        BLOCK = 32
        W_BITS = 4
        ACT_BITS = 16

        def act_qdq(x):
            qmax = 2.0 ** (ACT_BITS - 1) - 1.0
            scale = jnp.maximum(jnp.max(jnp.abs(x)) / qmax, 1e-12)
            return jnp.clip(jnp.round(x / scale), -qmax - 1.0, qmax) * scale

        def fixed_qdq_u16(x):
            scale = 1.0 / 65536.0
            return jnp.clip(jnp.round(x / scale), 0.0, 65535.0) * scale

        def lpbq_dequant(w):
            O, I = w.shape
            qmax = 2.0 ** (W_BITS - 1) - 1.0
            wb = w.reshape(O, I // BLOCK, BLOCK)
            s = jnp.maximum(jnp.max(jnp.abs(wb), axis=-1, keepdims=True) / qmax, 1e-12)
            wq = jnp.clip(jnp.round(wb / s), -qmax - 1.0, qmax) * s
            return wq.reshape(O, I)
        x = act_qdq(x)
        up = act_qdq(x @ lpbq_dequant(w_up).T)
        gate = act_qdq(x @ lpbq_dequant(w_gate).T)
        sig = fixed_qdq_u16(jax.nn.sigmoid(gate))
        gate = act_qdq(gate * sig)
        o = act_qdq(gate * up)
        return o @ lpbq_dequant(w_down).T

    def _L1_attn_ref(hidden, norm1_w, norm2_w, g_wq, g_kv_down, g_k_up, g_v_up, g_wo, l_wq, l_wk, l_wv, l_wo):
        import jax, jax.numpy as jnp
        import numpy as np
        D = 256
        H = 16
        KVH = 4
        HD = D // H
        LAT = 64
        WIN = 64
        B, S = (1, 512)
        BASE_G, BASE_L = (1000000.0, 10000.0)
        EPS = 1e-06

        def rmsnorm(x, w):
            return x * jax.lax.rsqrt(jnp.mean(x * x, axis=-1, keepdims=True) + EPS) * w

        def qk_norm(x):
            return x * jax.lax.rsqrt(jnp.mean(x * x, axis=-1, keepdims=True) + EPS)

        def rope(x, base):
            s, hd = (x.shape[-2], x.shape[-1])
            inv_freq = 1.0 / base ** (jnp.arange(0, hd, 2, dtype=jnp.float32) / hd)
            freqs = jnp.arange(s, dtype=jnp.float32)[:, None] * inv_freq[None, :]
            cos, sin = (jnp.cos(freqs), jnp.sin(freqs))
            xe, xo = (x[..., ::2], x[..., 1::2])
            out = jnp.stack([xe * cos - xo * sin, xe * sin + xo * cos], axis=-1)
            return out.reshape(x.shape)

        def split_heads(x, n_heads):
            b, s, _ = x.shape
            return x.reshape(b, s, n_heads, HD).transpose(0, 2, 1, 3)

        def repeat_kv(x):
            return jnp.repeat(x, H // KVH, axis=1)

        def sdpa(q, k, v, mask):
            scores = jnp.einsum('bhqd,bhkd->bhqk', q, k) / np.sqrt(HD).astype(np.float32)
            scores = jnp.where(mask, scores, jnp.float32(-1e+30))
            probs = jax.nn.softmax(scores, axis=-1)
            return jnp.einsum('bhqk,bhkd->bhqd', probs, v)

        def merge_heads(x):
            b, h, s, hd = x.shape
            return x.transpose(0, 2, 1, 3).reshape(b, s, h * hd)

        def global_latent_attn(x, wq, w_kv_down, w_k_up, w_v_up, wo):
            q = split_heads(x @ wq, H)
            latent = x @ w_kv_down
            k = split_heads(latent @ w_k_up, KVH)
            v = split_heads(latent @ w_v_up, KVH)
            q, k = (rope(q, BASE_G), rope(k, BASE_G))
            q, k = (qk_norm(q), qk_norm(k))
            k, v = (repeat_kv(k), repeat_kv(v))
            i = jnp.arange(x.shape[1])
            causal = i[:, None] >= i[None, :]
            return merge_heads(sdpa(q, k, v, causal)) @ wo

        def local_gqa_attn(x, wq, wk, wv, wo):
            q = split_heads(x @ wq, H)
            k = split_heads(x @ wk, KVH)
            v = split_heads(x @ wv, KVH)
            q, k = (rope(q, BASE_L), rope(k, BASE_L))
            q, k = (qk_norm(q), qk_norm(k))
            k, v = (repeat_kv(k), repeat_kv(v))
            i = jnp.arange(x.shape[1])
            diff = i[:, None] - i[None, :]
            mask = (diff >= 0) & (diff < WIN)
            return merge_heads(sdpa(q, k, v, mask)) @ wo
        x = hidden
        x = x + global_latent_attn(rmsnorm(x, norm1_w), g_wq, g_kv_down, g_k_up, g_v_up, g_wo)
        x = x + local_gqa_attn(rmsnorm(x, norm2_w), l_wq, l_wk, l_wv, l_wo)
        return x

    def _L1_ffn_ref(x, prototypes, B, A, bias, temp):
        import jax, jax.numpy as jnp
        import numpy as np
        IN_DIM, OUT_DIM, N_PROTO, RANK = (256, 256, 32, 16)
        lead = x.shape[:-1]
        xf = x.reshape(-1, IN_DIM)
        x2 = jnp.sum(xf * xf, axis=1, keepdims=True)
        p2 = jnp.sum(prototypes * prototypes, axis=1)
        d2 = x2 + p2[None, :] - 2.0 * (xf @ prototypes.T)
        dists = jnp.sqrt(jnp.maximum(d2, 0.0))
        t = jnp.maximum(jnp.abs(temp), 0.1)
        w = jax.nn.softmax(-dists / t, axis=1)
        topw, topi = jax.lax.top_k(w, 2)
        topw = topw / jnp.sum(topw, axis=1, keepdims=True)
        out = jnp.zeros((xf.shape[0], OUT_DIM), dtype=xf.dtype)
        for tslot in range(2):
            idx = topi[:, tslot]
            wt = topw[:, tslot:tslot + 1]
            h = jnp.einsum('nri,ni->nr', B[idx], xf)
            y = jnp.einsum('nor,nr->no', A[idx], h) + bias[idx]
            out = out + wt * y
        return out.reshape(*lead, OUT_DIM)
    h = _L0_tok_ref(x, L0_tok_W, L0_tok_b)
    h = h + _L0_attn_ref(_layernorm(h, axis=-1), L0_attn_Wq, L0_attn_Wk, L0_attn_Wv, L0_attn_Wo)
    h = h + _L0_ffn_ref(_layernorm(h, axis=-1), L0_ffn_w_gate, L0_ffn_w_up, L0_ffn_w_down)
    h = h + _L1_attn_ref(_layernorm(h, axis=-1), L1_attn_norm1_w, L1_attn_norm2_w, L1_attn_g_wq, L1_attn_g_kv_down, L1_attn_g_k_up, L1_attn_g_v_up, L1_attn_g_wo, L1_attn_l_wq, L1_attn_l_wk, L1_attn_l_wv, L1_attn_l_wo)
    h = h + _L1_ffn_ref(_layernorm(h, axis=-1), L1_ffn_prototypes, L1_ffn_B, L1_ffn_A, L1_ffn_bias, L1_ffn_temp)
    return h

_drawn_inputs = setup_inputs


def setup_inputs(seed=0):
    import zlib

    import numpy as np

    out = dict(_drawn_inputs(seed))
    spreads = {'L1_attn_norm1_w': (1.0, 0.6), 'L1_attn_norm2_w': (1.0, 0.6), 'L1_ffn_bias': (0.0, 0.59)}
    factors = {'L0_attn_Wq': 8.0,
     'L0_attn_Wk': 8.0,
     'L1_attn_g_wq': 8.0,
     'L1_attn_g_kv_down': 8.0,
     'L1_attn_g_k_up': 8.0,
     'L1_attn_g_v_up': 8.0,
     'L1_attn_g_wo': 8.0,
     'L1_attn_l_wq': 20.914,
     'L1_attn_l_wk': 21.651,
     'L1_ffn_B': 4.967,
     'L1_ffn_A': 4.96}
    for name, (base, spread) in spreads.items():
        noise = np.random.default_rng([zlib.crc32(name.encode()), seed]).standard_normal(out[name].shape)
        drawn = base * np.exp(spread * noise) if base else spread * noise
        out[name] = jnp.asarray(drawn.astype(out[name].dtype))
    for name, factor in factors.items():
        out[name] = (out[name] * factor).astype(out[name].dtype)
    return out
```

```python
from contextlib import ExitStack

import numpy as np
import concourse.bass as bass
from concourse import mybir

F32 = mybir.dt.float32
I16 = mybir.dt.int16
U16 = mybir.dt.uint16
U32 = mybir.dt.uint32
ALU = mybir.AluOpType
ACT = mybir.ActivationFunctionType
AX = mybir.AxisListType
MAX_ALL = bass.bass_isa.ReduceOp.max

P = 128
D = 256
KC = D // P
IMAGES, SEQ = 64, 64
TILE = 2 * SEQ
TILES = IMAGES * SEQ // TILE
PATCH = 3 * 16 * 16
PC = PATCH // P
HEADS, GROUPS, HD = 16, 4, 16
QK = D + GROUPS * HD
QKV = QK + GROUPS * HD
LATENT = 64
ROPED = HEADS + GROUPS
LN_EPS, RMS_EPS = 1e-5, 1e-6


def wait_for(eng, sem, count):
    if isinstance(count, int) and count <= 0:
        return
    eng.wait_ge(sem, count)


def carrier(nc, spare):
    nc.vector.memset(spare, 0.0)


def over(eng, step, count, depth, peel):
    for t in range(peel):
        step(t, t // 2, t % 2, lambda lag: lag <= t)
    with eng.Fori(peel // 2, count // 2) as i:
        for s in range(2):
            step(2 * i + s, i, s, lambda lag: True)
    for t in range(count, count + depth):
        step(t, t // 2, t % 2, lambda lag: t - lag < count)


def after(n, count):
    return 0 if isinstance(n, int) and n <= 0 else count


def upto_last(n, per=1):
    return per * min(n, TILES) if isinstance(n, int) else per * n


def attention_phase(nc, mode, dram, keep):
    patch, latent, normed = mode == "patch", mode == "global", mode != "patch"
    scale = 1.0 / 16 if patch else 1.0 / 4
    h_all, x_all, identity, consts = keep["h"], keep["x"], keep["identity"], keep["consts"]
    half_neg = consts[:, 0:1]
    with ExitStack() as ctx:
        def sb(name, shape, dt=F32):
            return ctx.enter_context(nc.sbuf_tensor(f"{mode}_{name}", shape, dt))

        def bank(name, shape):
            return ctx.enter_context(nc.psum_tensor(f"{mode}_{name}", shape, F32))

        def sem(name):
            return ctx.enter_context(nc.semaphore(f"{mode}_{name}"))

        qkv_cols = D if latent else QKV
        w_qkv = sb("w_qkv", [P, KC, qkv_cols])
        w_out = sb("w_out", [P, KC, D])
        cos_t = sb("cos", [P, QK])
        sin_t = sb("sin", [P, QK])
        k_mask = sb("k_mask", [P, 2])
        if patch:
            w_patch = sb("w_patch", [P, PC, D])
            b_patch = sb("b_patch", [P, D])
            patches = sb("patches", [P, 2, PC, TILE])
        else:
            causal = sb("causal", [P, SEQ])
            w_norm = sb("w_norm", [P, D])
        if latent:
            w_down = sb("w_down", [P, KC, LATENT])
            w_kv_up = sb("w_kv_up", [LATENT, 2 * GROUPS * HD])
            lat = sb("lat", [LATENT, 2, TILE])
        stats = sb("stats", [P, 2, 6])
        spare = sb("spare", [P, 1])
        mean_var = sb("mean_var", [P, 2, 2])
        small = sb("small", [P, 2, 4])
        rstd = sb("rstd", [P, 2, 2])
        xn = sb("xn", [P, 2, D])
        xT = sb("xT", [P, 2, KC, TILE])
        by_cos = sb("by_cos", [P, ROPED, 2, HD // 2])
        by_sin = sb("by_sin", [P, ROPED, 2, HD // 2])
        qk = sb("qk", [P, 2, ROPED, 2, HD // 2])
        qT = sb("qT", [P, 2, 2, 2, SEQ])
        k_diag = sb("k_diag", [P, 2, 2, 2, SEQ])
        v_diag = sb("v_diag", [P, 2, 2, 2, 2, HD + 1])
        probs = sb("probs", [P, 2, 4, 2 * P])
        rden = sb("rden", [P, 16])
        attn = sb("attn", [P, 2, 2, P])
        aT = sb("aT", [P, 2, 2, 2, SEQ])
        if patch:
            probsT = sb("probsT", [P, 2, 4, 2 * P])
            top = sb("top", [P, 2, 2, 8])
            stats2 = sb("stats2", [P, 2, 6])
            mean_var2 = sb("mean_var2", [P, 2, 2])
            rstd2 = sb("rstd2", [P, 2, 1])
            small2 = sb("small2", [P, 2, 1])
        else:
            squares = sb("squares", [P, ROPED, HD])
            sumsq = sb("sumsq", [P, 2, ROPED])
            qk_rms = sb("qk_rms", [P, 2, ROPED])
            half_negs = sb("half_negs", [P, ROPED])
            rms_eps = sb("rms_eps", [P, ROPED])
            qkn = sb("qkn", [P, 2, ROPED, HD])

        sc = bank("sc", [P, 4, 512])
        hy = bank("hy", [P, 512])
        xa = bank("xa", [P, 512])
        pj = bank("pj", [P, 512])
        qo = bank("qo", [P, 512])

        loads = sem("loads")
        consts_ready = sem("consts_ready")
        if patch:
            patches_loaded = [sem("patches_loaded0"), sem("patches_loaded1")]
            patch_done = sem("patch_done")
            pt_done, pt_ready = sem("pt_done"), sem("pt_ready")
            soft_steps = sem("soft_steps")
            final_steps, final_rstd = sem("final_steps"), sem("final_rstd")
        else:
            squares_ready, rms_steps, scaled, masked = sem("squares"), sem("rms"), sem("scaled"), sem("masked")
        if latent:
            lat_done, lat_ready = sem("lat_done"), sem("lat_ready")
        front_steps, front_pool, xn_ready = sem("front_steps"), sem("front_pool"), sem("xn_ready")
        xt_done, xt_ready = sem("xt_done"), sem("xt_ready")
        qkv_done, rope_steps = sem("qkv_done"), sem("rope_steps")
        qkt_done, qt_ready, kd_ready = sem("qkt_done"), sem("qt_ready"), sem("kd_ready")
        scores_done, exp_done = sem("scores_done"), sem("exp_done")
        pv_done, norm_steps = sem("pv_done"), sem("norm_steps")
        at_done, at_ready, y_done, out_steps = sem("at_done"), sem("at_ready"), sem("y_done"), sem("out_steps")

        FRONT = 3 if patch else 2
        POOLF = 2 if patch else (6 if latent else 4)
        XN = 1 if patch else 2
        ROPE = 8 if patch else 9
        OUT = 3 if patch else (1 if latent else 2)
        DEPTH, PEEL = 5, 8

        loaded = [(w_qkv, dram["w_qkv"]), (w_out, dram["w_out"]), (cos_t, dram["cos"]),
                  (sin_t, dram["sin"]), (k_mask, dram["k_mask"])]
        if patch:
            loaded += [(w_patch, dram["w_patch"]), (b_patch, dram["b_patch"])]
        else:
            loaded += [(causal, dram["causal"]), (w_norm, dram["w_norm"])]
        if latent:
            loaded += [(w_down, dram["w_down"]), (w_kv_up, dram["w_kv_up"])]
        LOADS = 16 * len(loaded)

        block = ctx.enter_context(nc.Block())

        @block.sync
        def _(sp):
            if patch:
                for s in range(2):
                    sp.dma_start(patches[:, s], dram["patches"][s]).then_inc(patches_loaded[s], 16)
            for to, frm in loaded:
                sp.dma_start(to[:], frm).then_inc(loads, 16)
            if patch:
                with sp.Fori(1, TILES // 2) as i:
                    for s in range(2):
                        sp.wait_ge(patch_done, 2 * i + s - 1)
                        sp.dma_start(patches[:, s], dram["patches"][2 * i + s]).then_inc(patches_loaded[s], 16)
            sp.wait_ge(loads, LOADS)

        @block.tensor
        def _(pe):
            pe.wait_ge(loads, LOADS)
            pe.wait_ge(consts_ready, 5)

            def transpose_x(n, s):
                wait_for(pe, xn_ready, XN * (n + 1))
                wait_for(pe, at_ready, n - 3)
                for c in range(KC):
                    mm = pe.transpose(xa[:, c * P:(c + 1) * P], xn[:, s, c * P:(c + 1) * P], identity[:, :])
                mm.then_inc(xt_done, 1)

            def transpose_qk(n, s):
                if patch:
                    wait_for(pe, rope_steps, ROPE * n + 4)
                    rows = qk[:, s].rearrange("p h e i -> p (h e i)")
                else:
                    wait_for(pe, scaled, n + 1)
                    rows = qkn[:, s].rearrange("p h d -> p (h d)")
                wait_for(pe, norm_steps, 2 * (n - 1))
                for a in range(2):
                    pe.transpose(qo[:, a * P:(a + 1) * P], rows[:, a * P:(a + 1) * P], identity[:, :])
                pe.transpose(qo[0:GROUPS * HD, 2 * P:3 * P], rows[:, D:QK], identity[:, :]).then_inc(qkt_done, 1)

            def embed(n, s, i):
                pe.wait_ge(patches_loaded[s], 16 * i + 16)
                wait_for(pe, front_steps, after(n, FRONT * (n - 1) + 1))
                wait_for(pe, out_steps, after(n - 4, OUT * (n - 5) + 1))
                for c in range(PC):
                    mm = pe.matmul(hy[:, 0:D], patches[:, s, c], w_patch[:, c], start=c == 0, stop=c == PC - 1)
                mm.then_inc(patch_done, 1)

            def down(n, s):
                wait_for(pe, xt_ready, n + 1)
                wait_for(pe, out_steps, after(n - 3, OUT * (n - 4) + 1))
                for c in range(KC):
                    mm = pe.matmul(hy[0:LATENT, D:D + TILE], w_down[:, c], xT[:, s, c], start=c == 0, stop=c == KC - 1)
                mm.then_inc(lat_done, 1)

            def project(n, s):
                wait_for(pe, xt_ready, n + 1)
                wait_for(pe, rope_steps, after(n, ROPE * (n - 1) + 8))
                for c in range(KC):
                    mm = pe.matmul(pj[:, 0:qkv_cols], xT[:, s, c], w_qkv[:, c], start=c == 0, stop=c == KC - 1)
                if latent:
                    wait_for(pe, lat_ready, n + 1)
                    mm = pe.matmul(pj[:, D:QKV], lat[:, s], w_kv_up[:, :], start=True, stop=True)
                mm.then_inc(qkv_done, 1)

            def score(n, s):
                wait_for(pe, qt_ready, n + 1)
                wait_for(pe, kd_ready, n + 1)
                for rl in range(2):
                    if patch:
                        wait_for(pe, pt_ready, after(n, 2 * (n - 1) + rl + 1))
                    else:
                        wait_for(pe, exp_done, after(n, 2 * (n - 1) + rl + 1))
                    for j in range(2):
                        t = 2 * rl + j
                        rows = slice(32 * t, 32 * t + 32)
                        for img in range(2):
                            q_side = qT[rows, s, img].rearrange("p a q -> p (a q)")
                            k_side = k_diag[rows, s, img].rearrange("p g k -> p (g k)")
                            out = sc[:, t, img * P:(img + 1) * P]
                            if patch:
                                mm = pe.matmul(out, q_side, k_side, start=True, stop=True)
                            else:
                                mm = pe.matmul(out, k_side, q_side, start=True, stop=True)
                    mm.then_inc(scores_done, 1)

            def transpose_probs(n, s):
                for rl in range(2):
                    wait_for(pe, exp_done, 2 * n + rl + 1)
                    for t in range(2 * rl, 2 * rl + 2):
                        for img in range(2):
                            cols = slice(img * P, (img + 1) * P)
                            mm = pe.transpose(sc[:, t, cols], probs[:, s, t, cols], identity[:, :])
                    mm.then_inc(pt_done, 1)

            def mix(n, s):
                wait_for(pe, pt_ready if patch else masked, 2 * (n + 1))
                wait_for(pe, rope_steps, ROPE * n + 8)
                wait_for(pe, qt_ready, upto_last(n + 2))
                wait_for(pe, kd_ready, upto_last(n + 2))
                src = probsT if patch else probs
                for img in range(2):
                    for t in range(4):
                        at = (img * 4 + t) * 2 * (HD + 1)
                        mm = pe.matmul(qo[:, at:at + 2 * (HD + 1)], src[:, s, t, img * P:(img + 1) * P],
                                       v_diag[:, s, img, t % 2].rearrange("p g d -> p (g d)"), start=True, stop=True)
                mm.then_inc(pv_done, 1)

            def transpose_attn(n, s):
                wait_for(pe, norm_steps, 2 * (n + 1))
                wait_for(pe, xt_ready, upto_last(n + 4))
                for img in range(2):
                    mm = pe.transpose(xa[:, img * P:(img + 1) * P], attn[:, s, img], identity[:, :])
                mm.then_inc(at_done, 1)

            def output(n, s):
                wait_for(pe, at_ready, n + 1)
                if patch:
                    wait_for(pe, front_steps, upto_last(n + 5, FRONT) - (FRONT - 1))
                if latent:
                    wait_for(pe, lat_ready, upto_last(n + 4))
                wait_for(pe, out_steps, after(n, OUT * (n - 1) + 1))
                for a in range(2):
                    mm = pe.matmul(hy[:, 0:D], aT[:, s, a].rearrange("p g q -> p (g q)"), w_out[:, a], start=a == 0, stop=a == 1)
                mm.then_inc(y_done, 1)

            def step(t, i, s, has):
                if has(1):
                    transpose_x(t - 1, 1 - s)
                if has(2):
                    transpose_qk(t - 2, s)
                if patch and has(0):
                    embed(t, s, i)
                if has(4):
                    transpose_attn(t - 4, s)
                if patch and has(3):
                    transpose_probs(t - 3, 1 - s)
                if latent and has(1):
                    down(t - 1, 1 - s)
                if has(3) and not patch:
                    mix(t - 3, 1 - s)
                if has(1):
                    project(t - 1, 1 - s)
                if has(3) and patch:
                    mix(t - 3, 1 - s)
                if has(2):
                    score(t - 2, s)
                if has(4):
                    output(t - 4, s)

            over(pe, step, TILES, DEPTH, PEEL)

        @block.scalar
        def _(act):
            act.wait_ge(consts_ready, 1)

            def keep_xT(n, s):
                wait_for(act, xt_done, n + 1)
                wait_for(act, qkv_done, n - 1)
                nc.scalar.copy(xT[:, s].rearrange("p c t -> p (c t)"), xa[:, 0:KC * TILE]).then_inc(xt_ready, 1)

            def keep_qT(n, s):
                wait_for(act, qkt_done, n + 1)
                wait_for(act, scores_done, 2 * (n - 1))
                nc.scalar.copy(qT[:, s].rearrange("p g a q -> p a g q"),
                               qo[:, 0:2 * TILE].rearrange("p (a g q) -> p a g q", a=2, g=2)).then_inc(qt_ready, 1)

            def keep_aT(n, s):
                wait_for(act, at_done, n + 1)
                wait_for(act, y_done, n - 1)
                nc.scalar.copy(aT[:, s].rearrange("p a g q -> p g a q"),
                               xa[:, 0:2 * P].rearrange("p (g a q) -> p g a q", g=2, a=2)).then_inc(at_ready, 1)

            def keep_probsT(n, s):
                for rl in range(2):
                    wait_for(act, pt_done, 2 * n + rl + 1)
                    wait_for(act, pv_done, n - 1)
                    nc.scalar.copy(probsT[:, s, 2 * rl:2 * rl + 2], sc[:, 2 * rl:2 * rl + 2, 0:2 * P]).then_inc(pt_ready, 1)

            def keep_latent(n, s):
                wait_for(act, lat_done, n + 1)
                wait_for(act, qkv_done, n - 1)
                nc.scalar.copy(lat[:, s], hy[0:LATENT, D:D + TILE]).then_inc(lat_ready, 1)

            def square(n, s):
                wait_for(act, rope_steps, ROPE * n + 4)
                nc.scalar.activation(squares[:].rearrange("p h d -> p (h d)"),
                                     qk[:, s].rearrange("p h e i -> p (h e i)"), ACT.Square, scale=HD ** -0.5).then_inc(squares_ready, 1)

            def exponent(n, s):
                for rl in range(2):
                    part = probs[:, s, 2 * rl:2 * rl + 2]
                    if patch:
                        wait_for(act, soft_steps, 4 * n + 2 * rl + 2)
                        nc.scalar.activation(part, part, ACT.Exp, scale=scale).then_inc(exp_done, 1)
                    else:
                        wait_for(act, scores_done, 2 * n + rl + 1)
                        wait_for(act, pv_done, n - 1)
                        nc.scalar.activation(part, sc[:, 2 * rl:2 * rl + 2, 0:2 * P], ACT.Exp,
                                             scale=scale).then_inc(exp_done, 1)

            def step(t, i, s, has):
                if has(1):
                    keep_xT(t - 1, 1 - s)
                if has(2):
                    keep_qT(t - 2, s)
                if has(4):
                    keep_aT(t - 4, s)
                if patch and has(3):
                    keep_probsT(t - 3, 1 - s)
                if latent and has(1):
                    keep_latent(t - 1, 1 - s)
                if normed and has(1):
                    square(t - 1, 1 - s)
                if has(2):
                    exponent(t - 2, s)

            over(act, step, TILES, DEPTH, PEEL)

        @block.gpsimd
        def _(pool):
            if normed:
                nc.gpsimd.memset(rms_eps[:], RMS_EPS)
                nc.gpsimd.memset(half_negs[:], -0.5).then_inc(front_pool, 1)
                pool.wait_ge(front_pool, 1)
            base = 1 if normed else 0

            def front(n, s):
                wait_for(pool, front_steps, FRONT * (n + 1))
                first = base + POOLF * n
                mean, var = mean_var[:, s, 0:1], mean_var[:, s, 1:2]
                a, b, c = small[:, s, 0:1], small[:, s, 1:2], small[:, s, 2:3]
                if mode != "local":
                    nc.gpsimd.tensor_tensor(a, var, consts[:, 3:4], ALU.add).then_inc(front_pool, 1)
                    pool.wait_ge(front_pool, first + 1)
                    nc.gpsimd.tensor_tensor(rstd[:, s, 0:1], a, half_neg, ALU.pow).then_inc(front_pool, 1)
                    if latent:
                        pool.wait_ge(front_pool, first + 2)
                        nc.gpsimd.tensor_tensor(b, rstd[:, s, 0:1], rstd[:, s, 0:1], ALU.mult).then_inc(front_pool, 1)
                        pool.wait_ge(front_pool, first + 3)
                        nc.gpsimd.tensor_tensor(c, b, var, ALU.mult).then_inc(front_pool, 1)
                        pool.wait_ge(front_pool, first + 4)
                        nc.gpsimd.tensor_tensor(b, c, rms_eps[:, 0:1], ALU.add).then_inc(front_pool, 1)
                        pool.wait_ge(front_pool, first + 5)
                        nc.gpsimd.tensor_tensor(rstd[:, s, 1:2], b, half_neg, ALU.pow).then_inc(front_pool, 1)
                else:
                    nc.gpsimd.tensor_tensor(a, mean, mean, ALU.mult).then_inc(front_pool, 1)
                    pool.wait_ge(front_pool, first + 1)
                    nc.gpsimd.tensor_tensor(b, a, var, ALU.add).then_inc(front_pool, 1)
                    pool.wait_ge(front_pool, first + 2)
                    nc.gpsimd.tensor_tensor(c, b, rms_eps[:, 0:1], ALU.add).then_inc(front_pool, 1)
                    pool.wait_ge(front_pool, first + 3)
                    nc.gpsimd.tensor_tensor(rstd[:, s, 1:2], c, half_neg, ALU.pow).then_inc(front_pool, 1)

            def head_norms(n, s):
                wait_for(pool, rope_steps, ROPE * (n + 1))
                nc.gpsimd.tensor_tensor(sumsq[:, s], sumsq[:, s], rms_eps[:], ALU.add).then_inc(rms_steps, 1)
                wait_for(pool, rms_steps, 2 * n + 1)
                nc.gpsimd.tensor_tensor(qk_rms[:, s], sumsq[:, s], half_negs[:], ALU.pow).then_inc(rms_steps, 1)

            def final(n, s):
                wait_for(pool, out_steps, OUT * (n + 1))
                nc.gpsimd.tensor_tensor(small2[:, s], mean_var2[:, s, 1:2], consts[:, 3:4], ALU.add).then_inc(final_rstd, 1)
                wait_for(pool, final_rstd, 2 * n + 1)
                nc.gpsimd.tensor_tensor(rstd2[:, s], small2[:, s], half_neg, ALU.pow).then_inc(final_rstd, 1)

            pool.wait_ge(consts_ready, 1)

            def step(t, i, s, has):
                if has(0):
                    front(t, s)
                if normed and has(1):
                    head_norms(t - 1, 1 - s)
                if patch and has(4):
                    final(t - 4, s)

            over(pool, step, TILES, DEPTH, PEEL)

        @block.vector
        def _(dve):
            if patch:
                nc.vector.memset(consts[:, 0:1], -0.5)
                nc.vector.memset(consts[:, 3:4], LN_EPS)
            nc.vector.memset(v_diag[:], 0.0).then_inc(consts_ready, 1)
            dve.wait_ge(consts_ready, 1)
            for par in range(2):
                part = slice(par * SEQ, (par + 1) * SEQ)
                for s in range(2):
                    nc.vector.memset(v_diag[part, s, :, :, par, HD:HD + 1].rearrange("p a b c -> p (a b c)"), 1.0).then_inc(consts_ready, 1)
            dve.wait_ge(loads, LOADS)

            def front(n, s):
                first = FRONT * n
                if patch:
                    wait_for(dve, patch_done, n + 1)
                    nc.vector.tensor_tensor(h_all[:, n], hy[:, 0:D], b_patch[:], ALU.add).then_inc(front_steps, 1)
                if patch:
                    dve.wait_ge(front_steps, first + 1)
                src = x_all if mode == "local" else h_all
                carrier(nc, spare[:])
                nc.vector.bn_stats(stats[:, s], src[:, n]).then_inc(front_steps, 1)
                dve.wait_ge(front_steps, first + FRONT - 1)
                wait_for(dve, xn_ready, XN * (n - 1))
                carrier(nc, spare[:])
                nc.vector.bn_aggr(mean_var[:, s], stats[:, s]).then_inc(front_steps, 1)

            def normalise(n, s):
                wait_for(dve, front_pool, (1 if normed else 0) + POOLF * (n + 1))
                wait_for(dve, xt_done, n - 1)
                if patch:
                    nc.vector.tensor_scalar(xn[:, s], h_all[:, n], mean_var[:, s, 0:1], rstd[:, s, 0:1],
                                            ALU.subtract, ALU.mult).then_inc(xn_ready, 1)
                    return
                if latent:
                    nc.vector.tensor_scalar(x_all[:, n], h_all[:, n], mean_var[:, s, 0:1], rstd[:, s, 0:1],
                                            ALU.subtract, ALU.mult).then_inc(xn_ready, 1)
                    wait_for(dve, xn_ready, XN * n + 1)
                    last = 1
                else:
                    last = 2
                nc.vector.scalar_tensor_tensor(xn[:, s], x_all[:, n], rstd[:, s, 1:2], w_norm[:],
                                               ALU.mult, ALU.mult).then_inc(xn_ready, last)

            def rope(n, s):
                first = ROPE * n
                wait_for(dve, qkv_done, n + 1)
                flat = "p h e i -> p (h e i)"
                nc.vector.tensor_tensor(by_cos[:].rearrange(flat), pj[:, 0:QK], cos_t[:], ALU.mult).then_inc(rope_steps, 1)
                nc.vector.tensor_tensor(by_sin[:].rearrange(flat), pj[:, 0:QK], sin_t[:], ALU.mult).then_inc(rope_steps, 1)
                wait_for(dve, qkt_done if patch else scaled, n - 1)
                dve.wait_ge(rope_steps, first + 2)
                for e in range(2):
                    nc.vector.tensor_tensor(qk[:, s, :, e], by_cos[:, :, e], by_sin[:, :, 1 - e], ALU.add).then_inc(rope_steps, 1)
                wait_for(dve, pv_done, n - 1)
                for img in range(2):
                    for par in range(2):
                        nc.vector.tensor_copy(
                            v_diag[par * SEQ:(par + 1) * SEQ, s, img, :, par, 0:HD],
                            pj[img * SEQ:(img + 1) * SEQ, QK + par * 32:QK + par * 32 + 32].rearrange("p (j d) -> p j d", j=2),
                        ).then_inc(rope_steps, 1)
                if normed:
                    wait_for(dve, squares_ready, n + 1)
                    wait_for(dve, rms_steps, 2 * (n - 1))
                    nc.vector.tensor_reduce(sumsq[:, s], squares[:], AX.X, ALU.add).then_inc(rope_steps, 1)

            def scale_heads(n, s):
                wait_for(dve, rms_steps, 2 * (n + 1))
                wait_for(dve, qkt_done, n - 1)
                nc.vector.tensor_tensor(qkn[:, s], qk[:, s].rearrange("p h e i -> p h (e i)"),
                                        qk_rms[:, s, :, None].broadcast_to([P, ROPED, HD]), ALU.mult).then_inc(scaled, 1)

            def mask(n, s):
                for rl in range(2):
                    wait_for(dve, exp_done, 2 * n + rl + 1)
                    part = probs[:, s, 2 * rl:2 * rl + 2].rearrange("p t (c q) -> p (t c) q", q=SEQ)
                    nc.vector.tensor_tensor(part, part, causal[:, None, :].broadcast_to([P, 8, SEQ]), ALU.mult).then_inc(masked, 1)

            def spread_k(n, s):
                wait_for(dve, qt_ready, n + 1)
                wait_for(dve, scores_done, 2 * (n - 1))
                half = [GROUPS * HD, 2, 2, SEQ]
                k_t = qo[0:GROUPS * HD, 2 * P:3 * P].rearrange("p (g k) -> p g k", g=2)[:, :, None, :].broadcast_to(half)
                own = k_mask[0:GROUPS * HD, None, :, None].broadcast_to(half)
                for rl in range(2):
                    ins = nc.vector.tensor_tensor(k_diag[rl * half[0]:(rl + 1) * half[0], s], k_t, own, ALU.mult)
                ins.then_inc(kd_ready, 1)

            def soften(n, s):
                for rl in range(2):
                    wait_for(dve, scores_done, 2 * n + rl + 1)
                    wait_for(dve, pt_done, after(n - 1, 2 * (n - 2) + rl + 1))
                    pair = sc[:, 2 * rl:2 * rl + 2, 0:2 * P].rearrange("p t (c k) -> p t c k", k=SEQ)
                    out = probs[:, s, 2 * rl:2 * rl + 2].rearrange("p t (c k) -> p t c k", k=SEQ)
                    peak = top[:, s, rl].rearrange("p (t c) -> p t c", t=2)
                    nc.vector.tensor_reduce(peak, pair, AX.X, ALU.max).then_inc(soft_steps, 1)
                    wait_for(dve, soft_steps, 4 * n + 2 * rl + 1)
                    nc.vector.tensor_tensor(out, pair, peak[:, :, :, None].broadcast_to([P, 2, 4, SEQ]),
                                            ALU.subtract).then_inc(soft_steps, 1)

            def divide(n, s):
                wait_for(dve, pv_done, n + 1)
                o = qo[:, 0:16 * (HD + 1)].rearrange("p (h d) -> p h d", d=HD + 1)
                nc.vector.reciprocal(rden[:, :, None], o[:, :, HD:HD + 1]).then_inc(norm_steps, 1)
                wait_for(dve, at_done, n - 1)
                wait_for(dve, norm_steps, 2 * n + 1)
                nc.vector.tensor_tensor(attn[:, s].rearrange("p g (h d) -> p (g h) d", d=HD), o[:, :, 0:HD],
                                        rden[:, :, None].broadcast_to([P, 16, HD]), ALU.mult).then_inc(norm_steps, 1)

            def residual(n, s):
                first = OUT * n
                wait_for(dve, y_done, n + 1)
                dst = h_all if patch else x_all
                nc.vector.tensor_tensor(dst[:, n], dst[:, n], hy[:, 0:D], ALU.add).then_inc(out_steps, 1)
                if latent:
                    return
                wait_for(dve, out_steps, first + 1)
                if patch:
                    carrier(nc, spare[:])
                    nc.vector.bn_stats(stats2[:, s], h_all[:, n]).then_inc(out_steps, 1)
                    wait_for(dve, out_steps, first + 2)
                    carrier(nc, spare[:])
                    nc.vector.bn_aggr(mean_var2[:, s], stats2[:, s]).then_inc(out_steps, 1)
                else:
                    nc.vector.tensor_tensor(h_all[:, n], h_all[:, n], x_all[:, n], ALU.add).then_inc(out_steps, 1)

            def final(n, s):
                wait_for(dve, final_rstd, 2 * (n + 1))
                nc.vector.tensor_scalar(x_all[:, n], h_all[:, n], mean_var2[:, s, 0:1], rstd2[:, s], ALU.subtract,
                                        ALU.mult).then_inc(final_steps, 1)
                wait_for(dve, final_steps, 2 * n + 1)
                nc.vector.tensor_reduce(keep["x_peaks"][:, bass.ds(n, 1)],
                                        x_all[:, n], AX.X, ALU.max, apply_absolute_value=True).then_inc(final_steps, 1)

            def step(t, i, s, has):
                if has(1):
                    normalise(t - 1, 1 - s)
                if normed and has(2):
                    scale_heads(t - 2, s)
                if normed and has(3):
                    mask(t - 3, 1 - s)
                if patch and has(5):
                    final(t - 5, 1 - s)
                if has(2):
                    spread_k(t - 2, s)
                if has(0):
                    front(t, s)
                if has(1):
                    rope(t - 1, 1 - s)
                if has(3):
                    divide(t - 3, 1 - s)
                if patch and has(2):
                    soften(t - 2, s)
                if has(4):
                    residual(t - 4, s)

            over(dve, step, TILES, DEPTH, PEEL)


FFN = 768
FC = FFN // P
BLOCK = 32
GROUP = 512
NG = IMAGES * SEQ // GROUP
TPG = GROUP // TILE
Q16, Q4 = 32767.0, 7.0
LEAST_SCALE = 1e-12
MAGIC = 1.5 * 2.0 ** 23


def weights_phase(nc, dram, keep):
    with ExitStack() as ctx:
        def sb(name, shape, dt=F32):
            return ctx.enter_context(nc.sbuf_tensor(f"weights_{name}", shape, dt))

        def sem(name):
            return ctx.enter_context(nc.semaphore(f"weights_{name}"))

        FREE = FC * D
        BLOCKS = FREE // BLOCK
        names = ("ffn_gate", "ffn_up", "ffn_down")
        raw = sb("raw", [P, 3, FREE])
        whole = sb("whole", [P, 3, FREE], I16)
        scale = sb("scale", [P, 3, 2, BLOCKS])
        turned = ctx.enter_context(nc.psum_tensor("weights_turned", [P, 2, 4, P], F32))
        loads, steps, turned_done, kept = sem("loads"), sem("steps"), sem("turned"), sem("kept")
        block = ctx.enter_context(nc.Block())

        @block.sync
        def _(sp):
            sp.dma_start(keep["identity"][:], dram["identity"]).then_inc(loads, 16)
            for w, name in enumerate(names):
                sp.dma_start(raw[:, w], dram[name]).then_inc(loads, 16)
            sp.wait_ge(loads, 64)

        @block.vector
        def _(dve):
            dve.wait_ge(loads, 64)
            for w in range(3):
                blocks = raw[:, w].rearrange("p (b i) -> p b i", i=BLOCK)
                ints = whole[:, w].rearrange("p (b i) -> p b i", i=BLOCK)
                s, inv = scale[:, w, 0], scale[:, w, 1]
                nc.vector.tensor_reduce(s, blocks, AX.X, ALU.max, apply_absolute_value=True).then_inc(steps, 1)
                dve.wait_ge(steps, 5 * w + 1)
                nc.vector.tensor_scalar(s, s, 1.0 / Q4, LEAST_SCALE, ALU.mult, ALU.max).then_inc(steps, 1)
                dve.wait_ge(steps, 5 * w + 2)
                nc.vector.reciprocal(inv, s).then_inc(steps, 1)
                dve.wait_ge(steps, 5 * w + 3)
                nc.vector.tensor_tensor(ints, blocks, inv[:, :, None].broadcast_to([P, BLOCKS, BLOCK]), ALU.mult).then_inc(steps, 1)
                dve.wait_ge(steps, 5 * w + 4)
                nc.vector.tensor_tensor(blocks, ints, s[:, :, None].broadcast_to([P, BLOCKS, BLOCK]), ALU.mult).then_inc(steps, 1)

        @block.tensor
        def _(pe):
            for w in range(3):
                pe.wait_ge(steps, 5 * w + 5)
                for q in range(3):
                    n = 3 * w + q
                    if n >= 2:
                        pe.wait_ge(kept, n - 1)
                    for b in range(4):
                        at = 4 * q + b
                        mm = pe.transpose(turned[:, n % 2, b], raw[:, w, at * P:(at + 1) * P], keep["identity"][:, :])
                    mm.then_inc(turned_done, 1)

        @block.scalar
        def _(act):
            for w, name in enumerate(names):
                for q in range(3):
                    n = 3 * w + q
                    act.wait_ge(turned_done, n + 1)
                    if name == "ffn_down":
                        for b in range(4):
                            oc, ic = divmod(4 * q + b, FC)
                            ins = nc.scalar.copy(keep[name][:, ic, oc * P:(oc + 1) * P], turned[:, n % 2, b])
                    else:
                        out = keep[name][:, :, 2 * q * P:2 * (q + 1) * P].rearrange("p k (o c) -> p o k c", o=2)
                        ins = nc.scalar.copy(out, turned[:, n % 2].rearrange("p (o k) c -> p o k c", o=2))
                    ins.then_inc(kept, 1)


def gate_phase(nc, keep):
    with ExitStack() as ctx:
        def sb(name, shape, dt=F32):
            return ctx.enter_context(nc.sbuf_tensor(f"gate_{name}", shape, dt))

        def sem(name):
            return ctx.enter_context(nc.semaphore(f"gate_{name}"))

        x_all, gate, w_gate, sc = keep["x"], keep["gate"], keep["ffn_gate"], keep["scales"]
        magic_x = sb("magic_x", [P, 2, TPG * D])
        top = sb("top", [P, 2])
        prod = ctx.enter_context(nc.psum_tensor("gate_prod", [P, FC, GROUP], F32))
        turned = ctx.enter_context(nc.psum_tensor("gate_turned", [P, 2, 512], F32))
        scale_steps, quant, turned_done, xq_ready = sem("scale_steps"), sem("quant"), sem("turned"), sem("xq_ready")
        prod_done, kept, peaked = sem("prod_done"), sem("kept"), sem("peaked")
        block = ctx.enter_context(nc.Block())

        @block.gpsimd
        def _(pool):
            pool.wait_ge(scale_steps, 1)
            nc.gpsimd.partition_all_reduce(top[:, 1:2], top[:, 0:1], P, MAX_ALL).then_inc(scale_steps, 1)

        @block.vector
        def _(dve):
            nc.vector.tensor_reduce(top[:, 0:1], keep["x_peaks"][:], AX.X, ALU.max).then_inc(scale_steps, 1)
            dve.wait_ge(scale_steps, 2)
            nc.vector.tensor_scalar(sc[:, 0:1], top[:, 1:2], 1.0 / Q16, LEAST_SCALE, ALU.mult, ALU.max).then_inc(scale_steps, 1)
            dve.wait_ge(scale_steps, 3)
            nc.vector.reciprocal(sc[:, 1:2], sc[:, 0:1]).then_inc(scale_steps, 1)
            dve.wait_ge(scale_steps, 4)

            def quantise(g, s):
                wait_for(dve, turned_done, 2 * (g - 1))
                nc.vector.tensor_scalar(magic_x[:, s], x_all[:, bass.ds(g * TPG, TPG)].rearrange("p t d -> p (t d)"),
                                        sc[:, 1:2], MAGIC, ALU.mult, ALU.add).then_inc(quant, 1)

            def peak(g):
                for oc in range(FC):
                    wait_for(dve, kept, FC * g + oc + 1)
                    nc.vector.tensor_reduce(keep["gate_peaks"][:, oc, bass.ds(g, 1)], gate[:, oc, bass.ds(g * GROUP, GROUP)],
                                            AX.X, ALU.max, apply_absolute_value=True).then_inc(peaked, 1)

            def step(t, i, s, has):
                if has(0):
                    quantise(t, s)
                if has(1):
                    peak(t - 1)

            over(dve, step, NG, 1, 2)

        @block.tensor
        def _(pe):
            def turn(g, s):
                wait_for(pe, quant, g + 1)
                for half in range(2):
                    wait_for(pe, xq_ready, after(g, 2 * (g - 1) + half + 1))
                    for c in range(4):
                        at = (4 * half + c) * P
                        mm = pe.transpose(turned[:, half, c * P:(c + 1) * P], magic_x[:, s, at:at + P], keep["identity"][:, :])
                    mm.then_inc(turned_done, 1)

            def product(g):
                wait_for(pe, xq_ready, 2 * (g + 1))
                for oc in range(FC):
                    wait_for(pe, kept, after(g, FC * (g - 1) + oc + 1))
                    for c in range(KC):
                        mm = pe.matmul(prod[:, oc], w_gate[:, c, oc * P:(oc + 1) * P],
                                       x_all[:, bass.ds(g * TPG, TPG), c * P:(c + 1) * P], start=c == 0, stop=c == KC - 1)
                    mm.then_inc(prod_done, 1)

            def step(t, i, s, has):
                if has(0):
                    turn(t, s)
                if has(1):
                    product(t - 1)

            over(pe, step, NG, 1, 2)

        @block.scalar
        def _(act):
            def keep_x(g, s):
                for half in range(2):
                    wait_for(act, turned_done, 2 * g + half + 1)
                    nc.scalar.activation(x_all[:, bass.ds(g * TPG + 2 * half, 2)].rearrange("p t d -> p (t d)"),
                                         turned[:, half], ACT.Copy, bias=-MAGIC).then_inc(xq_ready, 1)

            def keep_gate(g):
                for oc in range(FC):
                    wait_for(act, prod_done, FC * g + oc + 1)
                    nc.scalar.copy(gate[:, oc, bass.ds(g * GROUP, GROUP)], prod[:, oc]).then_inc(kept, 1)

            def step(t, i, s, has):
                if has(0):
                    keep_x(t, s)
                if has(1):
                    keep_gate(t - 1)

            over(act, step, NG, 1, 2)


def up_phase(nc, keep):
    with ExitStack() as ctx:
        def sb(name, shape, dt=F32):
            return ctx.enter_context(nc.sbuf_tensor(f"up_{name}", shape, dt))

        def sem(name):
            return ctx.enter_context(nc.semaphore(f"up_{name}"))

        x_all, gate, w_up, sc = keep["x"], keep["gate"], keep["ffn_up"], keep["scales"]
        up_rows = sb("up_rows", [P, 3, GROUP])
        gate_int = sb("gate_int", [P, 2, GROUP], I16)
        sig = sb("sig", [P, 2, GROUP])
        sig_int = sb("sig_int", [P, GROUP], U16)
        top = sb("top", [P, 4])
        prod = ctx.enter_context(nc.psum_tensor("up_prod", [P, FC, GROUP], F32))
        scale_steps, prod_done, kept, peaked, stored = (
            sem("scale_steps"), sem("prod_done"), sem("kept"), sem("peaked"), [sem("stored0"), sem("stored1"), sem("stored2")])
        gate_ready, sig_ready, chain = sem("gate_ready"), sem("sig_ready"), sem("chain")
        block = ctx.enter_context(nc.Block())

        @block.gpsimd
        def _(pool):
            pool.wait_ge(scale_steps, 1)
            nc.gpsimd.partition_all_reduce(top[:, 1:2], top[:, 0:1], P, MAX_ALL).then_inc(scale_steps, 1)

        @block.sync
        def _(sp):
            with sp.Fori(0, NG) as g:
                for oc in range(FC):
                    sp.wait_ge(kept, FC * g + oc + 1)
                    sp.dma_start(keep["up_dram"][:, oc, bass.ds(g * GROUP, GROUP)], up_rows[:, oc % 3]).then_inc(stored[oc % 3], 16)
            for q in stored:
                sp.wait_ge(q, 16 * NG * FC // 3)

        @block.tensor
        def _(pe):
            def product(g):
                for oc in range(FC):
                    wait_for(pe, peaked, after(g, FC * (g - 1) + oc + 1))
                    for c in range(KC):
                        mm = pe.matmul(prod[:, oc], w_up[:, c, oc * P:(oc + 1) * P],
                                       x_all[:, bass.ds(g * TPG, TPG), c * P:(c + 1) * P], start=c == 0, stop=c == KC - 1)
                    mm.then_inc(prod_done, 1)

            over(pe, lambda t, i, s, has: product(t), NG, 0, 2)

        @block.scalar
        def _(act):
            act.wait_ge(scale_steps, 6)

            def step(g, i, s, has):
                for oc in range(FC):
                    wait_for(act, prod_done, FC * g + oc + 1)
                    wait_for(act, stored[oc % 3], 16 * (2 * g + oc // 3))
                    nc.scalar.copy(up_rows[:, oc % 3], prod[:, oc]).then_inc(kept, 1)
                    wait_for(act, gate_ready, FC * g + oc + 1)
                    wait_for(act, chain, 2 * (FC * g + oc) - 3)
                    nc.scalar.activation(sig[:, oc % 2], gate_int[:, oc % 2], ACT.Sigmoid, scale=sc[:, 2:3]).then_inc(sig_ready, 1)

            over(act, step, NG, 0, 2)

        @block.vector
        def _(dve):
            nc.vector.tensor_reduce(top[:, 0:1], keep["gate_peaks"][:], AX.XY, ALU.max).then_inc(scale_steps, 1)
            dve.wait_ge(scale_steps, 2)
            nc.vector.tensor_scalar(top[:, 2:3], top[:, 1:2], sc[:, 0:1], None, ALU.mult).then_inc(scale_steps, 1)
            dve.wait_ge(scale_steps, 3)
            nc.vector.tensor_scalar(sc[:, 2:3], top[:, 2:3], 1.0 / Q16, LEAST_SCALE, ALU.mult, ALU.max).then_inc(scale_steps, 1)
            dve.wait_ge(scale_steps, 4)
            nc.vector.reciprocal(top[:, 3:4], sc[:, 2:3]).then_inc(scale_steps, 1)
            dve.wait_ge(scale_steps, 5)
            nc.vector.tensor_tensor(sc[:, 3:4], top[:, 3:4], sc[:, 0:1], ALU.mult).then_inc(scale_steps, 1)
            dve.wait_ge(scale_steps, 6)

            def whole_gate(g, oc):
                wait_for(dve, sig_ready, FC * g + oc - 1)
                nc.vector.tensor_scalar(gate_int[:, oc % 2], gate[:, oc, bass.ds(g * GROUP, GROUP)], sc[:, 3:4], None,
                                        ALU.mult).then_inc(gate_ready, 1)

            def rest(g, oc):
                n = FC * g + oc
                wait_for(dve, kept, n + 1)
                nc.vector.tensor_reduce(keep["up_peaks"][:, oc, bass.ds(g, 1)], prod[:, oc], AX.X, ALU.max,
                                        apply_absolute_value=True).then_inc(peaked, 1)
                wait_for(dve, sig_ready, n + 1)
                nc.vector.tensor_scalar(sig_int[:], sig[:, oc % 2], 65536.0, 65535.0, ALU.mult, ALU.min).then_inc(chain, 1)
                wait_for(dve, chain, 2 * n + 1)
                span = gate[:, oc, bass.ds(g * GROUP, GROUP)]
                nc.vector.tensor_tensor(span, gate_int[:, oc % 2], sig_int[:], ALU.mult).then_inc(chain, 1)
                wait_for(dve, chain, 2 * n + 2)
                nc.vector.tensor_reduce(keep["silu_peaks"][:, oc, bass.ds(g, 1)], span, AX.X, ALU.max, apply_absolute_value=True)

            def step(g, i, s, has):
                for oc in range(FC):
                    whole_gate(g, oc)
                    rest(g, oc)

            over(dve, step, NG, 0, 2)


def mix_phase(nc, keep):
    UNIT = 1024
    UNITS = IMAGES * SEQ // UNIT
    with ExitStack() as ctx:
        def sb(name, shape, dt=F32):
            return ctx.enter_context(nc.sbuf_tensor(f"mix_{name}", shape, dt))

        def sem(name):
            return ctx.enter_context(nc.semaphore(f"mix_{name}"))

        gate, sc = keep["gate"], keep["scales"]
        up_rows = sb("up_rows", [P, 3, UNIT])
        up_int = sb("up_int", [P, 2, UNIT], I16)
        gate_int = sb("gate_int", [P, UNIT], I16)
        top = sb("top", [P, 8])
        scale_steps, up_ready, chain = sem("scale_steps"), sem("up_ready"), sem("chain")
        loaded = [sem("loaded0"), sem("loaded1"), sem("loaded2")]
        block = ctx.enter_context(nc.Block())

        @block.sync
        def _(sp):
            def step(u, i, s, has):
                for oc in range(FC):
                    wait_for(sp, up_ready, FC * u + oc - 2)
                    sp.dma_start(up_rows[:, oc % 3], keep["up_dram"][:, oc, bass.ds(u * UNIT, UNIT)]).then_inc(loaded[oc % 3], 16)

            over(sp, step, UNITS, 0, 2)

        @block.gpsimd
        def _(pool):
            pool.wait_ge(scale_steps, 2)
            nc.gpsimd.partition_all_reduce(top[:, 2:4], top[:, 0:2], P, MAX_ALL).then_inc(scale_steps, 1)

        @block.scalar
        def _(act):
            act.wait_ge(scale_steps, 8)

            def step(u, i, s, has):
                for oc in range(FC):
                    n = FC * u + oc
                    wait_for(act, loaded[oc % 3], 16 * (2 * u + oc // 3 + 1))
                    wait_for(act, chain, 2 * (n - 1))
                    nc.scalar.activation(up_int[:, oc % 2], up_rows[:, oc % 3], ACT.Copy, scale=sc[:, 5:6]).then_inc(up_ready, 1)

            over(act, step, UNITS, 0, 2)

        @block.vector
        def _(dve):
            nc.vector.tensor_reduce(top[:, 0:1], keep["up_peaks"][:], AX.XY, ALU.max).then_inc(scale_steps, 1)
            nc.vector.tensor_reduce(top[:, 1:2], keep["silu_peaks"][:], AX.XY, ALU.max).then_inc(scale_steps, 1)
            dve.wait_ge(scale_steps, 3)
            nc.vector.tensor_scalar(top[:, 4:5], top[:, 2:3], sc[:, 0:1], None, ALU.mult).then_inc(scale_steps, 1)
            nc.vector.tensor_scalar(top[:, 5:6], top[:, 3:4], sc[:, 2:3], 1.0 / 65536, ALU.mult, ALU.mult).then_inc(scale_steps, 1)
            dve.wait_ge(scale_steps, 5)
            nc.vector.tensor_scalar(sc[:, 6:8], top[:, 4:6], 1.0 / Q16, LEAST_SCALE, ALU.mult, ALU.max).then_inc(scale_steps, 1)
            dve.wait_ge(scale_steps, 6)
            nc.vector.reciprocal(top[:, 0:2], sc[:, 6:8]).then_inc(scale_steps, 1)
            dve.wait_ge(scale_steps, 7)
            nc.vector.tensor_scalar(sc[:, 4:5], top[:, 1:2], sc[:, 2:3], 1.0 / 65536, ALU.mult, ALU.mult)
            nc.vector.tensor_tensor(sc[:, 5:6], top[:, 0:1], sc[:, 0:1], ALU.mult).then_inc(scale_steps, 1)
            dve.wait_ge(scale_steps, 8)

            def step(u, i, s, has):
                for oc in range(FC):
                    n = FC * u + oc
                    span = gate[:, oc, bass.ds(u * UNIT, UNIT)]
                    nc.vector.tensor_scalar(gate_int[:], span, sc[:, 4:5], None, ALU.mult).then_inc(chain, 1)
                    wait_for(dve, chain, 2 * n + 1)
                    wait_for(dve, up_ready, n + 1)
                    nc.vector.tensor_tensor(span, gate_int[:], up_int[:, oc % 2], ALU.mult).then_inc(chain, 1)
                    wait_for(dve, chain, 2 * n + 2)
                    nc.vector.tensor_reduce(keep["out_peaks"][:, oc, bass.ds(u, 1)], span, AX.X, ALU.max, apply_absolute_value=True)

            over(dve, step, UNITS, 0, 2)


def down_phase(nc, keep):
    with ExitStack() as ctx:
        def sb(name, shape, dt=F32):
            return ctx.enter_context(nc.sbuf_tensor(f"down_{name}", shape, dt))

        def sem(name):
            return ctx.enter_context(nc.semaphore(f"down_{name}"))

        h_all, gate, w_down, sc = keep["h"], keep["gate"], keep["ffn_down"], keep["scales"]
        magic = sb("magic", [P, 2, FC, TILE])
        whole = sb("whole", [P, 2, FC, TILE])
        top = sb("top", [P, 4])
        out = ctx.enter_context(nc.psum_tensor("down_out", [P, 2, 512], F32))
        scale_steps, rounded, whole_ready, down_done, added = (
            sem("scale_steps"), sem("rounded"), sem("whole_ready"), sem("down_done"), sem("added"))
        block = ctx.enter_context(nc.Block())

        @block.gpsimd
        def _(pool):
            pool.wait_ge(scale_steps, 1)
            nc.gpsimd.partition_all_reduce(top[:, 1:2], top[:, 0:1], P, MAX_ALL).then_inc(scale_steps, 1)

        @block.scalar
        def _(act):
            def step(n, i, s, has):
                wait_for(act, rounded, n + 1)
                wait_for(act, down_done, n - 1)
                nc.scalar.activation(whole[:, s].rearrange("p c t -> p (c t)"), magic[:, s].rearrange("p c t -> p (c t)"),
                                     ACT.Copy, bias=-MAGIC).then_inc(whole_ready, 1)

            over(act, step, TILES, 0, 4)

        @block.tensor
        def _(pe):
            def step(n, i, s, has):
                wait_for(pe, whole_ready, n + 1)
                wait_for(pe, added, n - 1)
                for c in range(FC):
                    mm = pe.matmul(out[:, s, 0:D], whole[:, s, c], w_down[:, c], start=c == 0, stop=c == FC - 1)
                mm.then_inc(down_done, 1)

            over(pe, step, TILES, 0, 4)

        @block.vector
        def _(dve):
            nc.vector.tensor_reduce(top[:, 0:1], keep["out_peaks"][:], AX.XY, ALU.max).then_inc(scale_steps, 1)
            dve.wait_ge(scale_steps, 2)
            nc.vector.tensor_scalar(top[:, 2:3], top[:, 1:2], sc[:, 6:7], sc[:, 7:8], ALU.mult, ALU.mult).then_inc(scale_steps, 1)
            dve.wait_ge(scale_steps, 3)
            nc.vector.tensor_scalar(sc[:, 8:9], top[:, 2:3], 1.0 / Q16, LEAST_SCALE, ALU.mult, ALU.max).then_inc(scale_steps, 1)
            dve.wait_ge(scale_steps, 4)
            nc.vector.reciprocal(top[:, 3:4], sc[:, 8:9]).then_inc(scale_steps, 1)
            dve.wait_ge(scale_steps, 5)
            nc.vector.tensor_scalar(sc[:, 9:10], top[:, 3:4], sc[:, 6:7], sc[:, 7:8], ALU.mult, ALU.mult).then_inc(scale_steps, 1)
            dve.wait_ge(scale_steps, 6)

            def round_out(n, s):
                wait_for(dve, whole_ready, n - 1)
                nc.vector.tensor_scalar(magic[:, s], gate[:, :, bass.ds(n * TILE, TILE)], sc[:, 9:10], MAGIC,
                                        ALU.mult, ALU.add).then_inc(rounded, 1)

            def add(n, s):
                wait_for(dve, down_done, n + 1)
                nc.vector.scalar_tensor_tensor(h_all[:, n], out[:, s, 0:D], sc[:, 8:9], h_all[:, n], ALU.mult,
                                               ALU.add).then_inc(added, 1)

            def step(t, i, s, has):
                if has(0):
                    round_out(t, s)
                if has(1):
                    add(t - 1, 1 - s)

            over(dve, step, TILES, 1, 4)


PROTOS, RANK = 32, 16
LOW = PROTOS * RANK


def experts_phase(nc, dram, out_dram, keep):
    with ExitStack() as ctx:
        def sb(name, shape, dt=F32):
            return ctx.enter_context(nc.sbuf_tensor(f"experts_{name}", shape, dt))

        def bank(name, shape):
            return ctx.enter_context(nc.psum_tensor(f"experts_{name}", shape, F32))

        def sem(name):
            return ctx.enter_context(nc.semaphore(f"experts_{name}"))

        h_all, identity, consts = keep["h"], keep["identity"], keep["consts"]
        protos = sb("protos", [P, KC, PROTOS])
        proto_sq = sb("proto_sq", [P, KC, PROTOS])
        norms = sb("norms", [P, PROTOS])
        ones = sb("ones", [P, P])
        b_maps = sb("b_maps", [P, KC, LOW])
        a_maps = sb("a_maps", [P, LOW // P, D])
        bias = sb("bias", [P, D])
        number = sb("number", [P, PROTOS])
        temp = sb("temp", [P, 4])
        stats = sb("stats", [P, 2, 6])
        spare = sb("spare", [P, 1])
        minus = sb("minus", [P, 2])
        mean_var = sb("mean_var", [P, 2, 2])
        small = sb("small", [P, 2, 1])
        rstd = sb("rstd", [P, 2, 1])
        xn = sb("xn", [P, 2, D])
        squares = sb("squares", [P, D])
        x_norm = sb("x_norm", [P, 2, 1])
        xT = sb("xT", [P, 2, KC, TILE])
        sums = sb("sums", [P, PROTOS])
        near = sb("near", [P, 2, PROTOS])
        best = sb("best", [P, 2, 8])
        best_at = sb("best_at", [P, 8], U32)
        at = sb("at", [P, 2, 2])
        dist = sb("dist", [P, 2, 4])
        share = sb("share", [P, 2, 4])
        picked = sb("picked", [P, 2, PROTOS])
        shares = sb("shares", [P, 2, P])
        low = sb("low", [P, 2, LOW])
        lowT = sb("lowT", [P, 2, LOW])
        sharesT = sb("sharesT", [P, 2, P])
        result = sb("result", [P, 2, D])

        xb = bank("xb", [P, 512])
        dots = bank("dots", [P, 512])
        first = bank("first", [P, 2, 512])
        lt = bank("lt", [P, 512])
        st = bank("st", [P, 512])
        yb = bank("yb", [P, 2, 512])

        loads, consts_ready, front_steps, front_pool = sem("loads"), sem("consts_ready"), sem("front"), sem("front_pool")
        xn_ready, xt_done, xt_ready, x_norm_ready = sem("xn_ready"), sem("xt_done"), sem("xt_ready"), sem("x_norm")
        dots_done, first_done, pick, roots, exp_done = sem("dots_done"), sem("first_done"), sem("pick"), sem("roots"), sem("exp_done")
        share_steps, lt_done, lt_ready, y_done, stored = sem("share"), sem("lt_done"), sem("lt_ready"), sem("y_done"), [sem("stored0"), sem("stored1")]
        result_ready = sem("result_ready")
        PICK = 6
        SHARE = 8
        DEPTH, PEEL = 4, 6

        loaded = [(protos, dram["protos"]), (b_maps, dram["b_maps"]), (a_maps, dram["a_maps"]), (number, dram["number"])]
        LOADS = 16 * (len(loaded) + 2)
        block = ctx.enter_context(nc.Block())

        @block.sync
        def _(sp):
            for to, frm in loaded:
                sp.dma_start(to[:], frm).then_inc(loads, 16)
            sp.dma_start(temp[:, 0:1], dram["temp"]).then_inc(loads, 16)
            sp.wait_ge(consts_ready, 1)
            sp.dma_start(bias[0:PROTOS], dram["bias"]).then_inc(loads, 16)

            def step(n, i, s, has):
                wait_for(sp, result_ready, n + 1)
                sp.dma_start(out_dram[n], result[:, s]).then_inc(stored[s], 16)

            over(sp, step, TILES, 0, 2)
            for s in range(2):
                sp.wait_ge(stored[s], 16 * TILES // 2)

        @block.tensor
        def _(pe):
            pe.wait_ge(consts_ready, 6)
            for c in range(KC):
                mm = pe.matmul(dots[:, 0:PROTOS], ones[:, :], proto_sq[:, c], start=c == 0, stop=c == KC - 1)
            mm.then_inc(dots_done, 1)
            pe.wait_ge(consts_ready, 9)

            def turn_x(n, s):
                wait_for(pe, xn_ready, n + 1)
                wait_for(pe, xt_ready, n)
                for c in range(KC):
                    mm = pe.transpose(xb[:, c * P:(c + 1) * P], xn[:, s, c * P:(c + 1) * P], identity[:, :])
                mm.then_inc(xt_done, 1)

            def products(n, s):
                wait_for(pe, xt_ready, n + 1)
                wait_for(pe, pick, after(n, PICK * (n - 1) + 2))
                for c in range(KC):
                    mm = pe.matmul(dots[:, 0:PROTOS], xT[:, s, c], protos[:, c], start=c == 0, stop=c == KC - 1)
                mm.then_inc(dots_done, 1)
                wait_for(pe, share_steps, after(n - 1, SHARE * (n - 2) + SHARE))
                for c in range(KC):
                    mm = pe.matmul(first[:, s], xT[:, s, c], b_maps[:, c], start=c == 0, stop=c == KC - 1)
                mm.then_inc(first_done, 1)

            def turn_low(n, s):
                wait_for(pe, share_steps, SHARE * (n + 1))
                wait_for(pe, lt_ready, 2 * n)
                for c in range(LOW // P):
                    mm = pe.transpose(lt[:, c * P:(c + 1) * P], low[:, s, c * P:(c + 1) * P], identity[:, :])
                mm.then_inc(lt_done, 1)
                pe.transpose(st[:, 0:P], shares[:, s], identity[:, :]).then_inc(lt_done, 1)

            def second(n, s):
                wait_for(pe, lt_ready, 2 * (n + 1))
                wait_for(pe, result_ready, n - 1)
                for c in range(LOW // P):
                    pe.matmul(yb[:, s, 0:D], lowT[:, s, c * P:(c + 1) * P], a_maps[:, c], start=c == 0, stop=False)
                pe.matmul(yb[:, s, 0:D], sharesT[:, s], bias[:, :], start=False, stop=True).then_inc(y_done, 1)

            def step(t, i, s, has):
                if has(1):
                    turn_x(t - 1, 1 - s)
                if has(3):
                    turn_low(t - 3, 1 - s)
                if has(1):
                    products(t - 1, 1 - s)
                if has(3):
                    second(t - 3, 1 - s)

            over(pe, step, TILES, DEPTH, PEEL)

        @block.scalar
        def _(act):
            act.wait_ge(consts_ready, 9)

            def keep_x(n, s):
                wait_for(act, xn_ready, n + 1)
                wait_for(act, pick, after(n - 1, PICK * (n - 2) + 1))
                nc.scalar.activation(squares[:], xn[:, s], ACT.Square, accum_out=x_norm[:, s]).then_inc(x_norm_ready, 1)
                wait_for(act, xt_done, n + 1)
                wait_for(act, first_done, n - 1)
                nc.scalar.copy(xT[:, s].rearrange("p c t -> p (c t)"), xb[:, 0:D]).then_inc(xt_ready, 1)

            def keep_low(n, s):
                wait_for(act, lt_done, 2 * n + 1)
                wait_for(act, y_done, n - 1)
                nc.scalar.copy(lowT[:, s], lt[:, :]).then_inc(lt_ready, 1)
                wait_for(act, lt_done, 2 * n + 2)
                nc.scalar.copy(sharesT[:, s], st[:, 0:P]).then_inc(lt_ready, 1)

            def exponent(n, s):
                wait_for(act, share_steps, SHARE * n + 1)
                nc.scalar.activation(share[:, s, 1:2], share[:, s, 0:1], ACT.Exp, scale=temp[:, 3:4]).then_inc(exp_done, 1)

            def step(t, i, s, has):
                if has(1):
                    keep_x(t - 1, 1 - s)
                if has(3):
                    keep_low(t - 3, 1 - s)
                if has(2):
                    exponent(t - 2, s)

            over(act, step, TILES, DEPTH, PEEL)

        @block.gpsimd
        def _(pool):
            def front(n, s):
                wait_for(pool, front_steps, 2 * (n + 1))
                nc.gpsimd.tensor_tensor(small[:, s], mean_var[:, s, 1:2], consts[:, 3:4], ALU.add).then_inc(front_pool, 1)
                wait_for(pool, front_pool, 2 * n + 1)
                nc.gpsimd.tensor_tensor(rstd[:, s], small[:, s], consts[:, 0:1], ALU.pow).then_inc(front_pool, 1)

            def distances(n, s):
                wait_for(pool, pick, PICK * (n + 1))
                nc.gpsimd.tensor_tensor(dist[:, s, 0:2], best[:, s, 0:2], minus[:], ALU.mult).then_inc(roots, 1)
                wait_for(pool, roots, 2 * n + 1)
                nc.gpsimd.tensor_tensor(dist[:, s, 2:4], dist[:, s, 0:2], consts[:, 1:3], ALU.pow).then_inc(roots, 1)

            pool.wait_ge(consts_ready, 9)

            def step(t, i, s, has):
                if has(0):
                    front(t, s)
                if has(1):
                    distances(t - 1, 1 - s)

            over(pool, step, TILES, DEPTH, PEEL)

        @block.vector
        def _(dve):
            nc.vector.memset(minus[:], -1.0)
            nc.vector.memset(bias[:], 0.0).then_inc(consts_ready, 1)
            nc.vector.memset(shares[:], 0.0).then_inc(consts_ready, 1)
            nc.vector.memset(ones[:], 1.0).then_inc(consts_ready, 1)
            nc.vector.memset(consts[:, 1:3], 0.5).then_inc(consts_ready, 1)
            dve.wait_ge(loads, LOADS)
            nc.vector.tensor_tensor(proto_sq[:], protos[:], protos[:], ALU.mult).then_inc(consts_ready, 1)
            nc.vector.tensor_scalar(temp[:, 1:2], temp[:, 0:1], -1.0, None, ALU.mult).then_inc(consts_ready, 1)
            dve.wait_ge(consts_ready, 6)
            nc.vector.scalar_tensor_tensor(temp[:, 2:3], temp[:, 0:1], 0.1, temp[:, 1:2], ALU.max, ALU.max).then_inc(consts_ready, 1)
            dve.wait_ge(consts_ready, 7)
            nc.vector.reciprocal(temp[:, 3:4], temp[:, 2:3]).then_inc(consts_ready, 1)
            dve.wait_ge(dots_done, 1)
            nc.vector.tensor_copy(norms[:], dots[:, 0:PROTOS]).then_inc(consts_ready, 1)
            dve.wait_ge(consts_ready, 9)

            def front(n, s):
                carrier(nc, spare[:])
                nc.vector.bn_stats(stats[:, s], h_all[:, n]).then_inc(front_steps, 1)
                wait_for(dve, front_steps, 2 * n + 1)
                carrier(nc, spare[:])
                nc.vector.bn_aggr(mean_var[:, s], stats[:, s]).then_inc(front_steps, 1)

            def normalise(n, s):
                wait_for(dve, front_pool, 2 * (n + 1))
                wait_for(dve, xt_done, n - 1)
                wait_for(dve, x_norm_ready, n - 1)
                nc.vector.tensor_scalar(xn[:, s], h_all[:, n], mean_var[:, s, 0:1], rstd[:, s], ALU.subtract,
                                        ALU.mult).then_inc(xn_ready, 1)

            def choose(n, s):
                at0 = PICK * n
                wait_for(dve, x_norm_ready, n + 1)
                wait_for(dve, roots, 2 * (n - 1))
                nc.vector.tensor_scalar(sums[:], norms[:], x_norm[:, s], None, ALU.add).then_inc(pick, 1)
                wait_for(dve, dots_done, n + 2)
                wait_for(dve, pick, at0 + 1)
                nc.vector.scalar_tensor_tensor(near[:, s], dots[:, 0:PROTOS], 2.0, sums[:], ALU.mult, ALU.subtract).then_inc(pick, 1)
                wait_for(dve, pick, at0 + 2)
                nc.vector.tensor_scalar(near[:, s], near[:, s], 0.0, None, ALU.min).then_inc(pick, 1)
                wait_for(dve, pick, at0 + 3)
                carrier(nc, spare[:])
                nc.vector.max(best[:, s], near[:, s]).then_inc(pick, 1)
                wait_for(dve, pick, at0 + 4)
                carrier(nc, spare[:])
                nc.vector.max_index(best_at[:], best[:, s], near[:, s]).then_inc(pick, 1)
                wait_for(dve, pick, at0 + 5)
                nc.vector.tensor_copy(at[:, s], best_at[:, 0:2]).then_inc(pick, 1)

            def weigh(n, s):
                at0 = SHARE * n
                wait_for(dve, roots, 2 * (n + 1))
                nc.vector.tensor_tensor(share[:, s, 0:1], dist[:, s, 2:3], dist[:, s, 3:4], ALU.subtract).then_inc(share_steps, 1)
                wait_for(dve, exp_done, n + 1)
                nc.vector.tensor_scalar(share[:, s, 2:3], share[:, s, 1:2], 1.0, None, ALU.add).then_inc(share_steps, 1)
                wait_for(dve, share_steps, at0 + 2)
                nc.vector.reciprocal(share[:, s, 0:1], share[:, s, 2:3]).then_inc(share_steps, 1)
                wait_for(dve, share_steps, at0 + 3)
                nc.vector.tensor_scalar(share[:, s, 3:4], share[:, s, 1:2], share[:, s, 0:1], None, ALU.mult).then_inc(share_steps, 1)
                nc.vector.tensor_scalar(picked[:, s], number[:], at[:, s, 0:1], share[:, s, 0:1], ALU.is_equal, ALU.mult).then_inc(share_steps, 1)
                wait_for(dve, share_steps, at0 + 5)
                wait_for(dve, lt_done, 2 * (n - 1))
                nc.vector.tensor_scalar(shares[:, s, 0:PROTOS], number[:], at[:, s, 1:2], share[:, s, 3:4], ALU.is_equal, ALU.mult).then_inc(share_steps, 1)
                wait_for(dve, share_steps, at0 + 6)
                nc.vector.tensor_tensor(shares[:, s, 0:PROTOS], shares[:, s, 0:PROTOS], picked[:, s], ALU.add).then_inc(share_steps, 1)
                wait_for(dve, share_steps, at0 + 7)
                wait_for(dve, first_done, n + 1)
                nc.vector.tensor_tensor(low[:, s].rearrange("p (e r) -> p e r", r=RANK), first[:, s].rearrange("p (e r) -> p e r", r=RANK),
                                        shares[:, s, 0:PROTOS, None].broadcast_to([P, PROTOS, RANK]), ALU.mult).then_inc(share_steps, 1)

            def finish(n, s, pair):
                wait_for(dve, y_done, n + 1)
                wait_for(dve, stored[s], 16 * pair)
                nc.vector.tensor_tensor(result[:, s], h_all[:, n], yb[:, s, 0:D], ALU.add).then_inc(result_ready, 1)

            def step(t, i, s, has):
                if has(1):
                    normalise(t - 1, 1 - s)
                if has(2):
                    weigh(t - 2, s)
                if has(0):
                    front(t, s)
                if has(1):
                    choose(t - 1, 1 - s)
                if has(3):
                    finish(t - 3, 1 - s, i - 2 + s)

            over(dve, step, TILES, DEPTH, PEEL)


def vit_tower(nc, dram, out_dram):
    with ExitStack() as ctx:
        def sb(name, shape, dt=F32):
            return ctx.enter_context(nc.sbuf_tensor(name, shape, dt))

        keep = {
            "h": sb("h_all", [P, TILES, D]), "x": sb("x_all", [P, TILES, D]), "identity": sb("identity", [P, P]),
            "consts": sb("consts", [P, 4]), "x_peaks": sb("x_peaks", [P, TILES]),
            "ffn_gate": sb("ffn_gate", [P, KC, FFN]), "ffn_up": sb("ffn_up", [P, KC, FFN]), "ffn_down": sb("ffn_down", [P, FC, D]),
            "gate_peaks": sb("gate_peaks", [P, FC, NG]), "up_peaks": sb("up_peaks", [P, FC, NG]),
            "silu_peaks": sb("silu_peaks", [P, FC, NG]), "out_peaks": sb("out_peaks", [P, FC, 4]),
            "scales": sb("scales", [P, 10]), "up_dram": nc.dram_tensor("up_rows_dram", (P, FC, IMAGES * SEQ), F32).ap(),
        }

        def of(mode):
            own = {k: dram[f"{mode}_{k}"] for k in ("w_qkv", "w_out", "cos", "sin", "w_norm") if f"{mode}_{k}" in dram}
            return {**dram, **own}

        weights_phase(nc, dram, keep)
        attention_phase(nc, "patch", of("patch"), keep)
        with nc.sbuf_tensor("gate", [P, FC, IMAGES * SEQ], F32) as gate:
            keep["gate"] = gate
            gate_phase(nc, keep)
            up_phase(nc, keep)
            mix_phase(nc, keep)
            down_phase(nc, keep)
        attention_phase(nc, "global", of("global"), keep)
        attention_phase(nc, "local", of("local"), keep)
        experts_phase(nc, dram, out_dram, keep)


def head_columns(w):
    return w.reshape(-1, GROUPS, HEADS // GROUPS, HD // 2, 2).transpose(0, 2, 1, 4, 3).reshape(-1, D)


def k_columns(w):
    return w.reshape(-1, GROUPS, HD // 2, 2).transpose(0, 1, 3, 2).reshape(-1, GROUPS * HD)


def v_columns(w):
    return w.reshape(-1, 2, 2, HD).transpose(0, 2, 1, 3).reshape(-1, GROUPS * HD)


def out_rows(w):
    return w.reshape(GROUPS, 2, 2, HD, -1).transpose(2, 0, 3, 1, 4).reshape(P, 2, -1)


def in_chunks(w):
    return w.reshape(-1, P, w.shape[1]).transpose(1, 0, 2)


def rope_tables(q_freq, k_freq):
    pos = np.arange(SEQ, dtype=np.float32)[:, None]
    q = head_columns(np.repeat(pos * q_freq[None, :], 2, axis=1))
    k = k_columns(np.repeat(pos * np.tile(k_freq, GROUPS)[None, :], 2, axis=1))
    angle = np.tile(np.concatenate([q, k], axis=1), (2, 1)).astype(np.float32)
    sign = np.tile(np.repeat(np.array([1, -1], np.float32), HD // 2), ROPED)
    return np.cos(angle), np.sin(angle) * sign


def frequencies(base, width):
    return (np.float32(1) / np.float32(base) ** (np.arange(0, width, 2, dtype=np.float32) / np.float32(width))).astype(np.float32)


def layouts(a):
    out = {}
    x = a["x"].reshape(TILES, 2, 3, 8, 16, 8, 16).transpose(2, 4, 6, 0, 1, 3, 5).reshape(PC, P, TILES, TILE)
    out["patches"] = x.transpose(2, 1, 0, 3)
    out["w_patch"] = in_chunks(a["L0_tok_W"].T)
    out["b_patch"] = np.broadcast_to(a["L0_tok_b"], (P, D))
    out["identity"] = np.eye(P, dtype=np.float32)
    par_of = (np.arange(P) // HD) % 2
    out["k_mask"] = (par_of[:, None] == np.arange(2)[None, :]).astype(np.float32)
    out["causal"] = ((np.arange(P) % SEQ)[:, None] <= np.arange(SEQ)[None, :]).astype(np.float32)
    f0 = frequencies(10000.0, D)
    out["patch_cos"], out["patch_sin"] = rope_tables(f0, f0[:HD // 2])
    for mode, base in (("global", 1000000.0), ("local", 10000.0)):
        f = frequencies(base, HD)
        out[mode + "_cos"], out[mode + "_sin"] = rope_tables(np.tile(f, HEADS), f)
    out["patch_w_qkv"] = in_chunks(np.concatenate([head_columns(a["L0_attn_Wq"]), k_columns(a["L0_attn_Wk"]), v_columns(a["L0_attn_Wv"])], axis=1))
    out["patch_w_out"] = out_rows(a["L0_attn_Wo"])
    out["global_w_qkv"] = in_chunks(head_columns(a["L1_attn_g_wq"]))
    out["w_down"] = in_chunks(a["L1_attn_g_kv_down"])
    out["w_kv_up"] = np.concatenate([k_columns(a["L1_attn_g_k_up"]), v_columns(a["L1_attn_g_v_up"])], axis=1)
    out["global_w_out"] = out_rows(a["L1_attn_g_wo"])
    out["local_w_qkv"] = in_chunks(np.concatenate([head_columns(a["L1_attn_l_wq"]), k_columns(a["L1_attn_l_wk"]), v_columns(a["L1_attn_l_wv"])], axis=1))
    out["local_w_out"] = out_rows(a["L1_attn_l_wo"])
    out["global_w_norm"] = np.broadcast_to(a["L1_attn_norm1_w"], (P, D))
    out["local_w_norm"] = np.broadcast_to(a["L1_attn_norm2_w"], (P, D))
    out["ffn_gate"] = in_chunks(a["L0_ffn_w_gate"]).reshape(P, -1)
    out["ffn_up"] = in_chunks(a["L0_ffn_w_up"]).reshape(P, -1)
    out["ffn_down"] = in_chunks(a["L0_ffn_w_down"]).reshape(P, -1)
    out["protos"] = in_chunks(a["L1_ffn_prototypes"].T)
    out["b_maps"] = in_chunks(a["L1_ffn_B"].reshape(LOW, D).T)
    out["a_maps"] = in_chunks(a["L1_ffn_A"].transpose(0, 2, 1).reshape(LOW, D))
    out["bias"] = a["L1_ffn_bias"]
    out["number"] = np.broadcast_to(np.arange(PROTOS, dtype=np.float32), (P, PROTOS))
    out["temp"] = np.broadcast_to(np.reshape(a["L1_ffn_temp"], (1, 1)), (P, 1))
    return {k: np.ascontiguousarray(v, dtype=np.float32) for k, v in out.items()}


def kernel(**inputs):
    import concourse.bacc as bacc
    from concourse.bass_utils import run_bass_kernel_spmd

    nc = bacc.Bacc("TRN2", target_bir_lowering=False, num_devices=1)
    arrays, dram = {}, {}
    for name, a in layouts({k: np.asarray(v) for k, v in inputs.items()}).items():
        arrays[f"in_{name}"] = a
        dram[name] = nc.dram_tensor(f"in_{name}", a.shape, mybir.dt.from_np(a.dtype), kind="ExternalInput").ap()
    out = nc.dram_tensor("out", (TILES, P, D), F32, kind="ExternalOutput").ap()
    vit_tower(nc, dram, out)
    ran = run_bass_kernel_spmd(nc, [arrays], core_ids=[0])
    return ran.results[0]["out"].reshape(IMAGES, SEQ, D)
```

```python
from contextlib import ExitStack

import numpy as np
import concourse.bass as bass
from concourse import mybir

F32 = mybir.dt.float32
I16 = mybir.dt.int16
U16 = mybir.dt.uint16
U32 = mybir.dt.uint32
ALU = mybir.AluOpType
ACT = mybir.ActivationFunctionType
AX = mybir.AxisListType
MAX_ALL = bass.bass_isa.ReduceOp.max

P = 128
D = 256
KC = D // P
IMAGES, SEQ = 64, 64
TILE = 2 * SEQ
TILES = IMAGES * SEQ // TILE
PATCH = 3 * 16 * 16
PC = PATCH // P
HEADS, GROUPS, HD = 16, 4, 16
QK = D + GROUPS * HD
QKV = QK + GROUPS * HD
LATENT = 64
ROPED = HEADS + GROUPS
LN_EPS, RMS_EPS = 1e-5, 1e-6


def wait_for(eng, sem, count):
    if isinstance(count, int) and count <= 0:
        return
    eng.wait_ge(sem, count)


def carrier(nc, spare):
    nc.vector.memset(spare, 0.0)


def over(eng, step, count, depth, peel):
    for t in range(peel):
        step(t, t // 2, t % 2, lambda lag: lag <= t)
    with eng.Fori(peel // 2, count // 2) as i:
        for s in range(2):
            step(2 * i + s, i, s, lambda lag: True)
    for t in range(count, count + depth):
        step(t, t // 2, t % 2, lambda lag: t - lag < count)


def after(n, count):
    return 0 if isinstance(n, int) and n <= 0 else count


def upto_last(n, per=1):
    return per * min(n, TILES) if isinstance(n, int) else per * n


def attention_phase(nc, mode, dram, keep):
    patch, latent, normed = mode == "patch", mode == "global", mode != "patch"
    scale = 1.0 / 16 if patch else 1.0 / 4
    h_all, x_all, identity, consts = keep["h"], keep["x"], keep["identity"], keep["consts"]
    half_neg = consts[:, 0:1]
    with ExitStack() as ctx:
        def sb(name, shape, dt=F32):
            return ctx.enter_context(nc.sbuf_tensor(f"{mode}_{name}", shape, dt))

        def bank(name, shape):
            return ctx.enter_context(nc.psum_tensor(f"{mode}_{name}", shape, F32))

        def sem(name):
            return ctx.enter_context(nc.semaphore(f"{mode}_{name}"))

        qkv_cols = D if latent else QKV
        w_qkv = sb("w_qkv", [P, KC, qkv_cols])
        w_out = sb("w_out", [P, KC, D])
        cos_t = sb("cos", [P, QK])
        sin_t = sb("sin", [P, QK])
        k_mask = sb("k_mask", [P, 2])
        if patch:
            w_patch = sb("w_patch", [P, PC, D])
            b_patch = sb("b_patch", [P, D])
            patches = sb("patches", [P, 2, PC, TILE])
        else:
            causal = sb("causal", [P, SEQ])
            w_norm = sb("w_norm", [P, KC])
        if latent:
            w_down = sb("w_down", [P, KC, LATENT])
            w_kv_up = sb("w_kv_up", [LATENT, 2 * GROUPS * HD])
            lat = sb("lat", [LATENT, 2, TILE])
        stats = sb("stats", [P, 2, 6])
        spare = sb("spare", [P, 1])
        mean_var = sb("mean_var", [P, 2, 2])
        small = sb("small", [P, 2, 4])
        rstd = sb("rstd", [P, 2, 2])
        xn = sb("xn", [P, 2, D])
        xT = sb("xT", [P, 2, KC, TILE])
        by_cos = sb("by_cos", [P, ROPED, 2, HD // 2])
        by_sin = sb("by_sin", [P, ROPED, 2, HD // 2])
        qk = sb("qk", [P, 2, ROPED, 2, HD // 2])
        qT = sb("qT", [P, 2, 2, 2, SEQ])
        k_diag = sb("k_diag", [P, 2, 2, 2, SEQ])
        v_rows = sb("v_rows", [P, 2, GROUPS * HD])
        v_diag = sb("v_diag", [P, 2, 2, 2, 2, HD + 1])
        probs = sb("probs", [P, 2, 4, 2 * P])
        rden = sb("rden", [P, 16])
        attn = sb("attn", [P, 2, 2, P])
        aT = sb("aT", [P, 2, 2, 2, SEQ])
        if patch:
            probsT = sb("probsT", [P, 2, 4, 2 * P])
            top = sb("top", [P, 2, 2, 8])
            stats2 = sb("stats2", [P, 2, 6])
            mean_var2 = sb("mean_var2", [P, 2, 2])
            rstd2 = sb("rstd2", [P, 2, 1])
            small2 = sb("small2", [P, 2, 1])
        else:
            squares = sb("squares", [P, ROPED, HD])
            sumsq = sb("sumsq", [P, 2, ROPED])
            qk_rms = sb("qk_rms", [P, 2, ROPED])
            half_negs = sb("half_negs", [P, ROPED])
            rms_eps = sb("rms_eps", [P, ROPED])
            pair_factor, pair_eps = sb("pair_factor", [P, 2]), sb("pair_eps", [P, 2])
            half_neg2 = sb("half_neg2", [P, 2])
            rms_eps_act = sb("rms_eps_act", [P, 1])
            three_halves = sb("three_halves", [P, ROPED])
            logs = sb("logs", [P, 2, ROPED])
            guess = sb("guess", [P, 2, ROPED])
            newton = sb("newton", [P, ROPED])
            qkn = sb("qkn", [P, 2, ROPED, HD])

        sc = bank("sc", [P, 4, 512])
        hy = bank("hy", [P, 512])
        xq = bank("xq", [P, 512])
        pj = bank("pj", [P, 512])
        ao = bank("ao", [P, 512])

        loads = sem("loads")
        consts_ready = sem("consts_ready")
        if patch:
            patches_loaded = [sem("patches_loaded0"), sem("patches_loaded1")]
            patch_done = sem("patch_done")
            pt_done, pt_ready = sem("pt_done"), sem("pt_ready")
            soft_steps = sem("soft_steps")
            final_steps, final_rstd = sem("final_steps"), sem("final_rstd")
        else:
            squares_ready, rms_steps, scaled, masked = sem("squares"), sem("rms"), sem("scaled"), sem("masked")
            sumsq_ready, guess_steps = sem("sumsq"), sem("guess")
        if latent:
            lat_done, lat_ready = sem("lat_done"), sem("lat_ready")
        front_steps, front_pool, xn_ready = sem("front_steps"), sem("front_pool"), sem("xn_ready")
        xt_done, xt_ready = sem("xt_done"), sem("xt_ready")
        qkv_done, rope_steps = sem("qkv_done"), sem("rope_steps")
        qkt_done, qt_ready, kd_ready = sem("qkt_done"), sem("qt_ready"), sem("kd_ready")
        v_ready = sem("v_ready")
        scores_done, exp_done = sem("scores_done"), sem("exp_done")
        pv_done, norm_steps = sem("pv_done"), sem("norm_steps")
        at_done, at_ready, y_done, out_steps = sem("at_done"), sem("at_ready"), sem("y_done"), sem("out_steps")

        FRONT = 3 if patch else 2
        POOLF = {"patch": 2, "global": 3, "local": 4}[mode]
        XN = 2 if latent else 1
        ROPE = 5
        SPREAD_V = 4
        OUT = 3 if patch else (1 if latent else 2)
        DEPTH, PEEL = (5 if patch else 6), 8

        loaded = [(w_qkv, dram["w_qkv"]), (w_out, dram["w_out"]), (cos_t, dram["cos"]),
                  (sin_t, dram["sin"]), (k_mask, dram["k_mask"])]
        if patch:
            loaded += [(w_patch, dram["w_patch"]), (b_patch, dram["b_patch"])]
        else:
            loaded += [(causal, dram["causal"]), (w_norm, dram["w_norm"])]
        if latent:
            loaded += [(w_down, dram["w_down"]), (w_kv_up, dram["w_kv_up"])]
        LOADS = 16 * len(loaded)
        CONSTS = 5 if patch else (9 if latent else 7)

        block = ctx.enter_context(nc.Block())

        @block.sync
        def _(sp):
            if patch:
                for s in range(2):
                    sp.dma_start(patches[:, s], dram["patches"][s]).then_inc(patches_loaded[s], 16)
            for to, frm in loaded:
                sp.dma_start(to[:], frm).then_inc(loads, 16)
            if patch:
                with sp.Fori(1, TILES // 2) as i:
                    for s in range(2):
                        sp.wait_ge(patch_done, 2 * i + s - 1)
                        sp.dma_start(patches[:, s], dram["patches"][2 * i + s]).then_inc(patches_loaded[s], 16)
            sp.wait_ge(loads, LOADS)

        @block.tensor
        def _(pe):
            pe.wait_ge(loads, LOADS)
            pe.wait_ge(consts_ready, CONSTS)

            def transpose_x(n, s):
                wait_for(pe, xn_ready, XN * (n + 1))
                wait_for(pe, qt_ready, n - 1)
                wait_for(pe, kd_ready, n - 1)
                for c in range(KC):
                    mm = pe.transpose(xq[:, c * P:(c + 1) * P], xn[:, s, c * P:(c + 1) * P], identity[:, :])
                mm.then_inc(xt_done, 1)

            def transpose_qk(n, s):
                if patch:
                    wait_for(pe, rope_steps, ROPE * n + 4)
                    rows = qk[:, s].rearrange("p h e i -> p (h e i)")
                else:
                    wait_for(pe, scaled, n + 1)
                    rows = qkn[:, s].rearrange("p h d -> p (h d)")
                wait_for(pe, xt_ready, upto_last(n + 2))
                for a in range(2):
                    pe.transpose(xq[:, a * P:(a + 1) * P], rows[:, a * P:(a + 1) * P], identity[:, :])
                pe.transpose(xq[0:GROUPS * HD, 2 * P:3 * P], rows[:, D:QK], identity[:, :]).then_inc(qkt_done, 1)

            def embed(n, s, i, chunks):
                if chunks[0] == 0:
                    pe.wait_ge(patches_loaded[s], 16 * i + 16)
                    wait_for(pe, front_steps, after(n, FRONT * (n - 1) + 1))
                    wait_for(pe, out_steps, after(n - 4, OUT * (n - 5) + 1))
                for c in chunks:
                    mm = pe.matmul(hy[:, 0:D], patches[:, s, c], w_patch[:, c], start=c == 0, stop=c == PC - 1)
                if c == PC - 1:
                    mm.then_inc(patch_done, 1)

            def down(n, s):
                wait_for(pe, xt_ready, n + 1)
                wait_for(pe, out_steps, after(n - 4, OUT * (n - 5) + 1))
                for c in range(KC):
                    mm = pe.matmul(hy[0:LATENT, D:D + TILE], w_down[:, c], xT[:, s, c], start=c == 0, stop=c == KC - 1)
                mm.then_inc(lat_done, 1)

            def project(n, s, chunks):
                if chunks[0] == 0:
                    wait_for(pe, xt_ready, n + 1)
                    wait_for(pe, rope_steps, ROPE * n)
                for c in chunks:
                    mm = pe.matmul(pj[:, 0:qkv_cols], xT[:, s, c], w_qkv[:, c], start=c == 0, stop=c == KC - 1)
                if c < KC - 1:
                    return
                if latent:
                    wait_for(pe, lat_ready, n + 1)
                    mm = pe.matmul(pj[:, D:QKV], lat[:, s], w_kv_up[:, :], start=True, stop=True)
                mm.then_inc(qkv_done, 1)

            def score(n, s, t):
                rl = t // 2
                if t == 0:
                    wait_for(pe, qt_ready, n + 1)
                    wait_for(pe, kd_ready, n + 1)
                if t % 2 == 0:
                    wait_for(pe, pt_ready if patch else exp_done, after(n, 2 * (n - 1) + rl + 1))
                rows = slice(32 * t, 32 * t + 32)
                for img in range(2):
                    q_side = qT[rows, s, img].rearrange("p a q -> p (a q)")
                    k_side = k_diag[rows, s, img].rearrange("p g k -> p (g k)")
                    out = sc[:, t, img * P:(img + 1) * P]
                    if patch:
                        mm = pe.matmul(out, q_side, k_side, start=True, stop=True)
                    else:
                        mm = pe.matmul(out, k_side, q_side, start=True, stop=True)
                if t % 2 == 1:
                    mm.then_inc(scores_done, 1)

            def transpose_probs(n, s):
                for rl in range(2):
                    wait_for(pe, exp_done, 2 * n + rl + 1)
                    for t in range(2 * rl, 2 * rl + 2):
                        for img in range(2):
                            cols = slice(img * P, (img + 1) * P)
                            mm = pe.transpose(sc[:, t, cols], probs[:, s, t, cols], identity[:, :])
                    mm.then_inc(pt_done, 1)

            def mix(n, s, pairs):
                if pairs[0] == 0:
                    wait_for(pe, pt_ready if patch else masked, 2 * (n + 1))
                    wait_for(pe, v_ready, SPREAD_V * (n + 1))
                    wait_for(pe, at_ready, n)
                src = probsT if patch else probs
                for pair in pairs:
                    img, t = pair // 4, pair % 4
                    at = pair * 2 * (HD + 1)
                    mm = pe.matmul(ao[:, at:at + 2 * (HD + 1)], src[:, s, t, img * P:(img + 1) * P],
                                   v_diag[:, s, img, t % 2].rearrange("p g d -> p (g d)"), start=True, stop=True)
                if pair == 7:
                    mm.then_inc(pv_done, 1)

            def transpose_attn(n, s):
                wait_for(pe, norm_steps, 2 * (n + 1))
                for img in range(2):
                    mm = pe.transpose(ao[:, img * P:(img + 1) * P], attn[:, s, img], identity[:, :])
                mm.then_inc(at_done, 1)

            def output(n, s, chunks):
                if chunks[0] == 0:
                    wait_for(pe, at_ready, n + 1)
                    if patch:
                        wait_for(pe, front_steps, upto_last(n + 5, FRONT) - (FRONT - 1))
                    if latent:
                        wait_for(pe, lat_ready, upto_last(n + 5))
                    wait_for(pe, out_steps, after(n, OUT * (n - 1) + 1))
                for a in chunks:
                    mm = pe.matmul(hy[:, 0:D], aT[:, s, a].rearrange("p g q -> p (g q)"), w_out[:, a], start=a == 0, stop=a == 1)
                if a == 1:
                    mm.then_inc(y_done, 1)

            def patch_step(t, i, s, has):
                if has(5):
                    output(t - 5, 1 - s, [0, 1])
                if has(3):
                    transpose_probs(t - 3, 1 - s)
                if has(1):
                    transpose_x(t - 1, 1 - s)
                if has(4):
                    transpose_attn(t - 4, s)
                if has(2):
                    transpose_qk(t - 2, s)
                if has(1):
                    project(t - 1, 1 - s, [0, 1])
                for bank_no in range(4):
                    if has(0):
                        embed(t, s, i, [bank_no])
                    if has(2):
                        score(t - 2, s, bank_no)
                if has(0):
                    embed(t, s, i, [4, 5])
                if has(3):
                    mix(t - 3, 1 - s, range(8))

            def normed_step(t, i, s, has):
                if has(1):
                    transpose_x(t - 1, 1 - s)
                if has(3):
                    score(t - 3, 1 - s, 0)
                if has(5):
                    transpose_attn(t - 5, 1 - s)
                if has(3):
                    score(t - 3, 1 - s, 1)
                if latent and has(1):
                    down(t - 1, 1 - s)
                if has(1):
                    project(t - 1, 1 - s, [0])
                    project(t - 1, 1 - s, [1])
                if has(5):
                    output(t - 5, 1 - s, [0])
                    output(t - 5, 1 - s, [1])
                if has(2):
                    transpose_qk(t - 2, s)
                if has(4):
                    mix(t - 4, s, range(8))
                if has(3):
                    score(t - 3, 1 - s, 2)
                    score(t - 3, 1 - s, 3)

            over(pe, patch_step if patch else normed_step, TILES, DEPTH, PEEL)

        @block.scalar
        def _(act):
            if normed:
                nc.scalar.preload_act_table_set("natural_log_exp_and_others")
            act.wait_ge(consts_ready, CONSTS)

            def keep_xT(n, s):
                wait_for(act, xt_done, n + 1)
                wait_for(act, qkv_done, n - 1)
                nc.scalar.copy(xT[:, s].rearrange("p c t -> p (c t)"), xq[:, 0:KC * TILE]).then_inc(xt_ready, 1)

            def spread_v(n, s):
                wait_for(act, rope_steps, ROPE * (n + 1))
                wait_for(act, pv_done, n - 1)
                for img in range(2):
                    for par in range(2):
                        nc.scalar.copy(
                            v_diag[par * SEQ:(par + 1) * SEQ, s, img, :, par, 0:HD],
                            v_rows[img * SEQ:(img + 1) * SEQ, s, par * 32:par * 32 + 32].rearrange("p (j d) -> p j d", j=2),
                        ).then_inc(v_ready, 1)

            def keep_qT(n, s):
                wait_for(act, qkt_done, n + 1)
                wait_for(act, scores_done, 2 * (n - 1))
                nc.scalar.copy(qT[:, s].rearrange("p g a q -> p a g q"),
                               xq[:, 0:2 * TILE].rearrange("p (a g q) -> p a g q", a=2, g=2)).then_inc(qt_ready, 1)

            def keep_aT(n, s):
                wait_for(act, at_done, n + 1)
                wait_for(act, y_done, n - 1)
                nc.scalar.copy(aT[:, s].rearrange("p a g q -> p g a q"),
                               ao[:, 0:2 * P].rearrange("p (g a q) -> p g a q", g=2, a=2)).then_inc(at_ready, 1)

            def keep_probsT(n, s, half):
                for rl in half:
                    wait_for(act, pt_done, 2 * n + rl + 1)
                    wait_for(act, pv_done, n - 1)
                    nc.scalar.copy(probsT[:, s, 2 * rl:2 * rl + 2], sc[:, 2 * rl:2 * rl + 2, 0:2 * P]).then_inc(pt_ready, 1)

            def keep_latent(n, s):
                wait_for(act, lat_done, n + 1)
                wait_for(act, qkv_done, n - 1)
                nc.scalar.copy(lat[:, s], hy[0:LATENT, D:D + TILE]).then_inc(lat_ready, 1)

            def square(n, s):
                wait_for(act, rope_steps, ROPE * n + 4)
                nc.scalar.activation(squares[:].rearrange("p h d -> p (h d)"),
                                     qk[:, s].rearrange("p h e i -> p (h e i)"), ACT.Square, scale=HD ** -0.5).then_inc(squares_ready, 1)

            def guess_norms(n, s):
                wait_for(act, sumsq_ready, n + 1)
                wait_for(act, rms_steps, 6 * (n - 1))
                nc.scalar.activation(logs[:, s], sumsq[:, s], ACT.Ln, bias=rms_eps_act[:]).then_inc(guess_steps, 1)
                wait_for(act, guess_steps, 2 * n + 1)
                nc.scalar.activation(guess[:, s], logs[:, s], ACT.Exp, scale=-0.5).then_inc(guess_steps, 1)

            def exponent(n, s, half):
                for rl in half:
                    part = probs[:, s, 2 * rl:2 * rl + 2]
                    if patch:
                        wait_for(act, soft_steps, 4 * n + 2 * rl + 2)
                        nc.scalar.activation(part, part, ACT.Exp, scale=scale).then_inc(exp_done, 1)
                    else:
                        wait_for(act, scores_done, 2 * n + rl + 1)
                        wait_for(act, pv_done, n - 1)
                        nc.scalar.activation(part, sc[:, 2 * rl:2 * rl + 2, 0:2 * P], ACT.Exp,
                                             scale=scale).then_inc(exp_done, 1)

            def patch_step(t, i, s, has):
                if has(3):
                    keep_probsT(t - 3, 1 - s, [0])
                if has(1):
                    keep_xT(t - 1, 1 - s)
                if has(4):
                    keep_aT(t - 4, s)
                if has(3):
                    keep_probsT(t - 3, 1 - s, [1])
                if has(2):
                    keep_qT(t - 2, s)
                if has(2):
                    spread_v(t - 2, s)
                    exponent(t - 2, s, [0, 1])

            def normed_step(t, i, s, has):
                if has(1):
                    keep_xT(t - 1, 1 - s)
                if has(5):
                    keep_aT(t - 5, 1 - s)
                if has(4):
                    exponent(t - 4, s, [1])
                if latent and has(1):
                    keep_latent(t - 1, 1 - s)
                if has(3):
                    exponent(t - 3, 1 - s, [0])
                if has(2):
                    keep_qT(t - 2, s)
                if has(1):
                    square(t - 1, 1 - s)
                if has(2):
                    spread_v(t - 2, s)
                if has(1):
                    guess_norms(t - 1, 1 - s)

            over(act, patch_step if patch else normed_step, TILES, DEPTH, PEEL)

        @block.gpsimd
        def _(pool):
            if normed:
                nc.gpsimd.memset(rms_eps[:], RMS_EPS)
                nc.gpsimd.memset(three_halves[:], 1.5)
                nc.gpsimd.memset(half_neg2[:], -0.5)
                nc.gpsimd.memset(pair_factor[:, 0:1], 1.0)
                nc.gpsimd.memset(pair_factor[:, 1:2], 1.0 + RMS_EPS)
                nc.gpsimd.memset(pair_eps[:, 0:1], LN_EPS)
                nc.gpsimd.memset(pair_eps[:, 1:2], RMS_EPS * LN_EPS)
                nc.gpsimd.memset(half_negs[:], -0.5).then_inc(front_pool, 1)
                pool.wait_ge(front_pool, 1)
            base = 1 if normed else 0

            def front(n, s):
                wait_for(pool, front_steps, FRONT * (n + 1))
                first = base + POOLF * n
                mean, var = mean_var[:, s, 0:1], mean_var[:, s, 1:2]
                a, b, c = small[:, s, 0:1], small[:, s, 1:2], small[:, s, 2:3]
                if patch:
                    nc.gpsimd.tensor_tensor(a, var, consts[:, 3:4], ALU.add).then_inc(front_pool, 1)
                    pool.wait_ge(front_pool, first + 1)
                    nc.gpsimd.tensor_tensor(rstd[:, s, 0:1], a, half_neg, ALU.pow).then_inc(front_pool, 1)
                elif latent:
                    both = small[:, s, 0:2]
                    nc.gpsimd.tensor_tensor(both, var.broadcast_to([P, 2]), pair_factor[:], ALU.mult).then_inc(front_pool, 1)
                    pool.wait_ge(front_pool, first + 1)
                    nc.gpsimd.tensor_tensor(both, both, pair_eps[:], ALU.add).then_inc(front_pool, 1)
                    pool.wait_ge(front_pool, first + 2)
                    nc.gpsimd.tensor_tensor(rstd[:, s], both, half_neg2[:], ALU.pow).then_inc(front_pool, 1)
                else:
                    nc.gpsimd.tensor_tensor(a, mean, mean, ALU.mult).then_inc(front_pool, 1)
                    pool.wait_ge(front_pool, first + 1)
                    nc.gpsimd.tensor_tensor(b, a, var, ALU.add).then_inc(front_pool, 1)
                    pool.wait_ge(front_pool, first + 2)
                    nc.gpsimd.tensor_tensor(c, b, rms_eps[:, 0:1], ALU.add).then_inc(front_pool, 1)
                    pool.wait_ge(front_pool, first + 3)
                    nc.gpsimd.tensor_tensor(rstd[:, s, 1:2], c, half_neg, ALU.pow).then_inc(front_pool, 1)

            def head_norms(n, s):
                first = 6 * n
                v, y, z = sumsq[:, s], guess[:, s], newton[:]
                wait_for(pool, sumsq_ready, n + 1)
                wait_for(pool, guess_steps, 2 * (n + 1))
                nc.gpsimd.tensor_tensor(v, v, rms_eps[:], ALU.add).then_inc(rms_steps, 1)
                wait_for(pool, rms_steps, first + 1)
                nc.gpsimd.tensor_tensor(z, v, y, ALU.mult).then_inc(rms_steps, 1)
                wait_for(pool, rms_steps, first + 2)
                nc.gpsimd.tensor_tensor(z, z, y, ALU.mult).then_inc(rms_steps, 1)
                wait_for(pool, rms_steps, first + 3)
                nc.gpsimd.tensor_tensor(z, z, half_negs[:], ALU.mult).then_inc(rms_steps, 1)
                wait_for(pool, rms_steps, first + 4)
                nc.gpsimd.tensor_tensor(z, z, three_halves[:], ALU.add).then_inc(rms_steps, 1)
                wait_for(pool, rms_steps, first + 5)
                nc.gpsimd.tensor_tensor(qk_rms[:, s], z, y, ALU.mult).then_inc(rms_steps, 1)

            def final(n, s):
                wait_for(pool, out_steps, OUT * (n + 1))
                nc.gpsimd.tensor_tensor(small2[:, s], mean_var2[:, s, 1:2], consts[:, 3:4], ALU.add).then_inc(final_rstd, 1)
                wait_for(pool, final_rstd, 2 * n + 1)
                nc.gpsimd.tensor_tensor(rstd2[:, s], small2[:, s], half_neg, ALU.pow).then_inc(final_rstd, 1)

            pool.wait_ge(consts_ready, 1)

            def step(t, i, s, has):
                if patch and has(5):
                    final(t - 5, 1 - s)
                if has(0):
                    front(t, s)
                if normed and has(1):
                    head_norms(t - 1, 1 - s)

            over(pool, step, TILES, DEPTH, PEEL)

        @block.vector
        def _(dve):
            if patch:
                nc.vector.memset(consts[:, 0:1], -0.5)
                nc.vector.memset(consts[:, 3:4], LN_EPS)
            if normed:
                nc.vector.memset(rms_eps_act[:], RMS_EPS)
            nc.vector.memset(v_diag[:], 0.0).then_inc(consts_ready, 1)
            dve.wait_ge(consts_ready, 1)
            for par in range(2):
                part = slice(par * SEQ, (par + 1) * SEQ)
                for s in range(2):
                    nc.vector.memset(v_diag[part, s, :, :, par, HD:HD + 1].rearrange("p a b c -> p (a b c)"), 1.0).then_inc(consts_ready, 1)
            dve.wait_ge(loads, LOADS)
            if normed:
                for w in ((w_qkv, w_down) if latent else (w_qkv,)):
                    for c in range(KC):
                        nc.vector.tensor_scalar(w[:, c], w[:, c], w_norm[:, c:c + 1], None, ALU.mult).then_inc(consts_ready, 1)

            def front(n, s):
                first = FRONT * n
                if patch:
                    wait_for(dve, patch_done, n + 1)
                    nc.vector.tensor_tensor(h_all[:, n], hy[:, 0:D], b_patch[:], ALU.add).then_inc(front_steps, 1)
                if patch:
                    dve.wait_ge(front_steps, first + 1)
                src = x_all if mode == "local" else h_all
                carrier(nc, spare[:])
                nc.vector.bn_stats(stats[:, s], src[:, n]).then_inc(front_steps, 1)
                dve.wait_ge(front_steps, first + FRONT - 1)
                wait_for(dve, xn_ready, XN * (n - 1))
                carrier(nc, spare[:])
                nc.vector.bn_aggr(mean_var[:, s], stats[:, s]).then_inc(front_steps, 1)

            def normalise(n, s):
                wait_for(dve, front_pool, (1 if normed else 0) + POOLF * (n + 1))
                wait_for(dve, xt_done, n - 1)
                if latent:
                    nc.vector.tensor_scalar(x_all[:, n], h_all[:, n], mean_var[:, s, 0:1], rstd[:, s, 0:1],
                                            ALU.subtract, ALU.mult).then_inc(xn_ready, 1)
                if normed and not latent:
                    nc.vector.tensor_scalar(xn[:, s], x_all[:, n], rstd[:, s, 1:2], None, ALU.mult).then_inc(xn_ready, 1)
                else:
                    nc.vector.tensor_scalar(xn[:, s], h_all[:, n], mean_var[:, s, 0:1], rstd[:, s, 1 if latent else 0:2 if latent else 1],
                                            ALU.subtract, ALU.mult).then_inc(xn_ready, 1)

            def rope(n, s):
                first = ROPE * n
                wait_for(dve, qkv_done, n + 1)
                flat = "p h e i -> p (h e i)"
                nc.vector.tensor_tensor(by_cos[:].rearrange(flat), pj[:, 0:QK], cos_t[:], ALU.mult).then_inc(rope_steps, 1)
                nc.vector.tensor_tensor(by_sin[:].rearrange(flat), pj[:, 0:QK], sin_t[:], ALU.mult).then_inc(rope_steps, 1)
                wait_for(dve, qkt_done if patch else scaled, n - 1)
                dve.wait_ge(rope_steps, first + 2)
                for e in range(2):
                    nc.vector.tensor_tensor(qk[:, s, :, e], by_cos[:, :, e], by_sin[:, :, 1 - e], ALU.add).then_inc(rope_steps, 1)
                wait_for(dve, v_ready, SPREAD_V * (n - 1))
                nc.vector.tensor_copy(v_rows[:, s], pj[:, QK:QKV]).then_inc(rope_steps, 1)

            def sum_squares(n, s):
                wait_for(dve, squares_ready, n + 1)
                nc.vector.tensor_reduce(sumsq[:, s], squares[:], AX.X, ALU.add).then_inc(sumsq_ready, 1)

            def scale_heads(n, s):
                wait_for(dve, rms_steps, 6 * (n + 1))
                wait_for(dve, qkt_done, n - 1)
                nc.vector.tensor_tensor(qkn[:, s], qk[:, s].rearrange("p h e i -> p h (e i)"),
                                        qk_rms[:, s, :, None].broadcast_to([P, ROPED, HD]), ALU.mult).then_inc(scaled, 1)

            def mask(n, s, half):
                for rl in half:
                    wait_for(dve, exp_done, 2 * n + rl + 1)
                    part = probs[:, s, 2 * rl:2 * rl + 2].rearrange("p t (c q) -> p (t c) q", q=SEQ)
                    nc.vector.tensor_tensor(part, part, causal[:, None, :].broadcast_to([P, 8, SEQ]), ALU.mult).then_inc(masked, 1)

            def spread_k(n, s):
                wait_for(dve, qt_ready, n + 1)
                wait_for(dve, scores_done, 2 * (n - 1))
                half = [GROUPS * HD, 2, 2, SEQ]
                k_t = xq[0:GROUPS * HD, 2 * P:3 * P].rearrange("p (g k) -> p g k", g=2)[:, :, None, :].broadcast_to(half)
                own = k_mask[0:GROUPS * HD, None, :, None].broadcast_to(half)
                for rl in range(2):
                    ins = nc.vector.tensor_tensor(k_diag[rl * half[0]:(rl + 1) * half[0], s], k_t, own, ALU.mult)
                ins.then_inc(kd_ready, 1)

            def soften(n, s):
                for rl in range(2):
                    wait_for(dve, scores_done, 2 * n + rl + 1)
                    wait_for(dve, pt_done, after(n - 1, 2 * (n - 2) + rl + 1))
                    pair = sc[:, 2 * rl:2 * rl + 2, 0:2 * P].rearrange("p t (c k) -> p t c k", k=SEQ)
                    out = probs[:, s, 2 * rl:2 * rl + 2].rearrange("p t (c k) -> p t c k", k=SEQ)
                    peak = top[:, s, rl].rearrange("p (t c) -> p t c", t=2)
                    nc.vector.tensor_reduce(peak, pair, AX.X, ALU.max).then_inc(soft_steps, 1)
                    wait_for(dve, soft_steps, 4 * n + 2 * rl + 1)
                    nc.vector.tensor_tensor(out, pair, peak[:, :, :, None].broadcast_to([P, 2, 4, SEQ]),
                                            ALU.subtract).then_inc(soft_steps, 1)

            def divide(n, s):
                wait_for(dve, pv_done, n + 1)
                o = ao[:, 0:16 * (HD + 1)].rearrange("p (h d) -> p h d", d=HD + 1)
                nc.vector.reciprocal(rden[:, :, None], o[:, :, HD:HD + 1]).then_inc(norm_steps, 1)
                wait_for(dve, at_done, n - 1)
                wait_for(dve, norm_steps, 2 * n + 1)
                nc.vector.tensor_tensor(attn[:, s].rearrange("p g (h d) -> p (g h) d", d=HD), o[:, :, 0:HD],
                                        rden[:, :, None].broadcast_to([P, 16, HD]), ALU.mult).then_inc(norm_steps, 1)

            def residual(n, s):
                first = OUT * n
                wait_for(dve, y_done, n + 1)
                dst = h_all if patch else x_all
                nc.vector.tensor_tensor(dst[:, n], dst[:, n], hy[:, 0:D], ALU.add).then_inc(out_steps, 1)
                if latent:
                    return
                wait_for(dve, out_steps, first + 1)
                if patch:
                    carrier(nc, spare[:])
                    nc.vector.bn_stats(stats2[:, s], h_all[:, n]).then_inc(out_steps, 1)
                    wait_for(dve, out_steps, first + 2)
                    carrier(nc, spare[:])
                    nc.vector.bn_aggr(mean_var2[:, s], stats2[:, s]).then_inc(out_steps, 1)
                else:
                    nc.vector.tensor_tensor(h_all[:, n], h_all[:, n], x_all[:, n], ALU.add).then_inc(out_steps, 1)

            def final(n, s):
                wait_for(dve, final_rstd, 2 * (n + 1))
                nc.vector.tensor_scalar(x_all[:, n], h_all[:, n], mean_var2[:, s, 0:1], rstd2[:, s], ALU.subtract,
                                        ALU.mult).then_inc(final_steps, 1)
                wait_for(dve, final_steps, 2 * n + 1)
                nc.vector.tensor_reduce(keep["x_peaks"][:, bass.ds(n, 1)],
                                        x_all[:, n], AX.X, ALU.max, apply_absolute_value=True).then_inc(final_steps, 1)

            def patch_step(t, i, s, has):
                if has(5):
                    residual(t - 5, 1 - s)
                if has(2):
                    spread_k(t - 2, s)
                if has(1):
                    rope(t - 1, 1 - s)
                if has(5):
                    final(t - 5, 1 - s)
                if has(2):
                    soften(t - 2, s)
                if has(0):
                    front(t, s)
                if has(3):
                    divide(t - 3, 1 - s)
                if has(0):
                    normalise(t, s)

            def normed_step(t, i, s, has):
                if has(5):
                    divide(t - 5, 1 - s)
                if has(6):
                    residual(t - 6, s)
                if has(0):
                    front(t, s)
                if has(4):
                    mask(t - 4, s, [0])
                if has(2):
                    scale_heads(t - 2, s)
                if has(4):
                    mask(t - 4, s, [1])
                if has(0):
                    normalise(t, s)
                if has(1):
                    rope(t - 1, 1 - s)
                if has(2):
                    spread_k(t - 2, s)
                if has(1):
                    sum_squares(t - 1, 1 - s)

            over(dve, patch_step if patch else normed_step, TILES, DEPTH, PEEL)


FFN = 768
FC = FFN // P
BLOCK = 32
GROUP = 512
NG = IMAGES * SEQ // GROUP
TPG = GROUP // TILE
Q16, Q4 = 32767.0, 7.0
LEAST_SCALE = 1e-12
MAGIC = 1.5 * 2.0 ** 23


def weights_phase(nc, dram, keep):
    with ExitStack() as ctx:
        def sb(name, shape, dt=F32):
            return ctx.enter_context(nc.sbuf_tensor(f"weights_{name}", shape, dt))

        def sem(name):
            return ctx.enter_context(nc.semaphore(f"weights_{name}"))

        FREE = FC * D
        BLOCKS = FREE // BLOCK
        names = ("ffn_gate", "ffn_up", "ffn_down")
        raw = sb("raw", [P, 3, FREE])
        whole = sb("whole", [P, 3, FREE], I16)
        scale = sb("scale", [P, 3, 2, BLOCKS])
        turned = ctx.enter_context(nc.psum_tensor("weights_turned", [P, 2, 4, P], F32))
        loads, steps, turned_done, kept = sem("loads"), sem("steps"), sem("turned"), sem("kept")
        block = ctx.enter_context(nc.Block())

        @block.sync
        def _(sp):
            sp.dma_start(keep["identity"][:], dram["identity"]).then_inc(loads, 16)
            for w, name in enumerate(names):
                sp.dma_start(raw[:, w], dram[name]).then_inc(loads, 16)
            sp.wait_ge(loads, 64)

        @block.vector
        def _(dve):
            dve.wait_ge(loads, 64)
            for w in range(3):
                blocks = raw[:, w].rearrange("p (b i) -> p b i", i=BLOCK)
                ints = whole[:, w].rearrange("p (b i) -> p b i", i=BLOCK)
                s, inv = scale[:, w, 0], scale[:, w, 1]
                nc.vector.tensor_reduce(s, blocks, AX.X, ALU.max, apply_absolute_value=True).then_inc(steps, 1)
                dve.wait_ge(steps, 5 * w + 1)
                nc.vector.tensor_scalar(s, s, 1.0 / Q4, LEAST_SCALE, ALU.mult, ALU.max).then_inc(steps, 1)
                dve.wait_ge(steps, 5 * w + 2)
                nc.vector.reciprocal(inv, s).then_inc(steps, 1)
                dve.wait_ge(steps, 5 * w + 3)
                nc.vector.tensor_tensor(ints, blocks, inv[:, :, None].broadcast_to([P, BLOCKS, BLOCK]), ALU.mult).then_inc(steps, 1)
                dve.wait_ge(steps, 5 * w + 4)
                nc.vector.tensor_tensor(blocks, ints, s[:, :, None].broadcast_to([P, BLOCKS, BLOCK]), ALU.mult).then_inc(steps, 1)

        @block.tensor
        def _(pe):
            for w in range(3):
                pe.wait_ge(steps, 5 * w + 5)
                for q in range(3):
                    n = 3 * w + q
                    if n >= 2:
                        pe.wait_ge(kept, n - 1)
                    for b in range(4):
                        at = 4 * q + b
                        mm = pe.transpose(turned[:, n % 2, b], raw[:, w, at * P:(at + 1) * P], keep["identity"][:, :])
                    mm.then_inc(turned_done, 1)

        @block.scalar
        def _(act):
            for w, name in enumerate(names):
                for q in range(3):
                    n = 3 * w + q
                    act.wait_ge(turned_done, n + 1)
                    if name == "ffn_down":
                        for b in range(4):
                            oc, ic = divmod(4 * q + b, FC)
                            ins = nc.scalar.copy(keep[name][:, ic, oc * P:(oc + 1) * P], turned[:, n % 2, b])
                    else:
                        out = keep[name][:, :, 2 * q * P:2 * (q + 1) * P].rearrange("p k (o c) -> p o k c", o=2)
                        ins = nc.scalar.copy(out, turned[:, n % 2].rearrange("p (o k) c -> p o k c", o=2))
                    ins.then_inc(kept, 1)


def gate_phase(nc, keep):
    with ExitStack() as ctx:
        def sb(name, shape, dt=F32):
            return ctx.enter_context(nc.sbuf_tensor(f"gate_{name}", shape, dt))

        def sem(name):
            return ctx.enter_context(nc.semaphore(f"gate_{name}"))

        x_all, gate, w_gate, sc = keep["x"], keep["gate"], keep["ffn_gate"], keep["scales"]
        magic_x = sb("magic_x", [P, 2, TPG * D])
        top = sb("top", [P, 2])
        prod = ctx.enter_context(nc.psum_tensor("gate_prod", [P, FC, GROUP], F32))
        turned = ctx.enter_context(nc.psum_tensor("gate_turned", [P, 2, 512], F32))
        scale_steps, quant, turned_done, xq_ready = sem("scale_steps"), sem("quant"), sem("turned"), sem("xq_ready")
        prod_done, kept, peaked = sem("prod_done"), sem("kept"), sem("peaked")
        block = ctx.enter_context(nc.Block())

        @block.gpsimd
        def _(pool):
            pool.wait_ge(scale_steps, 1)
            nc.gpsimd.partition_all_reduce(top[:, 1:2], top[:, 0:1], P, MAX_ALL).then_inc(scale_steps, 1)

        @block.vector
        def _(dve):
            nc.vector.tensor_reduce(top[:, 0:1], keep["x_peaks"][:], AX.X, ALU.max).then_inc(scale_steps, 1)
            dve.wait_ge(scale_steps, 2)
            nc.vector.tensor_scalar(sc[:, 0:1], top[:, 1:2], 1.0 / Q16, LEAST_SCALE, ALU.mult, ALU.max).then_inc(scale_steps, 1)
            dve.wait_ge(scale_steps, 3)
            nc.vector.reciprocal(sc[:, 1:2], sc[:, 0:1]).then_inc(scale_steps, 1)
            dve.wait_ge(scale_steps, 4)

            def quantise(g, s):
                wait_for(dve, turned_done, 2 * (g - 1))
                nc.vector.tensor_scalar(magic_x[:, s], x_all[:, bass.ds(g * TPG, TPG)].rearrange("p t d -> p (t d)"),
                                        sc[:, 1:2], MAGIC, ALU.mult, ALU.add).then_inc(quant, 1)

            def peak(g):
                for oc in range(FC):
                    wait_for(dve, kept, FC * g + oc + 1)
                    nc.vector.tensor_reduce(keep["gate_peaks"][:, oc, bass.ds(g, 1)], gate[:, oc, bass.ds(g * GROUP, GROUP)],
                                            AX.X, ALU.max, apply_absolute_value=True).then_inc(peaked, 1)

            def step(t, i, s, has):
                if has(0):
                    quantise(t, s)
                if has(1):
                    peak(t - 1)

            over(dve, step, NG, 1, 2)

        @block.tensor
        def _(pe):
            def turn(g, s):
                wait_for(pe, quant, g + 1)
                for half in range(2):
                    wait_for(pe, xq_ready, after(g, 2 * (g - 1) + half + 1))
                    for c in range(4):
                        at = (4 * half + c) * P
                        mm = pe.transpose(turned[:, half, c * P:(c + 1) * P], magic_x[:, s, at:at + P], keep["identity"][:, :])
                    mm.then_inc(turned_done, 1)

            def product(g):
                wait_for(pe, xq_ready, 2 * (g + 1))
                for oc in range(FC):
                    wait_for(pe, kept, after(g, FC * (g - 1) + oc + 1))
                    for c in range(KC):
                        mm = pe.matmul(prod[:, oc], w_gate[:, c, oc * P:(oc + 1) * P],
                                       x_all[:, bass.ds(g * TPG, TPG), c * P:(c + 1) * P], start=c == 0, stop=c == KC - 1)
                    mm.then_inc(prod_done, 1)

            def step(t, i, s, has):
                if has(0):
                    turn(t, s)
                if has(1):
                    product(t - 1)

            over(pe, step, NG, 1, 2)

        @block.scalar
        def _(act):
            def keep_x(g, s):
                for half in range(2):
                    wait_for(act, turned_done, 2 * g + half + 1)
                    nc.scalar.activation(x_all[:, bass.ds(g * TPG + 2 * half, 2)].rearrange("p t d -> p (t d)"),
                                         turned[:, half], ACT.Copy, bias=-MAGIC).then_inc(xq_ready, 1)

            def keep_gate(g):
                for oc in range(FC):
                    wait_for(act, prod_done, FC * g + oc + 1)
                    nc.scalar.copy(gate[:, oc, bass.ds(g * GROUP, GROUP)], prod[:, oc]).then_inc(kept, 1)

            def step(t, i, s, has):
                if has(0):
                    keep_x(t, s)
                if has(1):
                    keep_gate(t - 1)

            over(act, step, NG, 1, 2)


def up_phase(nc, keep):
    with ExitStack() as ctx:
        def sb(name, shape, dt=F32):
            return ctx.enter_context(nc.sbuf_tensor(f"up_{name}", shape, dt))

        def sem(name):
            return ctx.enter_context(nc.semaphore(f"up_{name}"))

        x_all, gate, w_up, sc = keep["x"], keep["gate"], keep["ffn_up"], keep["scales"]
        up_rows = sb("up_rows", [P, 3, GROUP])
        gate_int = sb("gate_int", [P, 3, GROUP], I16)
        sig = sb("sig", [P, 2, GROUP])
        sig_int = sb("sig_int", [P, 3, GROUP], U16)
        top = sb("top", [P, 4])
        prod = ctx.enter_context(nc.psum_tensor("up_prod", [P, FC, GROUP], F32))
        scale_steps, prod_done, kept, peaked, stored = (
            sem("scale_steps"), sem("prod_done"), sem("kept"), sem("peaked"), [sem("stored0"), sem("stored1"), sem("stored2")])
        gate_ready, sig_ready, sig_whole, gated = sem("gate_ready"), sem("sig_ready"), sem("sig_whole"), sem("gated")
        block = ctx.enter_context(nc.Block())

        @block.gpsimd
        def _(pool):
            pool.wait_ge(scale_steps, 1)
            nc.gpsimd.partition_all_reduce(top[:, 1:2], top[:, 0:1], P, MAX_ALL).then_inc(scale_steps, 1)

        @block.sync
        def _(sp):
            with sp.Fori(0, NG) as g:
                for oc in range(FC):
                    sp.wait_ge(kept, FC * g + oc + 1)
                    sp.dma_start(keep["up_dram"][:, oc, bass.ds(g * GROUP, GROUP)], up_rows[:, oc % 3]).then_inc(stored[oc % 3], 16)
            for q in stored:
                sp.wait_ge(q, 16 * NG * FC // 3)

        @block.tensor
        def _(pe):
            def product(g):
                for oc in range(FC):
                    wait_for(pe, peaked, after(g, FC * (g - 1) + oc + 1))
                    for c in range(KC):
                        mm = pe.matmul(prod[:, oc], w_up[:, c, oc * P:(oc + 1) * P],
                                       x_all[:, bass.ds(g * TPG, TPG), c * P:(c + 1) * P], start=c == 0, stop=c == KC - 1)
                    mm.then_inc(prod_done, 1)

            over(pe, lambda t, i, s, has: product(t), NG, 0, 2)

        @block.scalar
        def _(act):
            act.wait_ge(scale_steps, 6)

            def sigmoid(g, oc):
                wait_for(act, gate_ready, FC * g + oc + 1)
                wait_for(act, sig_whole, FC * g + oc - 1)
                nc.scalar.activation(sig[:, oc % 2], gate_int[:, oc % 3], ACT.Sigmoid, scale=sc[:, 2:3]).then_inc(sig_ready, 1)

            def step(g, i, s, has):
                for oc in range(FC):
                    if has(0):
                        wait_for(act, gated, FC * g + oc - 2)
                        nc.scalar.activation(gate_int[:, oc % 3], gate[:, oc, bass.ds(g * GROUP, GROUP)], ACT.Copy,
                                             scale=sc[:, 3:4]).then_inc(gate_ready, 1)
                        wait_for(act, prod_done, FC * g + oc + 1)
                        wait_for(act, stored[oc % 3], 16 * (2 * g + oc // 3))
                        nc.scalar.copy(up_rows[:, oc % 3], prod[:, oc]).then_inc(kept, 1)
                    if oc and has(0):
                        sigmoid(g, oc - 1)
                    if not oc and has(1):
                        sigmoid(g - 1, FC - 1)

            over(act, step, NG, 1, 2)

        @block.vector
        def _(dve):
            nc.vector.tensor_reduce(top[:, 0:1], keep["gate_peaks"][:], AX.XY, ALU.max).then_inc(scale_steps, 1)
            dve.wait_ge(scale_steps, 2)
            nc.vector.tensor_scalar(top[:, 2:3], top[:, 1:2], sc[:, 0:1], None, ALU.mult).then_inc(scale_steps, 1)
            dve.wait_ge(scale_steps, 3)
            nc.vector.tensor_scalar(sc[:, 2:3], top[:, 2:3], 1.0 / Q16, LEAST_SCALE, ALU.mult, ALU.max).then_inc(scale_steps, 1)
            dve.wait_ge(scale_steps, 4)
            nc.vector.reciprocal(top[:, 3:4], sc[:, 2:3]).then_inc(scale_steps, 1)
            dve.wait_ge(scale_steps, 5)
            nc.vector.tensor_tensor(sc[:, 3:4], top[:, 3:4], sc[:, 0:1], ALU.mult).then_inc(scale_steps, 1)
            dve.wait_ge(scale_steps, 6)

            def up_peak(g, oc):
                wait_for(dve, kept, FC * g + oc + 1)
                nc.vector.tensor_reduce(keep["up_peaks"][:, oc, bass.ds(g, 1)], prod[:, oc], AX.X, ALU.max,
                                        apply_absolute_value=True).then_inc(peaked, 1)

            def whole_sigmoid(g, oc):
                wait_for(dve, sig_ready, FC * g + oc + 1)
                wait_for(dve, gated, FC * g + oc - 2)
                nc.vector.tensor_scalar(sig_int[:, oc % 3], sig[:, oc % 2], 65536.0, 65535.0, ALU.mult, ALU.min).then_inc(sig_whole, 1)

            def multiply(g, oc):
                wait_for(dve, sig_whole, FC * g + oc + 1)
                nc.vector.tensor_tensor(gate[:, oc, bass.ds(g * GROUP, GROUP)], gate_int[:, oc % 3], sig_int[:, oc % 3],
                                        ALU.mult).then_inc(gated, 1)

            def gated_peak(g, oc):
                wait_for(dve, gated, FC * g + oc + 1)
                nc.vector.tensor_reduce(keep["silu_peaks"][:, oc, bass.ds(g, 1)], gate[:, oc, bass.ds(g * GROUP, GROUP)],
                                        AX.X, ALU.max, apply_absolute_value=True)

            def behind(stage, g, oc, lag, has):
                if oc >= lag and has(0):
                    stage(g, oc - lag)
                if oc < lag and has(1):
                    stage(g - 1, oc - lag + FC)

            def step(g, i, s, has):
                for oc in range(FC):
                    if has(0):
                        up_peak(g, oc)
                    behind(whole_sigmoid, g, oc, 1, has)
                    behind(gated_peak, g, oc, 2, has)
                    behind(multiply, g, oc, 1, has)

            over(dve, step, NG, 1, 2)


def mix_phase(nc, keep):
    UNIT = 1024
    UNITS = IMAGES * SEQ // UNIT
    with ExitStack() as ctx:
        def sb(name, shape, dt=F32):
            return ctx.enter_context(nc.sbuf_tensor(f"mix_{name}", shape, dt))

        def sem(name):
            return ctx.enter_context(nc.semaphore(f"mix_{name}"))

        gate, sc = keep["gate"], keep["scales"]
        up_rows = sb("up_rows", [P, 3, UNIT])
        up_int = sb("up_int", [P, 3, UNIT], I16)
        gate_int = sb("gate_int", [P, 3, UNIT], I16)
        top = sb("top", [P, 8])
        scale_steps, up_ready = sem("scale_steps"), sem("up_ready")
        gate_ready, mixed = sem("gate_ready"), sem("mixed")
        loaded = [sem("loaded0"), sem("loaded1"), sem("loaded2")]
        block = ctx.enter_context(nc.Block())

        @block.sync
        def _(sp):
            def step(u, i, s, has):
                for oc in range(FC):
                    wait_for(sp, up_ready, FC * u + oc - 2)
                    sp.dma_start(up_rows[:, oc % 3], keep["up_dram"][:, oc, bass.ds(u * UNIT, UNIT)]).then_inc(loaded[oc % 3], 16)

            over(sp, step, UNITS, 0, 2)

        @block.gpsimd
        def _(pool):
            pool.wait_ge(scale_steps, 2)
            nc.gpsimd.partition_all_reduce(top[:, 2:4], top[:, 0:2], P, MAX_ALL).then_inc(scale_steps, 1)

        @block.scalar
        def _(act):
            act.wait_ge(scale_steps, 8)

            def step(u, i, s, has):
                for oc in range(FC):
                    wait_for(act, loaded[oc % 3], 16 * (2 * u + oc // 3 + 1))
                    wait_for(act, mixed, FC * u + oc - 2)
                    nc.scalar.activation(up_int[:, oc % 3], up_rows[:, oc % 3], ACT.Copy, scale=sc[:, 5:6]).then_inc(up_ready, 1)
                    nc.scalar.activation(gate_int[:, oc % 3], gate[:, oc, bass.ds(u * UNIT, UNIT)], ACT.Copy,
                                         scale=sc[:, 4:5]).then_inc(gate_ready, 1)

            over(act, step, UNITS, 0, 2)

        @block.vector
        def _(dve):
            nc.vector.tensor_reduce(top[:, 0:1], keep["up_peaks"][:], AX.XY, ALU.max).then_inc(scale_steps, 1)
            nc.vector.tensor_reduce(top[:, 1:2], keep["silu_peaks"][:], AX.XY, ALU.max).then_inc(scale_steps, 1)
            dve.wait_ge(scale_steps, 3)
            nc.vector.tensor_scalar(top[:, 4:5], top[:, 2:3], sc[:, 0:1], None, ALU.mult).then_inc(scale_steps, 1)
            nc.vector.tensor_scalar(top[:, 5:6], top[:, 3:4], sc[:, 2:3], 1.0 / 65536, ALU.mult, ALU.mult).then_inc(scale_steps, 1)
            dve.wait_ge(scale_steps, 5)
            nc.vector.tensor_scalar(sc[:, 6:8], top[:, 4:6], 1.0 / Q16, LEAST_SCALE, ALU.mult, ALU.max).then_inc(scale_steps, 1)
            dve.wait_ge(scale_steps, 6)
            nc.vector.reciprocal(top[:, 0:2], sc[:, 6:8]).then_inc(scale_steps, 1)
            dve.wait_ge(scale_steps, 7)
            nc.vector.tensor_scalar(sc[:, 4:5], top[:, 1:2], sc[:, 2:3], 1.0 / 65536, ALU.mult, ALU.mult)
            nc.vector.tensor_tensor(sc[:, 5:6], top[:, 0:1], sc[:, 0:1], ALU.mult).then_inc(scale_steps, 1)
            dve.wait_ge(scale_steps, 8)

            def product(u, oc):
                wait_for(dve, up_ready, FC * u + oc + 1)
                wait_for(dve, gate_ready, FC * u + oc + 1)
                nc.vector.tensor_tensor(gate[:, oc, bass.ds(u * UNIT, UNIT)], gate_int[:, oc % 3], up_int[:, oc % 3],
                                        ALU.mult).then_inc(mixed, 1)

            def peak(u, oc):
                wait_for(dve, mixed, FC * u + oc + 1)
                nc.vector.tensor_reduce(keep["out_peaks"][:, oc, bass.ds(u, 1)], gate[:, oc, bass.ds(u * UNIT, UNIT)],
                                        AX.X, ALU.max, apply_absolute_value=True)

            def step(u, i, s, has):
                for oc in range(FC):
                    if has(0):
                        product(u, oc)
                    if oc and has(0):
                        peak(u, oc - 1)
                    if not oc and has(1):
                        peak(u - 1, FC - 1)

            over(dve, step, UNITS, 1, 2)


def down_phase(nc, keep):
    with ExitStack() as ctx:
        def sb(name, shape, dt=F32):
            return ctx.enter_context(nc.sbuf_tensor(f"down_{name}", shape, dt))

        def sem(name):
            return ctx.enter_context(nc.semaphore(f"down_{name}"))

        h_all, gate, w_down, sc = keep["h"], keep["gate"], keep["ffn_down"], keep["scales"]
        magic = sb("magic", [P, 2, FC, TILE])
        whole = sb("whole", [P, 2, FC, TILE])
        top = sb("top", [P, 4])
        out = ctx.enter_context(nc.psum_tensor("down_out", [P, 2, 512], F32))
        scale_steps, rounded, whole_ready, down_done, added = (
            sem("scale_steps"), sem("rounded"), sem("whole_ready"), sem("down_done"), sem("added"))
        block = ctx.enter_context(nc.Block())

        @block.gpsimd
        def _(pool):
            pool.wait_ge(scale_steps, 1)
            nc.gpsimd.partition_all_reduce(top[:, 1:2], top[:, 0:1], P, MAX_ALL).then_inc(scale_steps, 1)

        @block.scalar
        def _(act):
            def step(n, i, s, has):
                wait_for(act, rounded, n + 1)
                wait_for(act, down_done, n - 1)
                nc.scalar.activation(whole[:, s].rearrange("p c t -> p (c t)"), magic[:, s].rearrange("p c t -> p (c t)"),
                                     ACT.Copy, bias=-MAGIC).then_inc(whole_ready, 1)

            over(act, step, TILES, 0, 4)

        @block.tensor
        def _(pe):
            def step(n, i, s, has):
                wait_for(pe, whole_ready, n + 1)
                wait_for(pe, added, n - 1)
                for c in range(FC):
                    mm = pe.matmul(out[:, s, 0:D], whole[:, s, c], w_down[:, c], start=c == 0, stop=c == FC - 1)
                mm.then_inc(down_done, 1)

            over(pe, step, TILES, 0, 4)

        @block.vector
        def _(dve):
            nc.vector.tensor_reduce(top[:, 0:1], keep["out_peaks"][:], AX.XY, ALU.max).then_inc(scale_steps, 1)
            dve.wait_ge(scale_steps, 2)
            nc.vector.tensor_scalar(top[:, 2:3], top[:, 1:2], sc[:, 6:7], sc[:, 7:8], ALU.mult, ALU.mult).then_inc(scale_steps, 1)
            dve.wait_ge(scale_steps, 3)
            nc.vector.tensor_scalar(sc[:, 8:9], top[:, 2:3], 1.0 / Q16, LEAST_SCALE, ALU.mult, ALU.max).then_inc(scale_steps, 1)
            dve.wait_ge(scale_steps, 4)
            nc.vector.reciprocal(top[:, 3:4], sc[:, 8:9]).then_inc(scale_steps, 1)
            dve.wait_ge(scale_steps, 5)
            nc.vector.tensor_scalar(sc[:, 9:10], top[:, 3:4], sc[:, 6:7], sc[:, 7:8], ALU.mult, ALU.mult).then_inc(scale_steps, 1)
            dve.wait_ge(scale_steps, 6)

            def round_out(n, s):
                wait_for(dve, whole_ready, n - 1)
                nc.vector.tensor_scalar(magic[:, s], gate[:, :, bass.ds(n * TILE, TILE)], sc[:, 9:10], MAGIC,
                                        ALU.mult, ALU.add).then_inc(rounded, 1)

            def add(n, s):
                wait_for(dve, down_done, n + 1)
                nc.vector.scalar_tensor_tensor(h_all[:, n], out[:, s, 0:D], sc[:, 8:9], h_all[:, n], ALU.mult,
                                               ALU.add).then_inc(added, 1)

            def step(t, i, s, has):
                if has(0):
                    round_out(t, s)
                if has(1):
                    add(t - 1, 1 - s)

            over(dve, step, TILES, 1, 4)


PROTOS, RANK = 32, 16
LOW = PROTOS * RANK


def experts_phase(nc, dram, out_dram, keep):
    with ExitStack() as ctx:
        def sb(name, shape, dt=F32):
            return ctx.enter_context(nc.sbuf_tensor(f"experts_{name}", shape, dt))

        def bank(name, shape):
            return ctx.enter_context(nc.psum_tensor(f"experts_{name}", shape, F32))

        def sem(name):
            return ctx.enter_context(nc.semaphore(f"experts_{name}"))

        h_all, identity, consts = keep["h"], keep["identity"], keep["consts"]
        protos = sb("protos", [P, KC, PROTOS])
        proto_sq = sb("proto_sq", [P, KC, PROTOS])
        norms = sb("norms", [P, PROTOS])
        ones = sb("ones", [P, P])
        b_maps = sb("b_maps", [P, KC, LOW])
        a_maps = sb("a_maps", [P, LOW // P, D])
        bias = sb("bias", [P, D])
        number = sb("number", [P, PROTOS])
        temp = sb("temp", [P, 4])
        stats = sb("stats", [P, 2, 6])
        spare = sb("spare", [P, 1])
        minus = sb("minus", [P, 2])
        mean_var = sb("mean_var", [P, 2, 2])
        small = sb("small", [P, 2, 1])
        rstd = sb("rstd", [P, 2, 1])
        xn = sb("xn", [P, 2, D])
        squares = sb("squares", [P, D])
        x_norm = sb("x_norm", [P, 2, 1])
        xT = sb("xT", [P, 2, KC, TILE])
        sums = sb("sums", [P, PROTOS])
        near = sb("near", [P, 2, PROTOS])
        best = sb("best", [P, 2, 8])
        best_at = sb("best_at", [P, 8], U32)
        at = sb("at", [P, 2, 2])
        dist = sb("dist", [P, 2, 4])
        share = sb("share", [P, 2, 4])
        picked = sb("picked", [P, 2, PROTOS])
        shares = sb("shares", [P, 2, P])
        low = sb("low", [P, 2, LOW])
        lowT = sb("lowT", [P, 2, LOW])
        sharesT = sb("sharesT", [P, 2, P])
        result = sb("result", [P, 2, D])

        xb = bank("xb", [P, 512])
        dots = bank("dots", [P, 512])
        first = bank("first", [P, 2, 512])
        lt = bank("lt", [P, 512])
        st = bank("st", [P, 512])
        yb = bank("yb", [P, 2, 512])

        loads, consts_ready, front_steps, front_pool = sem("loads"), sem("consts_ready"), sem("front"), sem("front_pool")
        xn_ready, xt_done, xt_ready, x_norm_ready = sem("xn_ready"), sem("xt_done"), sem("xt_ready"), sem("x_norm")
        dots_done, first_done, pick, roots, exp_done = sem("dots_done"), sem("first_done"), sem("pick"), sem("roots"), sem("exp_done")
        share_steps, lt_done, lt_ready, y_done, stored = sem("share"), sem("lt_done"), sem("lt_ready"), sem("y_done"), [sem("stored0"), sem("stored1")]
        result_ready = sem("result_ready")
        PICK = 6
        SHARE = 8
        DEPTH, PEEL = 4, 6

        loaded = [(protos, dram["protos"]), (b_maps, dram["b_maps"]), (a_maps, dram["a_maps"]), (number, dram["number"])]
        LOADS = 16 * (len(loaded) + 2)
        block = ctx.enter_context(nc.Block())

        @block.sync
        def _(sp):
            for to, frm in loaded:
                sp.dma_start(to[:], frm).then_inc(loads, 16)
            sp.dma_start(temp[:, 0:1], dram["temp"]).then_inc(loads, 16)
            sp.wait_ge(consts_ready, 1)
            sp.dma_start(bias[0:PROTOS], dram["bias"]).then_inc(loads, 16)

            def step(n, i, s, has):
                wait_for(sp, result_ready, n + 1)
                sp.dma_start(out_dram[n], result[:, s]).then_inc(stored[s], 16)

            over(sp, step, TILES, 0, 2)
            for s in range(2):
                sp.wait_ge(stored[s], 16 * TILES // 2)

        @block.tensor
        def _(pe):
            pe.wait_ge(consts_ready, 6)
            for c in range(KC):
                mm = pe.matmul(dots[:, 0:PROTOS], ones[:, :], proto_sq[:, c], start=c == 0, stop=c == KC - 1)
            mm.then_inc(dots_done, 1)
            pe.wait_ge(consts_ready, 9)

            def turn_x(n, s):
                wait_for(pe, xn_ready, n + 1)
                wait_for(pe, xt_ready, n)
                for c in range(KC):
                    mm = pe.transpose(xb[:, c * P:(c + 1) * P], xn[:, s, c * P:(c + 1) * P], identity[:, :])
                mm.then_inc(xt_done, 1)

            def products(n, s):
                wait_for(pe, xt_ready, n + 1)
                wait_for(pe, pick, after(n, PICK * (n - 1) + 2))
                for c in range(KC):
                    mm = pe.matmul(dots[:, 0:PROTOS], xT[:, s, c], protos[:, c], start=c == 0, stop=c == KC - 1)
                mm.then_inc(dots_done, 1)
                wait_for(pe, share_steps, after(n - 1, SHARE * (n - 2) + SHARE))
                for c in range(KC):
                    mm = pe.matmul(first[:, s], xT[:, s, c], b_maps[:, c], start=c == 0, stop=c == KC - 1)
                mm.then_inc(first_done, 1)

            def turn_low(n, s):
                wait_for(pe, share_steps, SHARE * (n + 1))
                wait_for(pe, lt_ready, 2 * n)
                for c in range(LOW // P):
                    mm = pe.transpose(lt[:, c * P:(c + 1) * P], low[:, s, c * P:(c + 1) * P], identity[:, :])
                mm.then_inc(lt_done, 1)
                pe.transpose(st[:, 0:P], shares[:, s], identity[:, :]).then_inc(lt_done, 1)

            def second(n, s):
                wait_for(pe, lt_ready, 2 * (n + 1))
                wait_for(pe, result_ready, n - 1)
                for c in range(LOW // P):
                    pe.matmul(yb[:, s, 0:D], lowT[:, s, c * P:(c + 1) * P], a_maps[:, c], start=c == 0, stop=False)
                pe.matmul(yb[:, s, 0:D], sharesT[:, s], bias[:, :], start=False, stop=True).then_inc(y_done, 1)

            def step(t, i, s, has):
                if has(1):
                    turn_x(t - 1, 1 - s)
                if has(3):
                    turn_low(t - 3, 1 - s)
                if has(1):
                    products(t - 1, 1 - s)
                if has(3):
                    second(t - 3, 1 - s)

            over(pe, step, TILES, DEPTH, PEEL)

        @block.scalar
        def _(act):
            act.wait_ge(consts_ready, 9)

            def keep_x(n, s):
                wait_for(act, xn_ready, n + 1)
                wait_for(act, pick, after(n - 1, PICK * (n - 2) + 1))
                nc.scalar.activation(squares[:], xn[:, s], ACT.Square, accum_out=x_norm[:, s]).then_inc(x_norm_ready, 1)
                wait_for(act, xt_done, n + 1)
                wait_for(act, first_done, n - 1)
                nc.scalar.copy(xT[:, s].rearrange("p c t -> p (c t)"), xb[:, 0:D]).then_inc(xt_ready, 1)

            def keep_low(n, s):
                wait_for(act, lt_done, 2 * n + 1)
                wait_for(act, y_done, n - 1)
                nc.scalar.copy(lowT[:, s], lt[:, :]).then_inc(lt_ready, 1)
                wait_for(act, lt_done, 2 * n + 2)
                nc.scalar.copy(sharesT[:, s], st[:, 0:P]).then_inc(lt_ready, 1)

            def exponent(n, s):
                wait_for(act, share_steps, SHARE * n + 1)
                nc.scalar.activation(share[:, s, 1:2], share[:, s, 0:1], ACT.Exp, scale=temp[:, 3:4]).then_inc(exp_done, 1)

            def step(t, i, s, has):
                if has(1):
                    keep_x(t - 1, 1 - s)
                if has(3):
                    keep_low(t - 3, 1 - s)
                if has(2):
                    exponent(t - 2, s)

            over(act, step, TILES, DEPTH, PEEL)

        @block.gpsimd
        def _(pool):
            def front(n, s):
                wait_for(pool, front_steps, 2 * (n + 1))
                nc.gpsimd.tensor_tensor(small[:, s], mean_var[:, s, 1:2], consts[:, 3:4], ALU.add).then_inc(front_pool, 1)
                wait_for(pool, front_pool, 2 * n + 1)
                nc.gpsimd.tensor_tensor(rstd[:, s], small[:, s], consts[:, 0:1], ALU.pow).then_inc(front_pool, 1)

            def distances(n, s):
                wait_for(pool, pick, PICK * (n + 1))
                nc.gpsimd.tensor_tensor(dist[:, s, 0:2], best[:, s, 0:2], minus[:], ALU.mult).then_inc(roots, 1)
                wait_for(pool, roots, 2 * n + 1)
                nc.gpsimd.tensor_tensor(dist[:, s, 2:4], dist[:, s, 0:2], consts[:, 1:3], ALU.pow).then_inc(roots, 1)

            pool.wait_ge(consts_ready, 9)

            def step(t, i, s, has):
                if has(0):
                    front(t, s)
                if has(1):
                    distances(t - 1, 1 - s)

            over(pool, step, TILES, DEPTH, PEEL)

        @block.vector
        def _(dve):
            nc.vector.memset(minus[:], -1.0)
            nc.vector.memset(bias[:], 0.0).then_inc(consts_ready, 1)
            nc.vector.memset(shares[:], 0.0).then_inc(consts_ready, 1)
            nc.vector.memset(ones[:], 1.0).then_inc(consts_ready, 1)
            nc.vector.memset(consts[:, 1:3], 0.5).then_inc(consts_ready, 1)
            dve.wait_ge(loads, LOADS)
            nc.vector.tensor_tensor(proto_sq[:], protos[:], protos[:], ALU.mult).then_inc(consts_ready, 1)
            nc.vector.tensor_scalar(temp[:, 1:2], temp[:, 0:1], -1.0, None, ALU.mult).then_inc(consts_ready, 1)
            dve.wait_ge(consts_ready, 6)
            nc.vector.scalar_tensor_tensor(temp[:, 2:3], temp[:, 0:1], 0.1, temp[:, 1:2], ALU.max, ALU.max).then_inc(consts_ready, 1)
            dve.wait_ge(consts_ready, 7)
            nc.vector.reciprocal(temp[:, 3:4], temp[:, 2:3]).then_inc(consts_ready, 1)
            dve.wait_ge(dots_done, 1)
            nc.vector.tensor_copy(norms[:], dots[:, 0:PROTOS]).then_inc(consts_ready, 1)
            dve.wait_ge(consts_ready, 9)

            def front(n, s):
                carrier(nc, spare[:])
                nc.vector.bn_stats(stats[:, s], h_all[:, n]).then_inc(front_steps, 1)
                wait_for(dve, front_steps, 2 * n + 1)
                carrier(nc, spare[:])
                nc.vector.bn_aggr(mean_var[:, s], stats[:, s]).then_inc(front_steps, 1)

            def normalise(n, s):
                wait_for(dve, front_pool, 2 * (n + 1))
                wait_for(dve, xt_done, n - 1)
                wait_for(dve, x_norm_ready, n - 1)
                nc.vector.tensor_scalar(xn[:, s], h_all[:, n], mean_var[:, s, 0:1], rstd[:, s], ALU.subtract,
                                        ALU.mult).then_inc(xn_ready, 1)

            def choose(n, s):
                at0 = PICK * n
                wait_for(dve, x_norm_ready, n + 1)
                wait_for(dve, roots, 2 * (n - 1))
                nc.vector.tensor_scalar(sums[:], norms[:], x_norm[:, s], None, ALU.add).then_inc(pick, 1)
                wait_for(dve, dots_done, n + 2)
                wait_for(dve, pick, at0 + 1)
                nc.vector.scalar_tensor_tensor(near[:, s], dots[:, 0:PROTOS], 2.0, sums[:], ALU.mult, ALU.subtract).then_inc(pick, 1)
                wait_for(dve, pick, at0 + 2)
                nc.vector.tensor_scalar(near[:, s], near[:, s], 0.0, None, ALU.min).then_inc(pick, 1)
                wait_for(dve, pick, at0 + 3)
                carrier(nc, spare[:])
                nc.vector.max(best[:, s], near[:, s]).then_inc(pick, 1)
                wait_for(dve, pick, at0 + 4)
                carrier(nc, spare[:])
                nc.vector.max_index(best_at[:], best[:, s], near[:, s]).then_inc(pick, 1)
                wait_for(dve, pick, at0 + 5)
                nc.vector.tensor_copy(at[:, s], best_at[:, 0:2]).then_inc(pick, 1)

            def weigh(n, s):
                at0 = SHARE * n
                wait_for(dve, roots, 2 * (n + 1))
                nc.vector.tensor_tensor(share[:, s, 0:1], dist[:, s, 2:3], dist[:, s, 3:4], ALU.subtract).then_inc(share_steps, 1)
                wait_for(dve, exp_done, n + 1)
                nc.vector.tensor_scalar(share[:, s, 2:3], share[:, s, 1:2], 1.0, None, ALU.add).then_inc(share_steps, 1)
                wait_for(dve, share_steps, at0 + 2)
                nc.vector.reciprocal(share[:, s, 0:1], share[:, s, 2:3]).then_inc(share_steps, 1)
                wait_for(dve, share_steps, at0 + 3)
                nc.vector.tensor_scalar(share[:, s, 3:4], share[:, s, 1:2], share[:, s, 0:1], None, ALU.mult).then_inc(share_steps, 1)
                nc.vector.tensor_scalar(picked[:, s], number[:], at[:, s, 0:1], share[:, s, 0:1], ALU.is_equal, ALU.mult).then_inc(share_steps, 1)
                wait_for(dve, share_steps, at0 + 5)
                wait_for(dve, lt_done, 2 * (n - 1))
                nc.vector.tensor_scalar(shares[:, s, 0:PROTOS], number[:], at[:, s, 1:2], share[:, s, 3:4], ALU.is_equal, ALU.mult).then_inc(share_steps, 1)
                wait_for(dve, share_steps, at0 + 6)
                nc.vector.tensor_tensor(shares[:, s, 0:PROTOS], shares[:, s, 0:PROTOS], picked[:, s], ALU.add).then_inc(share_steps, 1)
                wait_for(dve, share_steps, at0 + 7)
                wait_for(dve, first_done, n + 1)
                nc.vector.tensor_tensor(low[:, s].rearrange("p (e r) -> p e r", r=RANK), first[:, s].rearrange("p (e r) -> p e r", r=RANK),
                                        shares[:, s, 0:PROTOS, None].broadcast_to([P, PROTOS, RANK]), ALU.mult).then_inc(share_steps, 1)

            def finish(n, s, pair):
                wait_for(dve, y_done, n + 1)
                wait_for(dve, stored[s], 16 * pair)
                nc.vector.tensor_tensor(result[:, s], h_all[:, n], yb[:, s, 0:D], ALU.add).then_inc(result_ready, 1)

            def step(t, i, s, has):
                if has(1):
                    normalise(t - 1, 1 - s)
                if has(2):
                    weigh(t - 2, s)
                if has(0):
                    front(t, s)
                if has(1):
                    choose(t - 1, 1 - s)
                if has(3):
                    finish(t - 3, 1 - s, i - 2 + s)

            over(dve, step, TILES, DEPTH, PEEL)


def vit_tower(nc, dram, out_dram):
    with ExitStack() as ctx:
        def sb(name, shape, dt=F32):
            return ctx.enter_context(nc.sbuf_tensor(name, shape, dt))

        keep = {
            "h": sb("h_all", [P, TILES, D]), "x": sb("x_all", [P, TILES, D]), "identity": sb("identity", [P, P]),
            "consts": sb("consts", [P, 4]), "x_peaks": sb("x_peaks", [P, TILES]),
            "ffn_gate": sb("ffn_gate", [P, KC, FFN]), "ffn_up": sb("ffn_up", [P, KC, FFN]), "ffn_down": sb("ffn_down", [P, FC, D]),
            "gate_peaks": sb("gate_peaks", [P, FC, NG]), "up_peaks": sb("up_peaks", [P, FC, NG]),
            "silu_peaks": sb("silu_peaks", [P, FC, NG]), "out_peaks": sb("out_peaks", [P, FC, 4]),
            "scales": sb("scales", [P, 10]), "up_dram": nc.dram_tensor("up_rows_dram", (P, FC, IMAGES * SEQ), F32).ap(),
        }

        def of(mode):
            own = {k: dram[f"{mode}_{k}"] for k in ("w_qkv", "w_out", "cos", "sin", "w_norm") if f"{mode}_{k}" in dram}
            return {**dram, **own}

        weights_phase(nc, dram, keep)
        attention_phase(nc, "patch", of("patch"), keep)
        with nc.sbuf_tensor("gate", [P, FC, IMAGES * SEQ], F32) as gate:
            keep["gate"] = gate
            gate_phase(nc, keep)
            up_phase(nc, keep)
            mix_phase(nc, keep)
            down_phase(nc, keep)
        attention_phase(nc, "global", of("global"), keep)
        attention_phase(nc, "local", of("local"), keep)
        experts_phase(nc, dram, out_dram, keep)


def head_columns(w):
    return w.reshape(-1, GROUPS, HEADS // GROUPS, HD // 2, 2).transpose(0, 2, 1, 4, 3).reshape(-1, D)


def k_columns(w):
    return w.reshape(-1, GROUPS, HD // 2, 2).transpose(0, 1, 3, 2).reshape(-1, GROUPS * HD)


def v_columns(w):
    return w.reshape(-1, 2, 2, HD).transpose(0, 2, 1, 3).reshape(-1, GROUPS * HD)


def out_rows(w):
    return w.reshape(GROUPS, 2, 2, HD, -1).transpose(2, 0, 3, 1, 4).reshape(P, 2, -1)


def in_chunks(w):
    return w.reshape(-1, P, w.shape[1]).transpose(1, 0, 2)


def rope_tables(q_freq, k_freq):
    pos = np.arange(SEQ, dtype=np.float32)[:, None]
    q = head_columns(np.repeat(pos * q_freq[None, :], 2, axis=1))
    k = k_columns(np.repeat(pos * np.tile(k_freq, GROUPS)[None, :], 2, axis=1))
    angle = np.tile(np.concatenate([q, k], axis=1), (2, 1)).astype(np.float32)
    sign = np.tile(np.repeat(np.array([1, -1], np.float32), HD // 2), ROPED)
    return np.cos(angle), np.sin(angle) * sign


def frequencies(base, width):
    return (np.float32(1) / np.float32(base) ** (np.arange(0, width, 2, dtype=np.float32) / np.float32(width))).astype(np.float32)


def layouts(a):
    out = {}
    x = a["x"].reshape(TILES, 2, 3, 8, 16, 8, 16).transpose(2, 4, 6, 0, 1, 3, 5).reshape(PC, P, TILES, TILE)
    out["patches"] = x.transpose(2, 1, 0, 3)
    out["w_patch"] = in_chunks(a["L0_tok_W"].T)
    out["b_patch"] = np.broadcast_to(a["L0_tok_b"], (P, D))
    out["identity"] = np.eye(P, dtype=np.float32)
    par_of = (np.arange(P) // HD) % 2
    out["k_mask"] = (par_of[:, None] == np.arange(2)[None, :]).astype(np.float32)
    out["causal"] = ((np.arange(P) % SEQ)[:, None] <= np.arange(SEQ)[None, :]).astype(np.float32)
    f0 = frequencies(10000.0, D)
    out["patch_cos"], out["patch_sin"] = rope_tables(f0, f0[:HD // 2])
    for mode, base in (("global", 1000000.0), ("local", 10000.0)):
        f = frequencies(base, HD)
        out[mode + "_cos"], out[mode + "_sin"] = rope_tables(np.tile(f, HEADS), f)
    out["patch_w_qkv"] = in_chunks(np.concatenate([head_columns(a["L0_attn_Wq"]), k_columns(a["L0_attn_Wk"]), v_columns(a["L0_attn_Wv"])], axis=1))
    out["patch_w_out"] = out_rows(a["L0_attn_Wo"])
    out["global_w_qkv"] = in_chunks(head_columns(a["L1_attn_g_wq"]))
    out["w_down"] = in_chunks(a["L1_attn_g_kv_down"])
    out["w_kv_up"] = np.concatenate([k_columns(a["L1_attn_g_k_up"]), v_columns(a["L1_attn_g_v_up"])], axis=1)
    out["global_w_out"] = out_rows(a["L1_attn_g_wo"])
    out["local_w_qkv"] = in_chunks(np.concatenate([head_columns(a["L1_attn_l_wq"]), k_columns(a["L1_attn_l_wk"]), v_columns(a["L1_attn_l_wv"])], axis=1))
    out["local_w_out"] = out_rows(a["L1_attn_l_wo"])
    out["global_w_norm"] = a["L1_attn_norm1_w"].reshape(KC, P).T
    out["local_w_norm"] = a["L1_attn_norm2_w"].reshape(KC, P).T
    out["ffn_gate"] = in_chunks(a["L0_ffn_w_gate"]).reshape(P, -1)
    out["ffn_up"] = in_chunks(a["L0_ffn_w_up"]).reshape(P, -1)
    out["ffn_down"] = in_chunks(a["L0_ffn_w_down"]).reshape(P, -1)
    out["protos"] = in_chunks(a["L1_ffn_prototypes"].T)
    out["b_maps"] = in_chunks(a["L1_ffn_B"].reshape(LOW, D).T)
    out["a_maps"] = in_chunks(a["L1_ffn_A"].transpose(0, 2, 1).reshape(LOW, D))
    out["bias"] = a["L1_ffn_bias"]
    out["number"] = np.broadcast_to(np.arange(PROTOS, dtype=np.float32), (P, PROTOS))
    out["temp"] = np.broadcast_to(np.reshape(a["L1_ffn_temp"], (1, 1)), (P, 1))
    return {k: np.ascontiguousarray(v, dtype=np.float32) for k, v in out.items()}


def kernel(**inputs):
    import concourse.bacc as bacc
    from concourse.bass_utils import run_bass_kernel_spmd

    nc = bacc.Bacc("TRN2", target_bir_lowering=False, num_devices=1)
    arrays, dram = {}, {}
    for name, a in layouts({k: np.asarray(v) for k, v in inputs.items()}).items():
        arrays[f"in_{name}"] = a
        dram[name] = nc.dram_tensor(f"in_{name}", a.shape, mybir.dt.from_np(a.dtype), kind="ExternalInput").ap()
    out = nc.dram_tensor("out", (TILES, P, D), F32, kind="ExternalOutput").ap()
    vit_tower(nc, dram, out)
    ran = run_bass_kernel_spmd(nc, [arrays], core_ids=[0])
    return ran.results[0]["out"].reshape(IMAGES, SEQ, D)
```

```python
from contextlib import ExitStack

import numpy as np
import concourse.bass as bass
from concourse import mybir

F32 = mybir.dt.float32
I16 = mybir.dt.int16
U16 = mybir.dt.uint16
U32 = mybir.dt.uint32
ALU = mybir.AluOpType
ACT = mybir.ActivationFunctionType
AX = mybir.AxisListType
MAX_ALL = bass.bass_isa.ReduceOp.max

P = 128
D = 256
KC = D // P
IMAGES, SEQ = 64, 64
TILE = 2 * SEQ
TILES = IMAGES * SEQ // TILE
PATCH = 3 * 16 * 16
PC = PATCH // P
HEADS, GROUPS, HD = 16, 4, 16
QK = D + GROUPS * HD
QKV = QK + GROUPS * HD
LATENT = 64
ROPED = HEADS + GROUPS
LN_EPS, RMS_EPS = 1e-5, 1e-6
FFN = 768
FC = FFN // P
BLOCK = 32
FFN_WEIGHTS = ("ffn_gate", "ffn_up", "ffn_down")
Q16, Q4 = 32767.0, 7.0
LEAST_SCALE = 1e-12
MAGIC = 1.5 * 2.0 ** 23


def wait_for(eng, sem, count):
    if isinstance(count, int) and count <= 0:
        return
    eng.wait_ge(sem, count)


def carrier(nc, spare):
    nc.vector.memset(spare, 0.0)


def over(eng, step, counts, depth, peel, unroll=2):
    total, first = sum(counts), counts[0]

    def single(t):
        step(t, t // 2, t % 2, lambda lag: lag <= t < total + lag, lambda lag: t - lag >= first)

    done = 0
    for kind, count in enumerate(counts):
        for t in range(done, done + peel):
            single(t)
        with eng.Fori((done + peel) // unroll, (done + count) // unroll) as turn:
            for u in range(unroll):
                step(unroll * turn + u, unroll // 2 * turn + u // 2, u % 2, lambda lag: True, lambda lag: kind == 1)
        done += count
    for t in range(total, total + depth):
        single(t)


def after(n, count):
    return 0 if isinstance(n, int) and n <= 0 else count


def upto_last(n, last, per=1):
    return per * min(n, last) if isinstance(n, int) else per * n


def attention_tables(nc, ctx, which, dram, spaces=()):
    used = [0] * len(spaces)

    def sb(what, shape):
        size = int(np.prod(shape[1:]))
        for k, space in enumerate(spaces):
            if shape[0] == P and used[k] + size <= FC * D:
                flat = space[:].rearrange("p a b -> p (a b)")[:, used[k]:used[k] + size]
                used[k] += size
                return flat.rearrange("p (a b) -> p a b", a=shape[1]) if len(shape) == 3 else flat
        return ctx.enter_context(nc.sbuf_tensor(f"{which[0]}_{what}", shape, F32))

    normed = "patch" not in which
    cols = [D if m == "global" else QKV for m in which]
    t = {"cols": cols, "w_qkv": [sb(f"w_qkv_{m}", [P, KC, c]) for m, c in zip(which, cols)], "k_mask": sb("k_mask", [P, 2])}
    for what, shape in (("w_out", [P, KC, D]), ("cos", [P, QK]), ("sin", [P, QK]), ("w_norm", [P, KC])):
        if what != "w_norm" or normed:
            t[what] = [sb(f"{what}_{m}", shape) for m in which]
    pairs = [(t["k_mask"], dram["k_mask"])]
    pairs += [(t[what][k], dram[f"{m}_{what}"]) for k, m in enumerate(which) for what in ("w_qkv", "w_out", "cos", "sin", "w_norm") if what in t]
    if normed:
        t["causal"], t["w_down"], t["w_kv_up"] = sb("causal", [P, SEQ]), sb("w_down", [P, KC, LATENT]), sb("w_kv_up", [LATENT, 2 * GROUPS * HD])
        pairs += [(t[what], dram[what]) for what in ("causal", "w_down", "w_kv_up")]
    t["loads"], t["sem"], t["pairs"] = 16 * len(pairs), ctx.enter_context(nc.semaphore(f"{which[0]}_tables")), pairs
    return t


def load(sp, tables):
    for to, frm in tables["pairs"]:
        sp.dma_start(to[:], frm).then_inc(tables["sem"], 16)


def turn_weights(nc, eng, keep, raw, k, turned, done, kept):
    name, to = FFN_WEIGHTS[k], keep[FFN_WEIGHTS[k]]
    for q in range(3):
        n = 3 * k + q
        if eng is nc.tensor:
            wait_for(eng, kept, n - 3)
            for b in range(4):
                at = (4 * q + b) * P
                mm = eng.transpose(turned[:, n % 4, b * P:(b + 1) * P], raw[:, k, at:at + P], keep["identity"][:, :])
            mm.then_inc(done, 1)
            continue
        eng.wait_ge(done, n + 1)
        if name == "ffn_down":
            for b in range(4):
                oc, ic = divmod(4 * q + b, FC)
                ins = nc.scalar.copy(to[:, ic, oc * P:(oc + 1) * P], turned[:, n % 4, b * P:(b + 1) * P])
        else:
            out = to[:, :, 2 * q * P:2 * (q + 1) * P].rearrange("p k (o c) -> p o k c", o=2)
            ins = nc.scalar.copy(out, turned[:, n % 4].rearrange("p (o k c) -> p o k c", o=2, k=2))
        ins.then_inc(kept, 1)


def weight_scales(nc, dve, w, scale, steps, k):
    s, inv = scale[:, 0], scale[:, 1]
    nc.vector.tensor_reduce(s, w.rearrange("p (b i) -> p b i", i=BLOCK), AX.X, ALU.max, apply_absolute_value=True).then_inc(steps, 1)
    dve.wait_ge(steps, 3 * k + 1)
    nc.vector.tensor_scalar(s, s, 1.0 / Q4, LEAST_SCALE, ALU.mult, ALU.max).then_inc(steps, 1)
    dve.wait_ge(steps, 3 * k + 2)
    nc.vector.reciprocal(inv, s).then_inc(steps, 1)


def whole_weights(nc, pool, w, s, inv, magic, room, spare, steps, n):
    blocks, room = w.rearrange("p (b i) -> p b i", i=BLOCK), room[:].rearrange("p (b i) -> p b i", i=BLOCK)
    spread = list(room.shape)
    magics = magic[:, 0:1, None].broadcast_to(spread)
    wait_for(pool, steps, 4 * n)
    nc.gpsimd.tensor_tensor(spare, magic[:], magic[:], ALU.add)
    nc.gpsimd.tensor_tensor(room, blocks, inv[:, :, None].broadcast_to(spread), ALU.mult).then_inc(steps, 1)
    wait_for(pool, steps, 4 * n + 1)
    nc.gpsimd.tensor_tensor(room, room, magics, ALU.add).then_inc(steps, 1)
    wait_for(pool, steps, 4 * n + 2)
    nc.gpsimd.tensor_tensor(room, room, magics, ALU.subtract).then_inc(steps, 1)
    wait_for(pool, steps, 4 * n + 3)
    nc.gpsimd.tensor_tensor(spare, magic[:], magic[:], ALU.add)
    nc.gpsimd.tensor_tensor(blocks, room, s[:, :, None].broadcast_to(spread), ALU.mult).then_inc(steps, 1)


def attention_phase(nc, name, dram, keep, tables, ahead):
    patch, normed = name == "patch", name == "layer"
    counts = (TILES,) if patch else (TILES, TILES)
    total = sum(counts)
    scale = 1.0 / 16 if patch else 1.0 / 4
    h_all, x_all, identity, consts = keep["h"], keep["x"], keep["identity"], keep["consts"]
    half_neg = consts[:, 0:1]
    DEPTH, PEEL = (5 if patch else 6), 8
    with ExitStack() as ctx:
        def sb(what, shape, dt=F32):
            return ctx.enter_context(nc.sbuf_tensor(f"{name}_{what}", shape, dt))

        def bank(what, shape):
            return ctx.enter_context(nc.psum_tensor(f"{name}_{what}", shape, F32))

        def sem(what):
            return ctx.enter_context(nc.semaphore(f"{name}_{what}"))

        w_qkv, w_out, cos_t, sin_t, k_mask, cols = (tables[k] for k in ("w_qkv", "w_out", "cos", "sin", "k_mask", "cols"))
        if patch:
            w_patch = sb("w_patch", [P, PC, D])
            b_patch = sb("b_patch", [P, D])
            patches = sb("patches", [P, 2, PC, TILE])
        else:
            w_norm, causal, w_down, w_kv_up = (tables[k] for k in ("w_norm", "causal", "w_down", "w_kv_up"))
            lat = sb("lat", [LATENT, 2, TILE])
        stats = sb("stats", [P, 2, 6])
        spare = sb("spare", [P, 1])
        mean_var = sb("mean_var", [P, 2, 2])
        small = sb("small", [P, 2, 4])
        rstd = sb("rstd", [P, 2, 2])
        xn = sb("xn", [P, 2, D])
        xT = sb("xT", [P, 2, KC, TILE])
        by_cos = sb("by_cos", [P, ROPED, 2, HD // 2])
        by_sin = sb("by_sin", [P, ROPED, 2, HD // 2])
        qk = sb("qk", [P, 2, ROPED, 2, HD // 2])
        qT = sb("qT", [P, 2, 2, 2, SEQ])
        k_diag = sb("k_diag", [P, 2, 2, 2, SEQ])
        v_rows = sb("v_rows", [P, 2, GROUPS * HD])
        v_diag = sb("v_diag", [P, 2, 2, 2, 2, HD + 1])
        probs = sb("probs", [P, 2, 4, 2 * P])
        rden = sb("rden", [P, 16])
        attn = sb("attn", [P, 2, 2, P])
        aT = sb("aT", [P, 2, 2, 2, SEQ])
        if patch:
            probsT = sb("probsT", [P, 2, 4, 2 * P])
            top = sb("top", [P, 2, 2, 8])
            stats2 = sb("stats2", [P, 2, 6])
            mean_var2 = sb("mean_var2", [P, 2, 2])
            rstd2 = sb("rstd2", [P, 2, 1])
            small2 = sb("small2", [P, 2, 1])
            raw = sb("ffn_raw", [P, 3, FC * D])
            ffn_scale = sb("ffn_scale", [P, 2, 3 * FC * D // BLOCK])
            magic = sb("magic", [P, 1])
            ffn_room = sb("ffn_room", [P, 3 * FC * D // (TILES - PEEL)])
            pool_spare = sb("pool_spare", [P, 1])
        else:
            squares = sb("squares", [P, ROPED, HD])
            sumsq = sb("sumsq", [P, 2, ROPED])
            qk_rms = sb("qk_rms", [P, 2, ROPED])
            half_negs = sb("half_negs", [P, ROPED])
            rms_eps = sb("rms_eps", [P, ROPED])
            pair_factor, pair_eps = sb("pair_factor", [P, 2]), sb("pair_eps", [P, 2])
            half_neg2 = sb("half_neg2", [P, 2])
            rms_eps_act = sb("rms_eps_act", [P, 1])
            three_halves = sb("three_halves", [P, ROPED])
            logs = sb("logs", [P, 2, ROPED])
            guess = sb("guess", [P, 2, ROPED])
            newton = sb("newton", [P, ROPED])
            qkn = sb("qkn", [P, 2, ROPED, HD])

        sc = bank("sc", [P, 4, 512])
        hy = bank("hy", [P, 512])
        xq = bank("xq", [P, 512])
        pj = bank("pj", [P, 512])
        ao = bank("ao", [P, 512])

        loaded, all_loads = tables["sem"], tables["loads"]
        consts_ready = sem("consts_ready")
        if patch:
            patches_loaded = [sem("patches_loaded0"), sem("patches_loaded1")]
            w_patch_loaded, ffn_loaded = sem("w_patch_loaded"), sem("ffn_loaded")
            ffn_whole = sem("ffn_whole")
            ffn_steps, ffn_turned, ffn_kept = sem("ffn_steps"), sem("ffn_turned"), sem("ffn_kept")
            patch_done = sem("patch_done")
            pt_done, pt_ready = sem("pt_done"), sem("pt_ready")
            soft_steps = sem("soft_steps")
            final_steps, final_rstd = sem("final_steps"), sem("final_rstd")
        else:
            squares_ready, rms_steps, scaled, masked = sem("squares"), sem("rms"), sem("scaled"), sem("masked")
            sumsq_ready, guess_steps = sem("sumsq"), sem("guess")
            lat_done, lat_ready = sem("lat_done"), sem("lat_ready")
        front_steps, front_pool, xn_ready = sem("front_steps"), sem("front_pool"), sem("xn_ready")
        xt_done, xt_ready = sem("xt_done"), sem("xt_ready")
        qkv_done, rope_steps = sem("qkv_done"), sem("rope_steps")
        qkt_done, qt_ready, kd_ready = sem("qkt_done"), sem("qt_ready"), sem("kd_ready")
        v_ready = sem("v_ready")
        scores_done, exp_done = sem("scores_done"), sem("exp_done")
        pv_done, norm_steps = sem("pv_done"), sem("norm_steps")
        at_done, at_ready, y_done, out_steps = sem("at_done"), sem("at_ready"), sem("y_done"), sem("out_steps")

        FRONT = 3 if patch else 2
        POOLF = 2 if patch else 4
        XN = 1 if patch else 2
        ROPE = 5
        SPREAD_V = 4
        OUT = 3 if patch else 2
        SCALE_PARTS = 6
        CONSTS = 5 if patch else 5 + 3 * KC

        def row(n, late):
            return n - TILES if late else n

        block = ctx.enter_context(nc.Block())

        @block.sync
        def _(sp):
            if patch:
                sp.dma_start(patches[:, 0], dram["patches"][0]).then_inc(patches_loaded[0], 16)
                sp.dma_start(w_patch[:], dram["w_patch"]).then_inc(w_patch_loaded, 16)
                sp.dma_start(patches[:, 1], dram["patches"][1]).then_inc(patches_loaded[1], 16)
                sp.dma_start(b_patch[:], dram["b_patch"]).then_inc(w_patch_loaded, 16)
                sp.dma_start(identity[:], dram["identity"]).then_inc(w_patch_loaded, 16)
                load(sp, tables)
                for k, what in enumerate(FFN_WEIGHTS):
                    sp.dma_start(raw[:, k], dram[what]).then_inc(ffn_loaded, 16)
                with sp.Fori(1, TILES // 2) as i:
                    for s in range(2):
                        sp.wait_ge(patch_done, 2 * i + s - 1)
                        sp.dma_start(patches[:, s], dram["patches"][2 * i + s]).then_inc(patches_loaded[s], 16)
            if ahead:
                load(sp, ahead)
                sp.wait_ge(ahead["sem"], ahead["loads"])

        @block.tensor
        def _(pe):
            if patch:
                pe.wait_ge(w_patch_loaded, 48)

            def tables_first(n):
                if isinstance(n, int) and n == 0:
                    pe.wait_ge(loaded, all_loads)
                    pe.wait_ge(consts_ready, CONSTS)

            def transpose_x(n, s):
                wait_for(pe, xn_ready, XN * (n + 1))
                wait_for(pe, qt_ready, n - 1)
                wait_for(pe, kd_ready, n - 1)
                for c in range(KC):
                    mm = pe.transpose(xq[:, c * P:(c + 1) * P], xn[:, s, c * P:(c + 1) * P], identity[:, :])
                mm.then_inc(xt_done, 1)

            def transpose_qk(n, s):
                if patch:
                    wait_for(pe, rope_steps, ROPE * n + 4)
                    rows = qk[:, s].rearrange("p h e i -> p (h e i)")
                else:
                    wait_for(pe, scaled, n + 1)
                    rows = qkn[:, s].rearrange("p h d -> p (h d)")
                wait_for(pe, xt_ready, upto_last(n + 2, total))
                for a in range(2):
                    pe.transpose(xq[:, a * P:(a + 1) * P], rows[:, a * P:(a + 1) * P], identity[:, :])
                pe.transpose(xq[0:GROUPS * HD, 2 * P:3 * P], rows[:, D:QK], identity[:, :]).then_inc(qkt_done, 1)

            def embed(n, s, i, chunks):
                if chunks[0] == 0:
                    pe.wait_ge(patches_loaded[s], 16 * i + 16)
                    wait_for(pe, front_steps, after(n, FRONT * (n - 1) + 1))
                    wait_for(pe, out_steps, after(n - 4, OUT * (n - 5) + 1))
                for c in chunks:
                    mm = pe.matmul(hy[:, 0:D], patches[:, s, c], w_patch[:, c], start=c == 0, stop=c == PC - 1)
                if c == PC - 1:
                    mm.then_inc(patch_done, 1)

            def down(n, s):
                tables_first(n)
                wait_for(pe, xt_ready, n + 1)
                wait_for(pe, out_steps, after(n - 4, OUT * (n - 5) + 1))
                for c in range(KC):
                    mm = pe.matmul(hy[0:LATENT, D:D + TILE], w_down[:, c], xT[:, s, c], start=c == 0, stop=c == KC - 1)
                mm.then_inc(lat_done, 1)

            def project(n, s, chunks, late):
                latent, width = normed and not late, cols[late]
                if chunks[0] == 0:
                    tables_first(n)
                    wait_for(pe, xt_ready, n + 1)
                    wait_for(pe, rope_steps, ROPE * n)
                for c in chunks:
                    mm = pe.matmul(pj[:, 0:width], xT[:, s, c], w_qkv[late][:, c], start=c == 0, stop=c == KC - 1)
                if c < KC - 1:
                    return
                if latent:
                    wait_for(pe, lat_ready, n + 1)
                    mm = pe.matmul(pj[:, D:QKV], lat[:, s], w_kv_up[:, :], start=True, stop=True)
                mm.then_inc(qkv_done, 1)

            def score(n, s, t):
                rl = t // 2
                if t == 0:
                    wait_for(pe, qt_ready, n + 1)
                    wait_for(pe, kd_ready, n + 1)
                if t % 2 == 0:
                    wait_for(pe, pt_ready if patch else exp_done, after(n, 2 * (n - 1) + rl + 1))
                rows = slice(32 * t, 32 * t + 32)
                for img in range(2):
                    q_side = qT[rows, s, img].rearrange("p a q -> p (a q)")
                    k_side = k_diag[rows, s, img].rearrange("p g k -> p (g k)")
                    out = sc[:, t, img * P:(img + 1) * P]
                    if patch:
                        mm = pe.matmul(out, q_side, k_side, start=True, stop=True)
                    else:
                        mm = pe.matmul(out, k_side, q_side, start=True, stop=True)
                if t % 2 == 1:
                    mm.then_inc(scores_done, 1)

            def transpose_probs(n, s):
                for rl in range(2):
                    wait_for(pe, exp_done, 2 * n + rl + 1)
                    for t in range(2 * rl, 2 * rl + 2):
                        for img in range(2):
                            cols = slice(img * P, (img + 1) * P)
                            mm = pe.transpose(sc[:, t, cols], probs[:, s, t, cols], identity[:, :])
                    mm.then_inc(pt_done, 1)

            def mix(n, s, pairs):
                if pairs[0] == 0:
                    wait_for(pe, pt_ready if patch else masked, 2 * (n + 1))
                    wait_for(pe, v_ready, SPREAD_V * (n + 1))
                    wait_for(pe, at_ready, n)
                src = probsT if patch else probs
                for pair in pairs:
                    img, t = pair // 4, pair % 4
                    at = pair * 2 * (HD + 1)
                    mm = pe.matmul(ao[:, at:at + 2 * (HD + 1)], src[:, s, t, img * P:(img + 1) * P],
                                   v_diag[:, s, img, t % 2].rearrange("p g d -> p (g d)"), start=True, stop=True)
                if pair == 7:
                    mm.then_inc(pv_done, 1)

            def transpose_attn(n, s):
                wait_for(pe, norm_steps, 2 * (n + 1))
                for img in range(2):
                    mm = pe.transpose(ao[:, img * P:(img + 1) * P], attn[:, s, img], identity[:, :])
                mm.then_inc(at_done, 1)

            def output(n, s, chunks, late):
                if chunks[0] == 0:
                    wait_for(pe, at_ready, n + 1)
                    if patch:
                        wait_for(pe, front_steps, upto_last(n + 5, total, FRONT) - (FRONT - 1))
                    elif not late:
                        wait_for(pe, lat_ready, upto_last(n + 5, TILES))
                    wait_for(pe, out_steps, after(n, OUT * (n - 1) + 1))
                for a in chunks:
                    mm = pe.matmul(hy[:, 0:D], aT[:, s, a].rearrange("p g q -> p (g q)"), w_out[late][:, a], start=a == 0, stop=a == 1)
                if a == 1:
                    mm.then_inc(y_done, 1)

            def beside(t):
                if isinstance(t, int) and t == TILES + 3:
                    pe.wait_ge(ffn_whole, 4 * (TILES - PEEL))
                    pe.wait_ge(pt_ready, 2 * TILES)
                    for k in range(3):
                        turn_weights(nc, pe, keep, raw, k, sc, ffn_turned, ffn_kept)

            def patch_step(t, i, s, has, late):
                if has(5):
                    output(t - 5, 1 - s, [0, 1], late(5))
                if has(3):
                    transpose_probs(t - 3, 1 - s)
                if has(1):
                    transpose_x(t - 1, 1 - s)
                if has(4):
                    transpose_attn(t - 4, s)
                if has(2):
                    transpose_qk(t - 2, s)
                if has(1):
                    project(t - 1, 1 - s, [0, 1], late(1))
                if has(0):
                    embed(t, s, i, [0])
                if has(2):
                    score(t - 2, s, 0)
                if has(0):
                    embed(t, s, i, [1])
                if has(2):
                    score(t - 2, s, 1)
                if has(0):
                    embed(t, s, i, [2])
                if has(2):
                    score(t - 2, s, 2)
                if has(0):
                    embed(t, s, i, [3])
                if has(2):
                    score(t - 2, s, 3)
                if has(0):
                    embed(t, s, i, [4])
                    embed(t, s, i, [5])
                if has(3):
                    mix(t - 3, 1 - s, range(4))
                    mix(t - 3, 1 - s, range(4, 8))
                beside(t)

            def normed_step(t, i, s, has, late):
                if has(1):
                    transpose_x(t - 1, 1 - s)
                if has(3):
                    score(t - 3, 1 - s, 0)
                if has(5):
                    transpose_attn(t - 5, 1 - s)
                if has(3):
                    score(t - 3, 1 - s, 1)
                if has(1) and not late(1):
                    down(t - 1, 1 - s)
                if has(1):
                    project(t - 1, 1 - s, [0], late(1))
                    project(t - 1, 1 - s, [1], late(1))
                if has(5):
                    output(t - 5, 1 - s, [0], late(5))
                if has(2):
                    transpose_qk(t - 2, s)
                if has(4):
                    mix(t - 4, s, range(4))
                    mix(t - 4, s, range(4, 8))
                if has(5):
                    output(t - 5, 1 - s, [1], late(5))
                if has(3):
                    score(t - 3, 1 - s, 2)
                    score(t - 3, 1 - s, 3)

            over(pe, patch_step if patch else normed_step, counts, DEPTH, PEEL, 4)

        @block.scalar
        def _(act):
            if normed:
                nc.scalar.preload_act_table_set("natural_log_exp_and_others")
            act.wait_ge(consts_ready, 1 + 4)

            def keep_xT(n, s):
                wait_for(act, xt_done, n + 1)
                wait_for(act, qkv_done, n - 1)
                nc.scalar.copy(xT[:, s].rearrange("p c t -> p (c t)"), xq[:, 0:KC * TILE]).then_inc(xt_ready, 1)

            def spread_v(n, s):
                wait_for(act, rope_steps, ROPE * (n + 1))
                wait_for(act, pv_done, n - 1)
                for img in range(2):
                    for par in range(2):
                        nc.scalar.copy(
                            v_diag[par * SEQ:(par + 1) * SEQ, s, img, :, par, 0:HD],
                            v_rows[img * SEQ:(img + 1) * SEQ, s, par * 32:par * 32 + 32].rearrange("p (j d) -> p j d", j=2),
                        ).then_inc(v_ready, 1)

            def keep_qT(n, s):
                wait_for(act, qkt_done, n + 1)
                wait_for(act, scores_done, 2 * (n - 1))
                nc.scalar.copy(qT[:, s].rearrange("p g a q -> p a g q"),
                               xq[:, 0:2 * TILE].rearrange("p (a g q) -> p a g q", a=2, g=2)).then_inc(qt_ready, 1)

            def keep_aT(n, s):
                wait_for(act, at_done, n + 1)
                wait_for(act, y_done, n - 1)
                nc.scalar.copy(aT[:, s].rearrange("p a g q -> p g a q"),
                               ao[:, 0:2 * P].rearrange("p (g a q) -> p g a q", g=2, a=2)).then_inc(at_ready, 1)

            def keep_probsT(n, s, half):
                for rl in half:
                    wait_for(act, pt_done, 2 * n + rl + 1)
                    wait_for(act, pv_done, n - 1)
                    nc.scalar.copy(probsT[:, s, 2 * rl:2 * rl + 2], sc[:, 2 * rl:2 * rl + 2, 0:2 * P]).then_inc(pt_ready, 1)

            def keep_latent(n, s):
                wait_for(act, lat_done, n + 1)
                wait_for(act, qkv_done, n - 1)
                nc.scalar.copy(lat[:, s], hy[0:LATENT, D:D + TILE]).then_inc(lat_ready, 1)

            def square(n, s):
                wait_for(act, rope_steps, ROPE * n + 4)
                nc.scalar.activation(squares[:].rearrange("p h d -> p (h d)"),
                                     qk[:, s].rearrange("p h e i -> p (h e i)"), ACT.Square, scale=HD ** -0.5).then_inc(squares_ready, 1)

            def guess_norms(n, s):
                wait_for(act, sumsq_ready, n + 1)
                wait_for(act, rms_steps, 6 * (n - 1))
                nc.scalar.activation(logs[:, s], sumsq[:, s], ACT.Ln, bias=rms_eps_act[:]).then_inc(guess_steps, 1)
                wait_for(act, guess_steps, 2 * n + 1)
                nc.scalar.activation(guess[:, s], logs[:, s], ACT.Exp, scale=-0.5).then_inc(guess_steps, 1)

            def exponent(n, s, half):
                for rl in half:
                    part = probs[:, s, 2 * rl:2 * rl + 2]
                    if patch:
                        wait_for(act, soft_steps, 4 * n + 2 * rl + 2)
                        nc.scalar.activation(part, part, ACT.Exp, scale=scale).then_inc(exp_done, 1)
                    else:
                        wait_for(act, scores_done, 2 * n + rl + 1)
                        wait_for(act, pv_done, n - 1)
                        nc.scalar.activation(part, sc[:, 2 * rl:2 * rl + 2, 0:2 * P], ACT.Exp,
                                             scale=scale).then_inc(exp_done, 1)

            def beside(t):
                if isinstance(t, int) and t == TILES + 3:
                    for k in range(3):
                        turn_weights(nc, act, keep, raw, k, sc, ffn_turned, ffn_kept)

            def patch_step(t, i, s, has, late):
                if has(3):
                    keep_probsT(t - 3, 1 - s, [0])
                if has(1):
                    keep_xT(t - 1, 1 - s)
                if has(4):
                    keep_aT(t - 4, s)
                if has(3):
                    keep_probsT(t - 3, 1 - s, [1])
                if has(2):
                    keep_qT(t - 2, s)
                    spread_v(t - 2, s)
                    exponent(t - 2, s, [0])
                    exponent(t - 2, s, [1])
                beside(t)

            def normed_step(t, i, s, has, late):
                if has(1):
                    keep_xT(t - 1, 1 - s)
                if has(4):
                    exponent(t - 4, s, [1])
                if has(1) and not late(1):
                    keep_latent(t - 1, 1 - s)
                if has(5):
                    keep_aT(t - 5, 1 - s)
                if has(2):
                    keep_qT(t - 2, s)
                if has(1):
                    square(t - 1, 1 - s)
                if has(3):
                    exponent(t - 3, 1 - s, [0])
                if has(1):
                    guess_norms(t - 1, 1 - s)
                if has(2):
                    spread_v(t - 2, s)

            over(act, patch_step if patch else normed_step, counts, DEPTH, PEEL, 4)

        @block.gpsimd
        def _(pool):
            if normed:
                nc.gpsimd.memset(rms_eps[:], RMS_EPS)
                nc.gpsimd.memset(three_halves[:], 1.5)
                nc.gpsimd.memset(half_neg2[:], -0.5)
                nc.gpsimd.memset(pair_factor[:, 0:1], 1.0)
                nc.gpsimd.memset(pair_factor[:, 1:2], 1.0 + RMS_EPS)
                nc.gpsimd.memset(pair_eps[:, 0:1], LN_EPS)
                nc.gpsimd.memset(pair_eps[:, 1:2], RMS_EPS * LN_EPS)
                nc.gpsimd.memset(half_negs[:], -0.5).then_inc(front_pool, 1)
                pool.wait_ge(front_pool, 1)
            base = 1 if normed else 0

            def front(n, s, late):
                wait_for(pool, front_steps, FRONT * (n + 1))
                first = base + POOLF * n
                mean, var = mean_var[:, s, 0:1], mean_var[:, s, 1:2]
                a, b, c = small[:, s, 0:1], small[:, s, 1:2], small[:, s, 2:3]
                if patch:
                    nc.gpsimd.tensor_tensor(a, var, consts[:, 3:4], ALU.add).then_inc(front_pool, 1)
                    pool.wait_ge(front_pool, first + 1)
                    nc.gpsimd.tensor_tensor(rstd[:, s, 0:1], a, half_neg, ALU.pow).then_inc(front_pool, 1)
                elif not late:
                    both = small[:, s, 0:2]
                    nc.gpsimd.tensor_tensor(both, var.broadcast_to([P, 2]), pair_factor[:], ALU.mult).then_inc(front_pool, 1)
                    pool.wait_ge(front_pool, first + 1)
                    nc.gpsimd.tensor_tensor(both, both, pair_eps[:], ALU.add).then_inc(front_pool, 1)
                    pool.wait_ge(front_pool, first + 2)
                    nc.gpsimd.tensor_tensor(rstd[:, s], both, half_neg2[:], ALU.pow).then_inc(front_pool, POOLF - 2)
                else:
                    nc.gpsimd.tensor_tensor(a, mean, mean, ALU.mult).then_inc(front_pool, 1)
                    pool.wait_ge(front_pool, first + 1)
                    nc.gpsimd.tensor_tensor(b, a, var, ALU.add).then_inc(front_pool, 1)
                    pool.wait_ge(front_pool, first + 2)
                    nc.gpsimd.tensor_tensor(c, b, rms_eps[:, 0:1], ALU.add).then_inc(front_pool, 1)
                    pool.wait_ge(front_pool, first + 3)
                    nc.gpsimd.tensor_tensor(rstd[:, s, 1:2], c, half_neg, ALU.pow).then_inc(front_pool, 1)

            def head_norms(n, s):
                first = 6 * n
                v, y, z = sumsq[:, s], guess[:, s], newton[:]
                wait_for(pool, sumsq_ready, n + 1)
                wait_for(pool, guess_steps, 2 * (n + 1))
                nc.gpsimd.tensor_tensor(v, v, rms_eps[:], ALU.add).then_inc(rms_steps, 1)
                wait_for(pool, rms_steps, first + 1)
                nc.gpsimd.tensor_tensor(z, v, y, ALU.mult).then_inc(rms_steps, 1)
                wait_for(pool, rms_steps, first + 2)
                nc.gpsimd.tensor_tensor(z, z, y, ALU.mult).then_inc(rms_steps, 1)
                wait_for(pool, rms_steps, first + 3)
                nc.gpsimd.tensor_tensor(z, z, half_negs[:], ALU.mult).then_inc(rms_steps, 1)
                wait_for(pool, rms_steps, first + 4)
                nc.gpsimd.tensor_tensor(z, z, three_halves[:], ALU.add).then_inc(rms_steps, 1)
                wait_for(pool, rms_steps, first + 5)
                nc.gpsimd.tensor_tensor(qk_rms[:, s], z, y, ALU.mult).then_inc(rms_steps, 1)

            def mask(n, s, half):
                for rl in half:
                    wait_for(pool, exp_done, 2 * n + rl + 1)
                    part = probs[:, s, 2 * rl:2 * rl + 2].rearrange("p t (c q) -> p (t c) q", q=SEQ)
                    nc.gpsimd.tensor_tensor(part, part, causal[:, None, :].broadcast_to([P, 8, SEQ]), ALU.mult).then_inc(masked, 1)

            def final(n, s):
                wait_for(pool, out_steps, OUT * (n + 1))
                nc.gpsimd.tensor_tensor(small2[:, s], mean_var2[:, s, 1:2], consts[:, 3:4], ALU.add).then_inc(final_rstd, 1)
                wait_for(pool, final_rstd, 2 * n + 1)
                nc.gpsimd.tensor_tensor(rstd2[:, s], small2[:, s], half_neg, ALU.pow).then_inc(final_rstd, 1)

            pool.wait_ge(consts_ready, 1)

            def beside(t):
                if not isinstance(t, int):
                    part, n = 3 * FC * D // (TILES - PEEL), t - PEEL
                    at = bass.ds(n * (part // BLOCK), part // BLOCK)
                    wait_for(pool, ffn_steps, 3 * SCALE_PARTS)
                    whole_weights(nc, pool, raw[:].rearrange("p k f -> p (k f)")[:, bass.ds(n * part, part)], ffn_scale[:, 0, at],
                                  ffn_scale[:, 1, at], magic, ffn_room, pool_spare[:], ffn_whole, n)

            def patch_step(t, i, s, has, late):
                if has(5):
                    final(t - 5, 1 - s)
                if has(0):
                    front(t, s, late(0))
                beside(t)

            def normed_step(t, i, s, has, late):
                if has(0):
                    front(t, s, late(0))
                if has(1):
                    head_norms(t - 1, 1 - s)

            over(pool, patch_step if patch else normed_step, counts, DEPTH, PEEL, 4)

        @block.vector
        def _(dve):
            if patch:
                nc.vector.memset(consts[:, 0:1], -0.5)
                nc.vector.memset(consts[:, 3:4], LN_EPS)
                nc.vector.memset(magic[:], MAGIC)
            if normed:
                nc.vector.memset(rms_eps_act[:], RMS_EPS)
            nc.vector.memset(v_diag[:], 0.0).then_inc(consts_ready, 1)
            dve.wait_ge(consts_ready, 1)
            for par in range(2):
                part = slice(par * SEQ, (par + 1) * SEQ)
                for s in range(2):
                    nc.vector.memset(v_diag[part, s, :, :, par, HD:HD + 1].rearrange("p a b c -> p (a b c)"), 1.0).then_inc(consts_ready, 1)
            if patch:
                dve.wait_ge(w_patch_loaded, 48)

            def front(n, s, late):
                first, tile = FRONT * n, row(n, late)
                if patch:
                    wait_for(dve, patch_done, n + 1)
                    nc.vector.tensor_tensor(h_all[:, n], hy[:, 0:D], b_patch[:], ALU.add).then_inc(front_steps, 1)
                    dve.wait_ge(front_steps, first + 1)
                carrier(nc, spare[:])
                nc.vector.bn_stats(stats[:, s], (x_all if late else h_all)[:, tile]).then_inc(front_steps, 1)
                dve.wait_ge(front_steps, first + FRONT - 1)
                wait_for(dve, xn_ready, XN * (n - 1))
                carrier(nc, spare[:])
                nc.vector.bn_aggr(mean_var[:, s], stats[:, s]).then_inc(front_steps, 1)

            def normalise(n, s, late):
                tile, mean = row(n, late), mean_var[:, s, 0:1]
                wait_for(dve, front_pool, (1 if normed else 0) + POOLF * (n + 1))
                wait_for(dve, xt_done, n - 1)
                if patch:
                    nc.vector.tensor_scalar(xn[:, s], h_all[:, n], mean, rstd[:, s, 0:1], ALU.subtract, ALU.mult).then_inc(xn_ready, 1)
                elif not late:
                    nc.vector.tensor_scalar(x_all[:, n], h_all[:, n], mean, rstd[:, s, 0:1], ALU.subtract, ALU.mult).then_inc(xn_ready, 1)
                    nc.vector.tensor_scalar(xn[:, s], h_all[:, n], mean, rstd[:, s, 1:2], ALU.subtract, ALU.mult).then_inc(xn_ready, 1)
                else:
                    nc.vector.tensor_scalar(xn[:, s], x_all[:, tile], rstd[:, s, 1:2], None, ALU.mult).then_inc(xn_ready, 2)

            def weights_of_norm():
                for w, norm in ((w_qkv[0], w_norm[0]), (w_down, w_norm[0]), (w_qkv[1], w_norm[1])):
                    for c in range(KC):
                        nc.vector.tensor_scalar(w[:, c], w[:, c], norm[:, c:c + 1], None, ALU.mult).then_inc(consts_ready, 1)

            def rope(n, s, late):
                if isinstance(n, int) and n == 0:
                    dve.wait_ge(loaded, all_loads)
                first = ROPE * n
                wait_for(dve, qkv_done, n + 1)
                flat = "p h e i -> p (h e i)"
                nc.vector.tensor_tensor(by_cos[:].rearrange(flat), pj[:, 0:QK], cos_t[late][:], ALU.mult).then_inc(rope_steps, 1)
                nc.vector.tensor_tensor(by_sin[:].rearrange(flat), pj[:, 0:QK], sin_t[late][:], ALU.mult).then_inc(rope_steps, 1)
                wait_for(dve, qkt_done if patch else scaled, n - 1)
                dve.wait_ge(rope_steps, first + 2)
                for e in range(2):
                    nc.vector.tensor_tensor(qk[:, s, :, e], by_cos[:, :, e], by_sin[:, :, 1 - e], ALU.add).then_inc(rope_steps, 1)
                wait_for(dve, v_ready, SPREAD_V * (n - 1))
                nc.vector.tensor_copy(v_rows[:, s], pj[:, QK:QKV]).then_inc(rope_steps, 1)

            def sum_squares(n, s):
                wait_for(dve, squares_ready, n + 1)
                nc.vector.tensor_reduce(sumsq[:, s], squares[:], AX.X, ALU.add).then_inc(sumsq_ready, 1)

            def scale_heads(n, s):
                wait_for(dve, rms_steps, 6 * (n + 1))
                wait_for(dve, qkt_done, n - 1)
                nc.vector.tensor_tensor(qkn[:, s], qk[:, s].rearrange("p h e i -> p h (e i)"),
                                        qk_rms[:, s, :, None].broadcast_to([P, ROPED, HD]), ALU.mult).then_inc(scaled, 1)

            def mask(n, s, half):
                for rl in half:
                    wait_for(dve, exp_done, 2 * n + rl + 1)
                    part = probs[:, s, 2 * rl:2 * rl + 2].rearrange("p t (c q) -> p (t c) q", q=SEQ)
                    nc.vector.tensor_tensor(part, part, causal[:, None, :].broadcast_to([P, 8, SEQ]), ALU.mult).then_inc(masked, 1)

            def spread_k(n, s):
                wait_for(dve, qt_ready, n + 1)
                wait_for(dve, scores_done, 2 * (n - 1))
                half = [GROUPS * HD, 2, 2, SEQ]
                k_t = xq[0:GROUPS * HD, 2 * P:3 * P].rearrange("p (g k) -> p g k", g=2)[:, :, None, :].broadcast_to(half)
                own = k_mask[0:GROUPS * HD, None, :, None].broadcast_to(half)
                for rl in range(2):
                    ins = nc.vector.tensor_tensor(k_diag[rl * half[0]:(rl + 1) * half[0], s], k_t, own, ALU.mult)
                ins.then_inc(kd_ready, 1)

            def soften(n, s, half):
                for rl in half:
                    wait_for(dve, scores_done, 2 * n + rl + 1)
                    wait_for(dve, pt_done, after(n - 1, 2 * (n - 2) + rl + 1))
                    pair = sc[:, 2 * rl:2 * rl + 2, 0:2 * P].rearrange("p t (c k) -> p t c k", k=SEQ)
                    out = probs[:, s, 2 * rl:2 * rl + 2].rearrange("p t (c k) -> p t c k", k=SEQ)
                    peak = top[:, s, rl].rearrange("p (t c) -> p t c", t=2)
                    nc.vector.tensor_reduce(peak, pair, AX.X, ALU.max).then_inc(soft_steps, 1)
                    wait_for(dve, soft_steps, 4 * n + 2 * rl + 1)
                    nc.vector.tensor_tensor(out, pair, peak[:, :, :, None].broadcast_to([P, 2, 4, SEQ]),
                                            ALU.subtract).then_inc(soft_steps, 1)

            def divide(n, s):
                wait_for(dve, pv_done, n + 1)
                o = ao[:, 0:16 * (HD + 1)].rearrange("p (h d) -> p h d", d=HD + 1)
                nc.vector.reciprocal(rden[:, :, None], o[:, :, HD:HD + 1]).then_inc(norm_steps, 1)
                wait_for(dve, at_done, n - 1)
                wait_for(dve, norm_steps, 2 * n + 1)
                nc.vector.tensor_tensor(attn[:, s].rearrange("p g (h d) -> p (g h) d", d=HD), o[:, :, 0:HD],
                                        rden[:, :, None].broadcast_to([P, 16, HD]), ALU.mult).then_inc(norm_steps, 1)

            def residual(n, s, late):
                first, tile = OUT * n, row(n, late)
                wait_for(dve, y_done, n + 1)
                dst = h_all if patch else x_all
                nc.vector.tensor_tensor(dst[:, tile], dst[:, tile], hy[:, 0:D], ALU.add).then_inc(out_steps, 1 if patch or late else OUT)
                if patch or late:
                    wait_for(dve, out_steps, first + 1)
                if patch:
                    carrier(nc, spare[:])
                    nc.vector.bn_stats(stats2[:, s], h_all[:, n]).then_inc(out_steps, 1)
                    wait_for(dve, out_steps, first + 2)
                    carrier(nc, spare[:])
                    nc.vector.bn_aggr(mean_var2[:, s], stats2[:, s]).then_inc(out_steps, 1)
                elif late:
                    nc.vector.tensor_tensor(h_all[:, tile], h_all[:, tile], x_all[:, tile], ALU.add).then_inc(out_steps, 1)

            def final(n, s):
                wait_for(dve, final_rstd, 2 * (n + 1))
                nc.vector.tensor_scalar(x_all[:, n], h_all[:, n], mean_var2[:, s, 0:1], rstd2[:, s], ALU.subtract,
                                        ALU.mult).then_inc(final_steps, 1)
                wait_for(dve, final_steps, 2 * n + 1)
                nc.vector.tensor_reduce(keep["x_peaks"][:, bass.ds(n, 1)],
                                        x_all[:, n], AX.X, ALU.max, apply_absolute_value=True).then_inc(final_steps, 1)

            def beside(t):
                if isinstance(t, int) and PEEL - SCALE_PARTS <= t < PEEL:
                    k, part = t - PEEL + SCALE_PARTS, 3 * FC * D // SCALE_PARTS
                    blocks = part // BLOCK
                    dve.wait_ge(ffn_loaded, 48)
                    weight_scales(nc, dve, raw[:].rearrange("p k f -> p (k f)")[:, k * part:(k + 1) * part],
                                  ffn_scale[:, :, k * blocks:(k + 1) * blocks], ffn_steps, k)

            def patch_step(t, i, s, has, late):
                if has(0):
                    beside(t)
                if has(5):
                    residual(t - 5, 1 - s, late(5))
                if has(2):
                    spread_k(t - 2, s)
                if has(1):
                    rope(t - 1, 1 - s, late(1))
                if has(5):
                    final(t - 5, 1 - s)
                if has(2):
                    soften(t - 2, s, [0])
                    soften(t - 2, s, [1])
                if has(0):
                    front(t, s, late(0))
                if has(3):
                    divide(t - 3, 1 - s)
                if has(0):
                    normalise(t, s, late(0))

            def normed_step(t, i, s, has, late):
                if has(5):
                    divide(t - 5, 1 - s)
                if has(6):
                    residual(t - 6, s, late(6))
                if has(4):
                    mask(t - 4, s, [0])
                if has(0):
                    front(t, s, late(0))
                if has(2):
                    scale_heads(t - 2, s)
                if has(4):
                    mask(t - 4, s, [1])
                if has(1):
                    rope(t - 1, 1 - s, late(1))
                if has(2):
                    spread_k(t - 2, s)
                if has(1):
                    sum_squares(t - 1, 1 - s)
                if has(0):
                    normalise(t, s, late(0))
                if isinstance(t, int) and t == 0:
                    weights_of_norm()

            over(dve, patch_step if patch else normed_step, counts, DEPTH, PEEL, 4)


GROUP = 512
NG = IMAGES * SEQ // GROUP
TPG = GROUP // TILE


def gate_phase(nc, keep):
    with ExitStack() as ctx:
        def sb(name, shape, dt=F32):
            return ctx.enter_context(nc.sbuf_tensor(f"gate_{name}", shape, dt))

        def sem(name):
            return ctx.enter_context(nc.semaphore(f"gate_{name}"))

        x_all, gate, w_gate, sc = keep["x"], keep["gate"], keep["ffn_gate"], keep["scales"]
        magic_x = sb("magic_x", [P, 2, TPG * D])
        top = sb("top", [P, 2])
        prod = ctx.enter_context(nc.psum_tensor("gate_prod", [P, FC, GROUP], F32))
        turned = ctx.enter_context(nc.psum_tensor("gate_turned", [P, 2, 512], F32))
        scale_steps, quant, turned_done, xq_ready = sem("scale_steps"), sem("quant"), sem("turned"), sem("xq_ready")
        prod_done, kept, peaked = sem("prod_done"), sem("kept"), sem("peaked")
        block = ctx.enter_context(nc.Block())

        @block.gpsimd
        def _(pool):
            pool.wait_ge(scale_steps, 1)
            nc.gpsimd.partition_all_reduce(top[:, 1:2], top[:, 0:1], P, MAX_ALL).then_inc(scale_steps, 1)

        @block.vector
        def _(dve):
            nc.vector.tensor_reduce(top[:, 0:1], keep["x_peaks"][:], AX.X, ALU.max).then_inc(scale_steps, 1)
            dve.wait_ge(scale_steps, 2)
            nc.vector.tensor_scalar(sc[:, 0:1], top[:, 1:2], 1.0 / Q16, LEAST_SCALE, ALU.mult, ALU.max).then_inc(scale_steps, 1)
            dve.wait_ge(scale_steps, 3)
            nc.vector.reciprocal(sc[:, 1:2], sc[:, 0:1]).then_inc(scale_steps, 1)
            dve.wait_ge(scale_steps, 4)

            def quantise(g, s):
                wait_for(dve, turned_done, 2 * (g - 1))
                nc.vector.tensor_scalar(magic_x[:, s], x_all[:, bass.ds(g * TPG, TPG)].rearrange("p t d -> p (t d)"),
                                        sc[:, 1:2], MAGIC, ALU.mult, ALU.add).then_inc(quant, 1)

            def peak(g):
                for oc in range(FC):
                    wait_for(dve, kept, FC * g + oc + 1)
                    nc.vector.tensor_reduce(keep["gate_peaks"][:, oc, bass.ds(g, 1)], gate[:, oc, bass.ds(g * GROUP, GROUP)],
                                            AX.X, ALU.max, apply_absolute_value=True).then_inc(peaked, 1)

            def step(t, i, s, has, late):
                if has(0):
                    quantise(t, s)
                if has(1):
                    peak(t - 1)

            over(dve, step, (NG,), 1, 2)

        @block.tensor
        def _(pe):
            def turn(g, s):
                wait_for(pe, quant, g + 1)
                for half in range(2):
                    wait_for(pe, xq_ready, after(g, 2 * (g - 1) + half + 1))
                    for c in range(4):
                        at = (4 * half + c) * P
                        mm = pe.transpose(turned[:, half, c * P:(c + 1) * P], magic_x[:, s, at:at + P], keep["identity"][:, :])
                    mm.then_inc(turned_done, 1)

            def product(g):
                wait_for(pe, xq_ready, 2 * (g + 1))
                for oc in range(FC):
                    wait_for(pe, kept, after(g, FC * (g - 1) + oc + 1))
                    for c in range(KC):
                        mm = pe.matmul(prod[:, oc], w_gate[:, c, oc * P:(oc + 1) * P],
                                       x_all[:, bass.ds(g * TPG, TPG), c * P:(c + 1) * P], start=c == 0, stop=c == KC - 1)
                    mm.then_inc(prod_done, 1)

            def step(t, i, s, has, late):
                if has(0):
                    turn(t, s)
                if has(1):
                    product(t - 1)

            over(pe, step, (NG,), 1, 2)

        @block.scalar
        def _(act):
            def keep_x(g, s):
                for half in range(2):
                    wait_for(act, turned_done, 2 * g + half + 1)
                    nc.scalar.activation(x_all[:, bass.ds(g * TPG + 2 * half, 2)].rearrange("p t d -> p (t d)"),
                                         turned[:, half], ACT.Copy, bias=-MAGIC).then_inc(xq_ready, 1)

            def keep_gate(g):
                for oc in range(FC):
                    wait_for(act, prod_done, FC * g + oc + 1)
                    nc.scalar.copy(gate[:, oc, bass.ds(g * GROUP, GROUP)], prod[:, oc]).then_inc(kept, 1)

            def step(t, i, s, has, late):
                if has(0):
                    keep_x(t, s)
                if has(1):
                    keep_gate(t - 1)

            over(act, step, (NG,), 1, 2)


def up_phase(nc, keep):
    with ExitStack() as ctx:
        def sb(name, shape, dt=F32):
            return ctx.enter_context(nc.sbuf_tensor(f"up_{name}", shape, dt))

        def sem(name):
            return ctx.enter_context(nc.semaphore(f"up_{name}"))

        x_all, gate, w_up, sc = keep["x"], keep["gate"], keep["ffn_up"], keep["scales"]
        up_rows = sb("up_rows", [P, 3, GROUP])
        gate_int = sb("gate_int", [P, 3, GROUP], I16)
        sig = sb("sig", [P, 2, GROUP])
        sig_int = sb("sig_int", [P, 3, GROUP], U16)
        top = sb("top", [P, 4])
        prod = ctx.enter_context(nc.psum_tensor("up_prod", [P, FC, GROUP], F32))
        scale_steps, prod_done, kept, peaked, stored = (
            sem("scale_steps"), sem("prod_done"), sem("kept"), sem("peaked"), [sem("stored0"), sem("stored1"), sem("stored2")])
        gate_ready, sig_ready, sig_whole, gated = sem("gate_ready"), sem("sig_ready"), sem("sig_whole"), sem("gated")
        block = ctx.enter_context(nc.Block())

        @block.gpsimd
        def _(pool):
            pool.wait_ge(scale_steps, 1)
            nc.gpsimd.partition_all_reduce(top[:, 1:2], top[:, 0:1], P, MAX_ALL).then_inc(scale_steps, 1)

        @block.sync
        def _(sp):
            with sp.Fori(0, NG) as g:
                for oc in range(FC):
                    sp.wait_ge(kept, FC * g + oc + 1)
                    sp.dma_start(keep["up_dram"][:, oc, bass.ds(g * GROUP, GROUP)], up_rows[:, oc % 3]).then_inc(stored[oc % 3], 16)
            for q in stored:
                sp.wait_ge(q, 16 * NG * FC // 3)

        @block.tensor
        def _(pe):
            def product(g):
                for oc in range(FC):
                    wait_for(pe, peaked, after(g, FC * (g - 1) + oc + 1))
                    for c in range(KC):
                        mm = pe.matmul(prod[:, oc], w_up[:, c, oc * P:(oc + 1) * P],
                                       x_all[:, bass.ds(g * TPG, TPG), c * P:(c + 1) * P], start=c == 0, stop=c == KC - 1)
                    mm.then_inc(prod_done, 1)

            over(pe, lambda t, i, s, has, late: product(t), (NG,), 0, 2)

        @block.scalar
        def _(act):
            act.wait_ge(scale_steps, 6)

            def sigmoid(g, oc):
                wait_for(act, gate_ready, FC * g + oc + 1)
                wait_for(act, sig_whole, FC * g + oc - 1)
                nc.scalar.activation(sig[:, oc % 2], gate_int[:, oc % 3], ACT.Sigmoid, scale=sc[:, 2:3]).then_inc(sig_ready, 1)

            def step(g, i, s, has, late):
                for oc in range(FC):
                    if has(0):
                        wait_for(act, gated, FC * g + oc - 2)
                        nc.scalar.activation(gate_int[:, oc % 3], gate[:, oc, bass.ds(g * GROUP, GROUP)], ACT.Copy,
                                             scale=sc[:, 3:4]).then_inc(gate_ready, 1)
                        wait_for(act, prod_done, FC * g + oc + 1)
                        wait_for(act, stored[oc % 3], 16 * (2 * g + oc // 3))
                        nc.scalar.copy(up_rows[:, oc % 3], prod[:, oc]).then_inc(kept, 1)
                    if oc and has(0):
                        sigmoid(g, oc - 1)
                    if not oc and has(1):
                        sigmoid(g - 1, FC - 1)

            over(act, step, (NG,), 1, 2)

        @block.vector
        def _(dve):
            nc.vector.tensor_reduce(top[:, 0:1], keep["gate_peaks"][:], AX.XY, ALU.max).then_inc(scale_steps, 1)
            dve.wait_ge(scale_steps, 2)
            nc.vector.tensor_scalar(top[:, 2:3], top[:, 1:2], sc[:, 0:1], None, ALU.mult).then_inc(scale_steps, 1)
            dve.wait_ge(scale_steps, 3)
            nc.vector.tensor_scalar(sc[:, 2:3], top[:, 2:3], 1.0 / Q16, LEAST_SCALE, ALU.mult, ALU.max).then_inc(scale_steps, 1)
            dve.wait_ge(scale_steps, 4)
            nc.vector.reciprocal(top[:, 3:4], sc[:, 2:3]).then_inc(scale_steps, 1)
            dve.wait_ge(scale_steps, 5)
            nc.vector.tensor_tensor(sc[:, 3:4], top[:, 3:4], sc[:, 0:1], ALU.mult).then_inc(scale_steps, 1)
            dve.wait_ge(scale_steps, 6)

            def up_peak(g, oc):
                wait_for(dve, kept, FC * g + oc + 1)
                nc.vector.tensor_reduce(keep["up_peaks"][:, oc, bass.ds(g, 1)], prod[:, oc], AX.X, ALU.max,
                                        apply_absolute_value=True).then_inc(peaked, 1)

            def whole_sigmoid(g, oc):
                wait_for(dve, sig_ready, FC * g + oc + 1)
                wait_for(dve, gated, FC * g + oc - 2)
                nc.vector.tensor_scalar(sig_int[:, oc % 3], sig[:, oc % 2], 65536.0, 65535.0, ALU.mult, ALU.min).then_inc(sig_whole, 1)

            def multiply(g, oc):
                wait_for(dve, sig_whole, FC * g + oc + 1)
                nc.vector.tensor_tensor(gate[:, oc, bass.ds(g * GROUP, GROUP)], gate_int[:, oc % 3], sig_int[:, oc % 3],
                                        ALU.mult).then_inc(gated, 1)

            def gated_peak(g, oc):
                wait_for(dve, gated, FC * g + oc + 1)
                nc.vector.tensor_reduce(keep["silu_peaks"][:, oc, bass.ds(g, 1)], gate[:, oc, bass.ds(g * GROUP, GROUP)],
                                        AX.X, ALU.max, apply_absolute_value=True)

            def behind(stage, g, oc, lag, has):
                if oc >= lag and has(0):
                    stage(g, oc - lag)
                if oc < lag and has(1):
                    stage(g - 1, oc - lag + FC)

            def step(g, i, s, has, late):
                for oc in range(FC):
                    if has(0):
                        up_peak(g, oc)
                    behind(whole_sigmoid, g, oc, 1, has)
                    behind(gated_peak, g, oc, 2, has)
                    behind(multiply, g, oc, 1, has)

            over(dve, step, (NG,), 1, 2)


def mix_phase(nc, keep):
    UNIT = 1024
    UNITS = IMAGES * SEQ // UNIT
    with ExitStack() as ctx:
        def sb(name, shape, dt=F32):
            return ctx.enter_context(nc.sbuf_tensor(f"mix_{name}", shape, dt))

        def sem(name):
            return ctx.enter_context(nc.semaphore(f"mix_{name}"))

        gate, sc = keep["gate"], keep["scales"]
        up_rows = sb("up_rows", [P, 3, UNIT])
        up_int = sb("up_int", [P, 3, UNIT], I16)
        gate_int = sb("gate_int", [P, 3, UNIT], I16)
        top = sb("top", [P, 8])
        scale_steps, up_ready = sem("scale_steps"), sem("up_ready")
        gate_ready, mixed = sem("gate_ready"), sem("mixed")
        loaded = [sem("loaded0"), sem("loaded1"), sem("loaded2")]
        block = ctx.enter_context(nc.Block())

        @block.sync
        def _(sp):
            def step(u, i, s, has, late):
                for oc in range(FC):
                    wait_for(sp, up_ready, FC * u + oc - 2)
                    sp.dma_start(up_rows[:, oc % 3], keep["up_dram"][:, oc, bass.ds(u * UNIT, UNIT)]).then_inc(loaded[oc % 3], 16)

            over(sp, step, (UNITS,), 0, 2)

        @block.gpsimd
        def _(pool):
            pool.wait_ge(scale_steps, 2)
            nc.gpsimd.partition_all_reduce(top[:, 2:4], top[:, 0:2], P, MAX_ALL).then_inc(scale_steps, 1)

        @block.scalar
        def _(act):
            act.wait_ge(scale_steps, 8)

            def step(u, i, s, has, late):
                for oc in range(FC):
                    wait_for(act, loaded[oc % 3], 16 * (2 * u + oc // 3 + 1))
                    wait_for(act, mixed, FC * u + oc - 2)
                    nc.scalar.activation(up_int[:, oc % 3], up_rows[:, oc % 3], ACT.Copy, scale=sc[:, 5:6]).then_inc(up_ready, 1)
                    nc.scalar.activation(gate_int[:, oc % 3], gate[:, oc, bass.ds(u * UNIT, UNIT)], ACT.Copy,
                                         scale=sc[:, 4:5]).then_inc(gate_ready, 1)

            over(act, step, (UNITS,), 0, 2)

        @block.vector
        def _(dve):
            nc.vector.tensor_reduce(top[:, 0:1], keep["up_peaks"][:], AX.XY, ALU.max).then_inc(scale_steps, 1)
            nc.vector.tensor_reduce(top[:, 1:2], keep["silu_peaks"][:], AX.XY, ALU.max).then_inc(scale_steps, 1)
            dve.wait_ge(scale_steps, 3)
            nc.vector.tensor_scalar(top[:, 4:5], top[:, 2:3], sc[:, 0:1], None, ALU.mult).then_inc(scale_steps, 1)
            nc.vector.tensor_scalar(top[:, 5:6], top[:, 3:4], sc[:, 2:3], 1.0 / 65536, ALU.mult, ALU.mult).then_inc(scale_steps, 1)
            dve.wait_ge(scale_steps, 5)
            nc.vector.tensor_scalar(sc[:, 6:8], top[:, 4:6], 1.0 / Q16, LEAST_SCALE, ALU.mult, ALU.max).then_inc(scale_steps, 1)
            dve.wait_ge(scale_steps, 6)
            nc.vector.reciprocal(top[:, 0:2], sc[:, 6:8]).then_inc(scale_steps, 1)
            dve.wait_ge(scale_steps, 7)
            nc.vector.tensor_scalar(sc[:, 4:5], top[:, 1:2], sc[:, 2:3], 1.0 / 65536, ALU.mult, ALU.mult)
            nc.vector.tensor_tensor(sc[:, 5:6], top[:, 0:1], sc[:, 0:1], ALU.mult).then_inc(scale_steps, 1)
            dve.wait_ge(scale_steps, 8)

            def product(u, oc):
                wait_for(dve, up_ready, FC * u + oc + 1)
                wait_for(dve, gate_ready, FC * u + oc + 1)
                nc.vector.tensor_tensor(gate[:, oc, bass.ds(u * UNIT, UNIT)], gate_int[:, oc % 3], up_int[:, oc % 3],
                                        ALU.mult).then_inc(mixed, 1)

            def peak(u, oc):
                wait_for(dve, mixed, FC * u + oc + 1)
                nc.vector.tensor_reduce(keep["out_peaks"][:, oc, bass.ds(u, 1)], gate[:, oc, bass.ds(u * UNIT, UNIT)],
                                        AX.X, ALU.max, apply_absolute_value=True)

            def step(u, i, s, has, late):
                for oc in range(FC):
                    if has(0):
                        product(u, oc)
                    if oc and has(0):
                        peak(u, oc - 1)
                    if not oc and has(1):
                        peak(u - 1, FC - 1)

            over(dve, step, (UNITS,), 1, 2)


def down_phase(nc, keep, ahead):
    with ExitStack() as ctx:
        def sb(name, shape, dt=F32):
            return ctx.enter_context(nc.sbuf_tensor(f"down_{name}", shape, dt))

        def sem(name):
            return ctx.enter_context(nc.semaphore(f"down_{name}"))

        h_all, gate, w_down, sc = keep["h"], keep["gate"], keep["ffn_down"], keep["scales"]
        magic = sb("magic", [P, 2, FC, TILE])
        whole = sb("whole", [P, 2, FC, TILE])
        top = sb("top", [P, 4])
        out = ctx.enter_context(nc.psum_tensor("down_out", [P, 2, 512], F32))
        scale_steps, rounded, whole_ready, down_done, added = (
            sem("scale_steps"), sem("rounded"), sem("whole_ready"), sem("down_done"), sem("added"))
        block = ctx.enter_context(nc.Block())

        @block.sync
        def _(sp):
            load(sp, ahead)
            sp.wait_ge(ahead["sem"], ahead["loads"])

        @block.gpsimd
        def _(pool):
            pool.wait_ge(scale_steps, 1)
            nc.gpsimd.partition_all_reduce(top[:, 1:2], top[:, 0:1], P, MAX_ALL).then_inc(scale_steps, 1)

        @block.scalar
        def _(act):
            def step(n, i, s, has, late):
                wait_for(act, rounded, n + 1)
                wait_for(act, down_done, n - 1)
                nc.scalar.activation(whole[:, s].rearrange("p c t -> p (c t)"), magic[:, s].rearrange("p c t -> p (c t)"),
                                     ACT.Copy, bias=-MAGIC).then_inc(whole_ready, 1)

            over(act, step, (TILES,), 0, 4, 4)

        @block.tensor
        def _(pe):
            def step(n, i, s, has, late):
                wait_for(pe, whole_ready, n + 1)
                wait_for(pe, added, n - 1)
                for c in range(FC):
                    mm = pe.matmul(out[:, s, 0:D], whole[:, s, c], w_down[:, c], start=c == 0, stop=c == FC - 1)
                mm.then_inc(down_done, 1)

            over(pe, step, (TILES,), 0, 4, 4)

        @block.vector
        def _(dve):
            nc.vector.tensor_reduce(top[:, 0:1], keep["out_peaks"][:], AX.XY, ALU.max).then_inc(scale_steps, 1)
            dve.wait_ge(scale_steps, 2)
            nc.vector.tensor_scalar(top[:, 2:3], top[:, 1:2], sc[:, 6:7], sc[:, 7:8], ALU.mult, ALU.mult).then_inc(scale_steps, 1)
            dve.wait_ge(scale_steps, 3)
            nc.vector.tensor_scalar(sc[:, 8:9], top[:, 2:3], 1.0 / Q16, LEAST_SCALE, ALU.mult, ALU.max).then_inc(scale_steps, 1)
            dve.wait_ge(scale_steps, 4)
            nc.vector.reciprocal(top[:, 3:4], sc[:, 8:9]).then_inc(scale_steps, 1)
            dve.wait_ge(scale_steps, 5)
            nc.vector.tensor_scalar(sc[:, 9:10], top[:, 3:4], sc[:, 6:7], sc[:, 7:8], ALU.mult, ALU.mult).then_inc(scale_steps, 1)
            dve.wait_ge(scale_steps, 6)

            def round_out(n, s):
                wait_for(dve, whole_ready, n - 1)
                nc.vector.tensor_scalar(magic[:, s], gate[:, :, bass.ds(n * TILE, TILE)], sc[:, 9:10], MAGIC,
                                        ALU.mult, ALU.add).then_inc(rounded, 1)

            def add(n, s):
                wait_for(dve, down_done, n + 1)
                nc.vector.scalar_tensor_tensor(h_all[:, n], out[:, s, 0:D], sc[:, 8:9], h_all[:, n], ALU.mult,
                                               ALU.add).then_inc(added, 1)

            def step(t, i, s, has, late):
                if has(0):
                    round_out(t, s)
                if has(1):
                    add(t - 1, 1 - s)

            over(dve, step, (TILES,), 1, 4, 4)


PROTOS, RANK = 32, 16
LOW = PROTOS * RANK


def experts_tables(nc, ctx, dram):
    shapes = {"protos": [P, KC, PROTOS], "b_maps": [P, KC, LOW], "a_maps": [P, LOW // P, D], "number": [P, PROTOS],
              "temp": [P, 4], "bias": [P, D]}
    t = {what: ctx.enter_context(nc.sbuf_tensor(f"experts_{what}", shape, F32)) for what, shape in shapes.items()}
    pairs = [(t[what], dram[what]) for what in ("protos", "b_maps", "a_maps", "number")]
    pairs += [(t["temp"][:, 0:1], dram["temp"]), (t["bias"][0:PROTOS], dram["bias"])]
    t["loads"], t["sem"], t["pairs"] = 16 * len(pairs), ctx.enter_context(nc.semaphore("experts_tables")), pairs
    return t


def experts_phase(nc, dram, out_dram, keep, tables):
    with ExitStack() as ctx:
        def sb(name, shape, dt=F32):
            return ctx.enter_context(nc.sbuf_tensor(f"experts_{name}", shape, dt))

        def bank(name, shape):
            return ctx.enter_context(nc.psum_tensor(f"experts_{name}", shape, F32))

        def sem(name):
            return ctx.enter_context(nc.semaphore(f"experts_{name}"))

        h_all, identity, consts = keep["h"], keep["identity"], keep["consts"]
        protos, b_maps, a_maps, bias, number, temp = (tables[k] for k in ("protos", "b_maps", "a_maps", "bias", "number", "temp"))
        proto_sq = sb("proto_sq", [P, KC, PROTOS])
        norms = sb("norms", [P, PROTOS])
        ones = sb("ones", [P, P])
        stats = sb("stats", [P, 2, 6])
        spare = sb("spare", [P, 1])
        minus = sb("minus", [P, 2])
        mean_var = sb("mean_var", [P, 2, 2])
        small = sb("small", [P, 2, 1])
        rstd = sb("rstd", [P, 2, 1])
        xn = sb("xn", [P, 2, D])
        squares = sb("squares", [P, D])
        x_norm = sb("x_norm", [P, 2, 1])
        xT = sb("xT", [P, 2, KC, TILE])
        sums = sb("sums", [P, PROTOS])
        near = sb("near", [P, 2, PROTOS])
        best = sb("best", [P, 2, 8])
        best_at = sb("best_at", [P, 8], U32)
        at = sb("at", [P, 2, 2])
        dist = sb("dist", [P, 2, 4])
        share = sb("share", [P, 2, 4])
        picked = sb("picked", [P, 2, PROTOS])
        shares = sb("shares", [P, 2, P])
        low = sb("low", [P, 2, LOW])
        lowT = sb("lowT", [P, 2, LOW])
        sharesT = sb("sharesT", [P, 2, P])
        result = sb("result", [P, 2, D])

        xb = bank("xb", [P, 512])
        dots = bank("dots", [P, 512])
        first = bank("first", [P, 2, 512])
        lt = bank("lt", [P, 512])
        st = bank("st", [P, 512])
        yb = bank("yb", [P, 2, 512])

        consts_ready, front_steps, front_pool = sem("consts_ready"), sem("front"), sem("front_pool")
        xn_ready, xt_done, xt_ready, x_norm_ready = sem("xn_ready"), sem("xt_done"), sem("xt_ready"), sem("x_norm")
        dots_done, first_done, pick, roots, exp_done = sem("dots_done"), sem("first_done"), sem("pick"), sem("roots"), sem("exp_done")
        share_steps, lt_done, lt_ready, y_done, stored = sem("share"), sem("lt_done"), sem("lt_ready"), sem("y_done"), [sem("stored0"), sem("stored1")]
        result_ready, gap_ready = sem("result_ready"), sem("gap_ready")
        PICK = 6
        SHARE = 7
        DEPTH, PEEL = 6, 8

        block = ctx.enter_context(nc.Block())

        @block.sync
        def _(sp):
            def step(n, i, s, has, late):
                wait_for(sp, result_ready, n + 1)
                sp.dma_start(out_dram[n], result[:, s]).then_inc(stored[s], 16)

            over(sp, step, (TILES,), 0, 2)
            for s in range(2):
                sp.wait_ge(stored[s], 16 * TILES // 2)

        @block.tensor
        def _(pe):
            pe.wait_ge(consts_ready, 6)
            for c in range(KC):
                mm = pe.matmul(dots[:, 0:PROTOS], ones[:, :], proto_sq[:, c], start=c == 0, stop=c == KC - 1)
            mm.then_inc(dots_done, 1)
            pe.wait_ge(consts_ready, 9)

            def turn_x(n, s):
                wait_for(pe, xn_ready, n + 1)
                wait_for(pe, xt_ready, n)
                for c in range(KC):
                    mm = pe.transpose(xb[:, c * P:(c + 1) * P], xn[:, s, c * P:(c + 1) * P], identity[:, :])
                mm.then_inc(xt_done, 1)

            def compare(n, s):
                wait_for(pe, xt_ready, n + 1)
                wait_for(pe, pick, after(n, PICK * (n - 1) + 2))
                for c in range(KC):
                    mm = pe.matmul(dots[:, 0:PROTOS], xT[:, s, c], protos[:, c], start=c == 0, stop=c == KC - 1)
                mm.then_inc(dots_done, 1)

            def first_maps(n, s):
                wait_for(pe, share_steps, SHARE * (n - 1))
                for c in range(KC):
                    mm = pe.matmul(first[:, s], xT[:, s, c], b_maps[:, c], start=c == 0, stop=c == KC - 1)
                mm.then_inc(first_done, 1)

            def turn_low(n, s):
                wait_for(pe, share_steps, SHARE * (n + 1))
                wait_for(pe, lt_ready, 2 * n)
                for c in range(LOW // P):
                    mm = pe.transpose(lt[:, c * P:(c + 1) * P], low[:, s, c * P:(c + 1) * P], identity[:, :])
                mm.then_inc(lt_done, 1)
                pe.transpose(st[:, 0:P], shares[:, s], identity[:, :]).then_inc(lt_done, 1)

            def second(n, s):
                wait_for(pe, lt_ready, 2 * (n + 1))
                wait_for(pe, result_ready, n - 1)
                for c in range(LOW // P):
                    pe.matmul(yb[:, s, 0:D], lowT[:, s, c * P:(c + 1) * P], a_maps[:, c], start=c == 0, stop=False)
                pe.matmul(yb[:, s, 0:D], sharesT[:, s], bias[:, :], start=False, stop=True).then_inc(y_done, 1)

            def step(t, i, s, has, late):
                if has(1):
                    turn_x(t - 1, 1 - s)
                if has(4):
                    turn_low(t - 4, s)
                if has(1):
                    compare(t - 1, 1 - s)
                    first_maps(t - 1, 1 - s)
                if has(4):
                    second(t - 4, s)

            over(pe, step, (TILES,), DEPTH, PEEL, 4)

        @block.scalar
        def _(act):
            act.wait_ge(consts_ready, 9)

            def keep_x(n, s):
                wait_for(act, xn_ready, n + 1)
                wait_for(act, pick, after(n - 1, PICK * (n - 2) + 1))
                nc.scalar.activation(squares[:], xn[:, s], ACT.Square, accum_out=x_norm[:, s]).then_inc(x_norm_ready, 1)
                wait_for(act, xt_done, n + 1)
                wait_for(act, first_done, n - 1)
                nc.scalar.copy(xT[:, s].rearrange("p c t -> p (c t)"), xb[:, 0:D]).then_inc(xt_ready, 1)

            def keep_low(n, s):
                wait_for(act, lt_done, 2 * n + 1)
                wait_for(act, y_done, n - 1)
                nc.scalar.copy(lowT[:, s], lt[:, :]).then_inc(lt_ready, 1)
                wait_for(act, lt_done, 2 * n + 2)
                nc.scalar.copy(sharesT[:, s], st[:, 0:P]).then_inc(lt_ready, 1)

            def exponent(n, s):
                wait_for(act, gap_ready, n + 1)
                wait_for(act, share_steps, SHARE * (n - 1))
                nc.scalar.activation(share[:, s, 1:2], share[:, s, 0:1], ACT.Exp, scale=temp[:, 3:4]).then_inc(exp_done, 1)

            def step(t, i, s, has, late):
                if has(1):
                    keep_x(t - 1, 1 - s)
                if has(4):
                    keep_low(t - 4, s)
                if has(2):
                    exponent(t - 2, s)

            over(act, step, (TILES,), DEPTH, PEEL, 4)

        @block.gpsimd
        def _(pool):
            def front(n, s):
                wait_for(pool, front_steps, 2 * (n + 1))
                nc.gpsimd.tensor_tensor(small[:, s], mean_var[:, s, 1:2], consts[:, 3:4], ALU.add).then_inc(front_pool, 1)
                wait_for(pool, front_pool, 2 * n + 1)
                nc.gpsimd.tensor_tensor(rstd[:, s], small[:, s], consts[:, 0:1], ALU.pow).then_inc(front_pool, 1)

            def distances(n, s):
                wait_for(pool, pick, PICK * (n + 1))
                nc.gpsimd.tensor_tensor(dist[:, s, 0:2], best[:, s, 0:2], minus[:], ALU.mult).then_inc(roots, 1)
                wait_for(pool, roots, 2 * n + 1)
                nc.gpsimd.tensor_tensor(dist[:, s, 2:4], dist[:, s, 0:2], consts[:, 1:3], ALU.pow).then_inc(roots, 1)

            pool.wait_ge(consts_ready, 9)

            def step(t, i, s, has, late):
                if has(0):
                    front(t, s)
                if has(1):
                    distances(t - 1, 1 - s)

            over(pool, step, (TILES,), DEPTH, PEEL, 4)

        @block.vector
        def _(dve):
            nc.vector.memset(minus[:], -1.0)
            nc.vector.memset(bias[PROTOS:2 * PROTOS], 0.0)
            nc.vector.memset(bias[2 * PROTOS:P], 0.0).then_inc(consts_ready, 1)
            nc.vector.memset(shares[:], 0.0).then_inc(consts_ready, 1)
            nc.vector.memset(ones[:], 1.0).then_inc(consts_ready, 1)
            nc.vector.memset(consts[:, 1:3], 0.5).then_inc(consts_ready, 1)
            dve.wait_ge(tables["sem"], tables["loads"])
            nc.vector.tensor_tensor(proto_sq[:], protos[:], protos[:], ALU.mult).then_inc(consts_ready, 1)
            nc.vector.tensor_scalar(temp[:, 1:2], temp[:, 0:1], -1.0, None, ALU.mult).then_inc(consts_ready, 1)
            dve.wait_ge(consts_ready, 6)
            nc.vector.scalar_tensor_tensor(temp[:, 2:3], temp[:, 0:1], 0.1, temp[:, 1:2], ALU.max, ALU.max).then_inc(consts_ready, 1)
            dve.wait_ge(consts_ready, 7)
            nc.vector.reciprocal(temp[:, 3:4], temp[:, 2:3]).then_inc(consts_ready, 1)
            dve.wait_ge(dots_done, 1)
            nc.vector.tensor_copy(norms[:], dots[:, 0:PROTOS]).then_inc(consts_ready, 1)
            dve.wait_ge(consts_ready, 9)

            def spread_of(n, s):
                carrier(nc, spare[:])
                nc.vector.bn_stats(stats[:, s], h_all[:, n]).then_inc(front_steps, 1)

            def mean_and_variance(n, s):
                wait_for(dve, front_steps, 2 * n + 1)
                carrier(nc, spare[:])
                nc.vector.bn_aggr(mean_var[:, s], stats[:, s]).then_inc(front_steps, 1)

            def normalise(n, s):
                wait_for(dve, front_pool, 2 * (n + 1))
                wait_for(dve, xt_done, n - 1)
                wait_for(dve, x_norm_ready, n - 1)
                nc.vector.tensor_scalar(xn[:, s], h_all[:, n], mean_var[:, s, 0:1], rstd[:, s], ALU.subtract,
                                        ALU.mult).then_inc(xn_ready, 1)

            def gap(n, s):
                wait_for(dve, roots, 2 * (n + 1))
                nc.vector.tensor_tensor(share[:, s, 0:1], dist[:, s, 2:3], dist[:, s, 3:4], ALU.subtract).then_inc(gap_ready, 1)


            def choose(n, s, k):
                if k:
                    wait_for(dve, pick, PICK * n + k)
                if k == 0:
                    wait_for(dve, x_norm_ready, n + 1)
                    wait_for(dve, roots, 2 * (n - 1))
                    ins = nc.vector.tensor_scalar(sums[:], norms[:], x_norm[:, s], None, ALU.add)
                elif k == 1:
                    wait_for(dve, dots_done, n + 2)
                    ins = nc.vector.scalar_tensor_tensor(near[:, s], dots[:, 0:PROTOS], 2.0, sums[:], ALU.mult, ALU.subtract)
                elif k == 2:
                    ins = nc.vector.tensor_scalar(near[:, s], near[:, s], 0.0, None, ALU.min)
                elif k == 3:
                    carrier(nc, spare[:])
                    ins = nc.vector.max(best[:, s], near[:, s])
                elif k == 4:
                    carrier(nc, spare[:])
                    ins = nc.vector.max_index(best_at[:], best[:, s], near[:, s])
                else:
                    ins = nc.vector.tensor_copy(at[:, s], best_at[:, 0:2])
                ins.then_inc(pick, 1)

            def weigh(n, s, k):
                if k:
                    wait_for(dve, share_steps, SHARE * n + k)
                one, two, all_of = share[:, s, 0:1], share[:, s, 3:4], shares[:, s, 0:PROTOS]
                if k == 0:
                    wait_for(dve, exp_done, n + 1)
                    ins = nc.vector.tensor_scalar(share[:, s, 2:3], share[:, s, 1:2], 1.0, None, ALU.add)
                elif k == 1:
                    ins = nc.vector.reciprocal(one, share[:, s, 2:3])
                elif k == 2:
                    ins = nc.vector.tensor_scalar(two, share[:, s, 1:2], one, None, ALU.mult)
                elif k == 3:
                    ins = nc.vector.tensor_scalar(picked[:, s], number[:], at[:, s, 0:1], one, ALU.is_equal, ALU.mult)
                elif k == 4:
                    wait_for(dve, lt_done, 2 * (n - 1))
                    ins = nc.vector.tensor_scalar(all_of, number[:], at[:, s, 1:2], two, ALU.is_equal, ALU.mult)
                elif k == 5:
                    ins = nc.vector.tensor_tensor(all_of, all_of, picked[:, s], ALU.add)
                else:
                    wait_for(dve, first_done, n + 1)
                    ins = nc.vector.tensor_tensor(low[:, s].rearrange("p (e r) -> p e r", r=RANK), first[:, s].rearrange("p (e r) -> p e r", r=RANK),
                                                  all_of[:, :, None].broadcast_to([P, PROTOS, RANK]), ALU.mult)
                ins.then_inc(share_steps, 1)

            def finish(n, s, pair):
                wait_for(dve, y_done, n + 1)
                wait_for(dve, stored[s], 16 * pair)
                nc.vector.tensor_tensor(result[:, s], h_all[:, n], yb[:, s, 0:D], ALU.add).then_inc(result_ready, 1)

            def step(t, i, s, has, late):
                if has(3):
                    weigh(t - 3, 1 - s, 0)
                if has(0):
                    spread_of(t, s)
                if has(3):
                    weigh(t - 3, 1 - s, 1)
                if has(0):
                    mean_and_variance(t, s)
                if has(3):
                    weigh(t - 3, 1 - s, 2)
                    weigh(t - 3, 1 - s, 3)
                if has(1):
                    choose(t - 1, 1 - s, 0)
                if has(3):
                    for k in range(4, SHARE):
                        weigh(t - 3, 1 - s, k)
                if has(2):
                    gap(t - 2, s)
                if has(1):
                    for k in range(1, 4):
                        choose(t - 1, 1 - s, k)
                if has(0):
                    normalise(t, s)
                if has(1):
                    for k in range(4, PICK):
                        choose(t - 1, 1 - s, k)
                if has(5):
                    finish(t - 5, 1 - s, i - 3 + s)

            over(dve, step, (TILES,), DEPTH, PEEL, 4)


def vit_tower(nc, dram, out_dram):
    with ExitStack() as ctx:
        def sb(name, shape, dt=F32):
            return ctx.enter_context(nc.sbuf_tensor(name, shape, dt))

        keep = {
            "h": sb("h_all", [P, TILES, D]), "x": sb("x_all", [P, TILES, D]), "identity": sb("identity", [P, P]),
            "consts": sb("consts", [P, 4]), "x_peaks": sb("x_peaks", [P, TILES]),
            "ffn_gate": sb("ffn_gate", [P, KC, FFN]), "ffn_up": sb("ffn_up", [P, KC, FFN]), "ffn_down": sb("ffn_down", [P, FC, D]),
            "gate_peaks": sb("gate_peaks", [P, FC, NG]), "up_peaks": sb("up_peaks", [P, FC, NG]),
            "silu_peaks": sb("silu_peaks", [P, FC, NG]), "out_peaks": sb("out_peaks", [P, FC, 4]),
            "scales": sb("scales", [P, 10]), "up_dram": nc.dram_tensor("up_rows_dram", (P, FC, IMAGES * SEQ), F32).ap(),
        }

        with ExitStack() as own:
            attention_phase(nc, "patch", dram, keep, attention_tables(nc, own, ("patch",), dram), None)
        with ExitStack() as own:
            tables = attention_tables(nc, own, ("global", "local"), dram, (keep["ffn_gate"], keep["ffn_up"]))
            with nc.sbuf_tensor("gate", [P, FC, IMAGES * SEQ], F32) as gate:
                keep["gate"] = gate
                gate_phase(nc, keep)
                up_phase(nc, keep)
                mix_phase(nc, keep)
                down_phase(nc, keep, tables)
            experts = experts_tables(nc, own, dram)
            attention_phase(nc, "layer", dram, keep, tables, experts)
            experts_phase(nc, dram, out_dram, keep, experts)


def head_columns(w):
    return w.reshape(-1, GROUPS, HEADS // GROUPS, HD // 2, 2).transpose(0, 2, 1, 4, 3).reshape(-1, D)


def k_columns(w):
    return w.reshape(-1, GROUPS, HD // 2, 2).transpose(0, 1, 3, 2).reshape(-1, GROUPS * HD)


def v_columns(w):
    return w.reshape(-1, 2, 2, HD).transpose(0, 2, 1, 3).reshape(-1, GROUPS * HD)


def out_rows(w):
    return w.reshape(GROUPS, 2, 2, HD, -1).transpose(2, 0, 3, 1, 4).reshape(P, 2, -1)


def in_chunks(w):
    return w.reshape(-1, P, w.shape[1]).transpose(1, 0, 2)


def rope_tables(q_freq, k_freq):
    pos = np.arange(SEQ, dtype=np.float32)[:, None]
    q = head_columns(np.repeat(pos * q_freq[None, :], 2, axis=1))
    k = k_columns(np.repeat(pos * np.tile(k_freq, GROUPS)[None, :], 2, axis=1))
    angle = np.tile(np.concatenate([q, k], axis=1), (2, 1)).astype(np.float32)
    sign = np.tile(np.repeat(np.array([1, -1], np.float32), HD // 2), ROPED)
    return np.cos(angle), np.sin(angle) * sign


def frequencies(base, width):
    return (np.float32(1) / np.float32(base) ** (np.arange(0, width, 2, dtype=np.float32) / np.float32(width))).astype(np.float32)


def layouts(a):
    out = {}
    x = a["x"].reshape(TILES, 2, 3, 8, 16, 8, 16).transpose(2, 4, 6, 0, 1, 3, 5).reshape(PC, P, TILES, TILE)
    out["patches"] = x.transpose(2, 1, 0, 3)
    out["w_patch"] = in_chunks(a["L0_tok_W"].T)
    out["b_patch"] = np.broadcast_to(a["L0_tok_b"], (P, D))
    out["identity"] = np.eye(P, dtype=np.float32)
    par_of = (np.arange(P) // HD) % 2
    out["k_mask"] = (par_of[:, None] == np.arange(2)[None, :]).astype(np.float32)
    out["causal"] = ((np.arange(P) % SEQ)[:, None] <= np.arange(SEQ)[None, :]).astype(np.float32)
    f0 = frequencies(10000.0, D)
    out["patch_cos"], out["patch_sin"] = rope_tables(f0, f0[:HD // 2])
    for mode, base in (("global", 1000000.0), ("local", 10000.0)):
        f = frequencies(base, HD)
        out[mode + "_cos"], out[mode + "_sin"] = rope_tables(np.tile(f, HEADS), f)
    out["patch_w_qkv"] = in_chunks(np.concatenate([head_columns(a["L0_attn_Wq"]), k_columns(a["L0_attn_Wk"]), v_columns(a["L0_attn_Wv"])], axis=1))
    out["patch_w_out"] = out_rows(a["L0_attn_Wo"])
    out["global_w_qkv"] = in_chunks(head_columns(a["L1_attn_g_wq"]))
    out["w_down"] = in_chunks(a["L1_attn_g_kv_down"])
    out["w_kv_up"] = np.concatenate([k_columns(a["L1_attn_g_k_up"]), v_columns(a["L1_attn_g_v_up"])], axis=1)
    out["global_w_out"] = out_rows(a["L1_attn_g_wo"])
    out["local_w_qkv"] = in_chunks(np.concatenate([head_columns(a["L1_attn_l_wq"]), k_columns(a["L1_attn_l_wk"]), v_columns(a["L1_attn_l_wv"])], axis=1))
    out["local_w_out"] = out_rows(a["L1_attn_l_wo"])
    out["global_w_norm"] = a["L1_attn_norm1_w"].reshape(KC, P).T
    out["local_w_norm"] = a["L1_attn_norm2_w"].reshape(KC, P).T
    out["ffn_gate"] = in_chunks(a["L0_ffn_w_gate"]).reshape(P, -1)
    out["ffn_up"] = in_chunks(a["L0_ffn_w_up"]).reshape(P, -1)
    out["ffn_down"] = in_chunks(a["L0_ffn_w_down"]).reshape(P, -1)
    out["protos"] = in_chunks(a["L1_ffn_prototypes"].T)
    out["b_maps"] = in_chunks(a["L1_ffn_B"].reshape(LOW, D).T)
    out["a_maps"] = in_chunks(a["L1_ffn_A"].transpose(0, 2, 1).reshape(LOW, D))
    out["bias"] = a["L1_ffn_bias"]
    out["number"] = np.broadcast_to(np.arange(PROTOS, dtype=np.float32), (P, PROTOS))
    out["temp"] = np.broadcast_to(np.reshape(a["L1_ffn_temp"], (1, 1)), (P, 1))
    return {k: np.ascontiguousarray(v, dtype=np.float32) for k, v in out.items()}


def kernel(**inputs):
    import concourse.bacc as bacc
    from concourse.bass_utils import run_bass_kernel_spmd

    nc = bacc.Bacc("TRN2", target_bir_lowering=False, num_devices=1)
    arrays, dram = {}, {}
    for name, a in layouts({k: np.asarray(v) for k, v in inputs.items()}).items():
        arrays[f"in_{name}"] = a
        dram[name] = nc.dram_tensor(f"in_{name}", a.shape, mybir.dt.from_np(a.dtype), kind="ExternalInput").ap()
    out = nc.dram_tensor("out", (TILES, P, D), F32, kind="ExternalOutput").ap()
    vit_tower(nc, dram, out)
    ran = run_bass_kernel_spmd(nc, [arrays], core_ids=[0])
    return ran.results[0]["out"].reshape(IMAGES, SEQ, D)
```
